# Optimizing a Trainium2 kernel written in Bass

```python
import numpy as np
import jax
import jax.numpy as jnp

def _softmax(x, axis=-1):
    return jax.nn.softmax(x, axis=axis)

def _gelu(x):
    return jax.nn.gelu(x, approximate=True)

def _silu(x):
    return jax.nn.silu(x)

def _sigmoid(x):
    return jax.nn.sigmoid(x)

def _layernorm(x, axis=-1, eps=1e-05):
    m = jnp.mean(x, axis=axis, keepdims=True)
    v = jnp.var(x, axis=axis, keepdims=True)
    return (x - m) / jnp.sqrt(v + eps)

def _scatter_add(tgt, idx, src, axis=0):
    return tgt.at[idx].add(src)

def _segment_sum(src, seg, n):
    return jax.ops.segment_sum(src, seg, n)
kernel_name = 'mk_decoder_postln_d1_seqx_r4_4de6a4'

def setup_inputs(seed: int=0):
    np.random.seed(seed)
    _w = jnp.asarray

    def _rec_inputs():
        import jax
        import jax.numpy as jnp
        _rk = jax.random.key(seed)
        x = -0.000125 + 0.9999 * jax.random.normal(jax.random.fold_in(_rk, 1), (4, 512, 512), jnp.float32)
        _lenS = 512 - jax.random.randint(jax.random.fold_in(_rk, 7), (4,), 0, max(1, 512 // 4) + 1, jnp.int32)
        _lenS2 = 512 - jax.random.randint(jax.random.fold_in(_rk, 8), (4,), 0, max(1, 512 // 4) + 1, jnp.int32)
        itok_BxS_13_99985 = jax.random.randint(jax.random.fold_in(_rk, 11), (4, 512), 13, 99986, jnp.int32)
        _ctx_2048P = jax.random.normal(jax.random.fold_in(_rk, 12), (4, 16, 512), jnp.float32)
        _ctx_2048c = jax.random.dirichlet(jax.random.fold_in(_rk, 512), 0.3 * jnp.ones((16,), jnp.float32), (4, 512))
        _ctx_2048t = jnp.einsum('bsk,bkd->bsd', _ctx_2048c, _ctx_2048P)
        _ctx_2048t = _ctx_2048t * jax.lax.rsqrt(jnp.mean(jnp.square(_ctx_2048t)) + 1e-12) * 0.953939
        ctx_2048 = 6.82029e-06 + 0.0200006 * (_ctx_2048t + 0.3 * jax.random.normal(jax.random.fold_in(_rk, 612), (4, 512, 512), jnp.float32))
        return (x, itok_BxS_13_99985, ctx_2048)
    x, itok_BxS_13_99985, ctx_2048 = _rec_inputs()

    def _L0_attn_setup():
        import jax, jax.numpy as jnp
        import numpy as np
        EMBED = 512
        HEADS = 16
        HEAD_DIM = EMBED // HEADS
        CHUNK = 128
        BASE = 10000.0
        EPS = 1e-06

        def _alibi_log_decay(h):
            slopes = 2.0 ** (-8.0 * (jnp.arange(h, dtype=jnp.float32) + 1.0) / h)
            return -slopes

        def _lrpe_rotate(x):
            b, n, h, d = x.shape
            half = d // 2
            theta = BASE ** (-2.0 * jnp.arange(half, dtype=jnp.float32) / d)
            ang = jnp.arange(n, dtype=jnp.float32)[:, None] * theta[None, :]
            cos = jnp.cos(ang)[None, :, None, :]
            sin = jnp.sin(ang)[None, :, None, :]
            x1, x2 = (x[..., :half], x[..., half:])
            return jnp.concatenate([x1 * cos - x2 * sin, x1 * sin + x2 * cos], axis=-1)

        def _lightning_attn(q, k, v, log_lam):
            b, n, h, d = q.shape
            C = CHUNK
            nc = n // C
            qc = q.reshape(b, nc, C, h, d).transpose(1, 0, 2, 3, 4)
            kc = k.reshape(b, nc, C, h, d).transpose(1, 0, 2, 3, 4)
            vc = v.reshape(b, nc, C, h, d).transpose(1, 0, 2, 3, 4)
            i = jnp.arange(C, dtype=jnp.float32)
            diff = i[:, None] - i[None, :]
            D = jnp.where(diff[None] >= 0, jnp.exp(log_lam[:, None, None] * diff[None]), 0.0)
            decay_q = jnp.exp(log_lam[None, :] * (i[:, None] + 1.0))
            decay_k = jnp.exp(log_lam[None, :] * (C - 1.0 - i[:, None]))
            lam_C = jnp.exp(log_lam * C)

            def step(S, qkv):
                qi, ki, vi = qkv
                scores = jnp.einsum('bthd,bshd->bhts', qi, ki) * D[None]
                o_intra = jnp.einsum('bhts,bshd->bthd', scores, vi)
                o_inter = jnp.einsum('bthd,bhde->bthe', qi * decay_q[None, :, :, None], S)
                S_new = lam_C[None, :, None, None] * S + jnp.einsum('bshd,bshe->bhde', ki * decay_k[None, :, :, None], vi)
                return (S_new, o_intra + o_inter)
            S0 = jnp.zeros((b, h, d, d), q.dtype)
            _, o = jax.lax.scan(step, S0, (qc, kc, vc))
            return o.transpose(1, 0, 2, 3, 4).reshape(b, n, h, d)

        def _gated_group_rmsnorm(o, gate, weight):
            b, n, d = o.shape
            x = o * jax.nn.sigmoid(gate)
            xg = x.reshape(b, n, HEADS, HEAD_DIM)
            ms = jnp.mean(xg * xg, axis=-1, keepdims=True)
            xg = xg * jax.lax.rsqrt(ms + EPS)
            return xg.reshape(b, n, d) * weight
        key = jax.random.key(seed)
        ks = jax.random.split(key, 8)
        b, n, d = (2, 512, EMBED)
        std = 0.02
        return {'x': jax.random.normal(ks[0], (b, n, d), jnp.float32), 'Wq': jax.random.normal(ks[1], (d, d), jnp.float32) * std, 'Wk': jax.random.normal(ks[2], (d, d), jnp.float32) * std, 'Wv': jax.random.normal(ks[3], (d, d), jnp.float32) * std, 'Wo': jax.random.normal(ks[4], (d, d), jnp.float32) * std, 'Wg1': jax.random.normal(ks[5], (d, HEAD_DIM), jnp.float32) * std, 'Wg2': jax.random.normal(ks[6], (HEAD_DIM, d), jnp.float32) * std, 'norm_weight': jnp.ones((d,), jnp.float32)}
    _L0_attn_all = _L0_attn_setup()
    _L0_attn_in = {k: v for k, v in _L0_attn_all.items() if k in ('Wq', 'Wk', 'Wv', 'Wo', 'Wg1', 'Wg2', 'norm_weight')}
    del _L0_attn_all

    def _L0_xattn_setup():
        import jax, jax.numpy as jnp
        import numpy as np
        B, S, D = (4, 1024, 512)
        E = 4
        F = 2048 // E
        VOCAB = 25000
        key = jax.random.key(seed)
        k1, k2, k3, k4, k5 = jax.random.split(key, 5)
        hidden_states = jax.random.normal(k1, (B, S, D), dtype=jnp.float32)
        token_ids = jax.random.randint(k2, (B, S), 0, VOCAB, dtype=jnp.int64)
        Wg = jax.random.normal(k3, (E, F, D), dtype=jnp.float32) * 0.02
        Wu = jax.random.normal(k4, (E, F, D), dtype=jnp.float32) * 0.02
        Wd = jax.random.normal(k5, (E, D, F), dtype=jnp.float32) * 0.02
        return {'hidden_states': hidden_states, 'token_ids': token_ids, 'Wg': Wg, 'Wu': Wu, 'Wd': Wd}
    _L0_xattn_all = _L0_xattn_setup()
    _L0_xattn_in = {k: v for k, v in _L0_xattn_all.items() if k in ()}
    del _L0_xattn_all

    def _L0_ffn_setup():
        import jax, jax.numpy as jnp
        import numpy as np
        NUM_EXPERTS = 128
        NUM_KEPT = 48
        TOP_K = 8
        HIDDEN = 512
        INTER = 192
        CAP = 192
        BATCH, SEQ = (2, 256)
        key = jax.random.key(seed)
        k1, k2, k3, k4 = jax.random.split(key, 4)
        hidden_states = jax.random.normal(k1, (BATCH, SEQ, HIDDEN), jnp.float32)
        gate_weight = jax.random.normal(k2, (NUM_EXPERTS, HIDDEN), jnp.float32) * 0.02
        gate_up_proj = jax.random.normal(k3, (NUM_KEPT, 2 * INTER, HIDDEN), jnp.float32) * 0.02
        down_proj = jax.random.normal(k4, (NUM_KEPT, HIDDEN, INTER), jnp.float32) * 0.02
        o2n = -np.ones(NUM_EXPERTS, np.int32)
        o2n[np.arange(NUM_KEPT) * 2] = np.arange(NUM_KEPT, dtype=np.int32)
        old_to_new = jnp.asarray(o2n)
        return {'hidden_states': hidden_states, 'gate_weight': gate_weight, 'gate_up_proj': gate_up_proj, 'down_proj': down_proj, 'old_to_new': old_to_new}
    _L0_ffn_all = _L0_ffn_setup()
    _L0_ffn_in = {k: v for k, v in _L0_ffn_all.items() if k in ('gate_weight', 'gate_up_proj', 'down_proj', 'old_to_new')}
    del _L0_ffn_all
    return {'x': x, 'itok_BxS_13_99985': itok_BxS_13_99985, 'ctx_2048': ctx_2048, 'L0_attn_Wq': _L0_attn_in['Wq'], 'L0_attn_Wk': _L0_attn_in['Wk'], 'L0_attn_Wv': _L0_attn_in['Wv'], 'L0_attn_Wo': _L0_attn_in['Wo'], 'L0_attn_Wg1': _L0_attn_in['Wg1'], 'L0_attn_Wg2': _L0_attn_in['Wg2'], 'L0_attn_norm_weight': _L0_attn_in['norm_weight'], 'L0_ffn_gate_weight': _L0_ffn_in['gate_weight'], 'L0_ffn_gate_up_proj': _L0_ffn_in['gate_up_proj'], 'L0_ffn_down_proj': _L0_ffn_in['down_proj'], 'L0_ffn_old_to_new': _L0_ffn_in['old_to_new']}

def reference(x, itok_BxS_13_99985, ctx_2048, L0_attn_Wq, L0_attn_Wk, L0_attn_Wv, L0_attn_Wo, L0_attn_Wg1, L0_attn_Wg2, L0_attn_norm_weight, L0_ffn_gate_weight, L0_ffn_gate_up_proj, L0_ffn_down_proj, L0_ffn_old_to_new):
    import jax
    import jax.numpy as jnp

    def _L0_attn_ref(x, Wq, Wk, Wv, Wo, Wg1, Wg2, norm_weight):
        import jax, jax.numpy as jnp
        import numpy as np
        EMBED = 512
        HEADS = 16
        HEAD_DIM = EMBED // HEADS
        CHUNK = 128
        BASE = 10000.0
        EPS = 1e-06

        def _alibi_log_decay(h):
            slopes = 2.0 ** (-8.0 * (jnp.arange(h, dtype=jnp.float32) + 1.0) / h)
            return -slopes

        def _lrpe_rotate(x):
            b, n, h, d = x.shape
            half = d // 2
            theta = BASE ** (-2.0 * jnp.arange(half, dtype=jnp.float32) / d)
            ang = jnp.arange(n, dtype=jnp.float32)[:, None] * theta[None, :]
            cos = jnp.cos(ang)[None, :, None, :]
            sin = jnp.sin(ang)[None, :, None, :]
            x1, x2 = (x[..., :half], x[..., half:])
            return jnp.concatenate([x1 * cos - x2 * sin, x1 * sin + x2 * cos], axis=-1)

        def _lightning_attn(q, k, v, log_lam):
            b, n, h, d = q.shape
            C = CHUNK
            nc = n // C
            qc = q.reshape(b, nc, C, h, d).transpose(1, 0, 2, 3, 4)
            kc = k.reshape(b, nc, C, h, d).transpose(1, 0, 2, 3, 4)
            vc = v.reshape(b, nc, C, h, d).transpose(1, 0, 2, 3, 4)
            i = jnp.arange(C, dtype=jnp.float32)
            diff = i[:, None] - i[None, :]
            D = jnp.where(diff[None] >= 0, jnp.exp(log_lam[:, None, None] * diff[None]), 0.0)
            decay_q = jnp.exp(log_lam[None, :] * (i[:, None] + 1.0))
            decay_k = jnp.exp(log_lam[None, :] * (C - 1.0 - i[:, None]))
            lam_C = jnp.exp(log_lam * C)

            def step(S, qkv):
                qi, ki, vi = qkv
                scores = jnp.einsum('bthd,bshd->bhts', qi, ki) * D[None]
                o_intra = jnp.einsum('bhts,bshd->bthd', scores, vi)
                o_inter = jnp.einsum('bthd,bhde->bthe', qi * decay_q[None, :, :, None], S)
                S_new = lam_C[None, :, None, None] * S + jnp.einsum('bshd,bshe->bhde', ki * decay_k[None, :, :, None], vi)
                return (S_new, o_intra + o_inter)
            S0 = jnp.zeros((b, h, d, d), q.dtype)
            _, o = jax.lax.scan(step, S0, (qc, kc, vc))
            return o.transpose(1, 0, 2, 3, 4).reshape(b, n, h, d)

        def _gated_group_rmsnorm(o, gate, weight):
            b, n, d = o.shape
            x = o * jax.nn.sigmoid(gate)
            xg = x.reshape(b, n, HEADS, HEAD_DIM)
            ms = jnp.mean(xg * xg, axis=-1, keepdims=True)
            xg = xg * jax.lax.rsqrt(ms + EPS)
            return xg.reshape(b, n, d) * weight
        b, n, d = x.shape
        q = (x @ Wq).reshape(b, n, HEADS, HEAD_DIM)
        k = (x @ Wk).reshape(b, n, HEADS, HEAD_DIM)
        v = (x @ Wv).reshape(b, n, HEADS, HEAD_DIM)
        q = jax.nn.silu(q)
        k = jax.nn.silu(k)
        q = _lrpe_rotate(q)
        k = _lrpe_rotate(k)
        log_lam = _alibi_log_decay(HEADS)
        o = _lightning_attn(q, k, v, log_lam).reshape(b, n, d)
        gate = x @ Wg1 @ Wg2
        o = _gated_group_rmsnorm(o, gate, norm_weight)
        return o @ Wo

    def _L0_xattn_ref(hidden_states, token_ids, Wg, Wu, Wd):
        import jax, jax.numpy as jnp
        import numpy as np
        B, S, D = (4, 1024, 512)
        E = 4
        F = 2048 // E
        VOCAB = 25000
        tokens_per_expert = VOCAB // E
        tid = jnp.clip(token_ids, 0, VOCAB - 1)
        expert_ids = jnp.minimum(tid // tokens_per_expert, E - 1)
        out = jnp.zeros_like(hidden_states)
        for e in range(E):
            g = jax.nn.silu(jnp.einsum('bsd,fd->bsf', hidden_states, Wg[e]))
            u = jnp.einsum('bsd,fd->bsf', hidden_states, Wu[e])
            y = jnp.einsum('bsf,df->bsd', g * u, Wd[e])
            out = jnp.where((expert_ids == e)[..., None], y, out)
        return out

    def _L0_ffn_ref(hidden_states, gate_weight, gate_up_proj, down_proj, old_to_new):
        import jax, jax.numpy as jnp
        import numpy as np
        NUM_EXPERTS = 128
        NUM_KEPT = 48
        TOP_K = 8
        HIDDEN = 512
        INTER = 192
        CAP = 192
        BATCH, SEQ = (2, 256)
        B, S, H = hidden_states.shape
        x = hidden_states.reshape(-1, H)
        T = x.shape[0]
        logits = x @ gate_weight.T
        logits = jnp.where(old_to_new[None, :] == -1, -jnp.inf, logits)
        probs = jax.nn.softmax(logits.astype(jnp.float32), axis=-1).astype(logits.dtype)
        top_v, top_i = jax.lax.top_k(probs, TOP_K)
        top_v = top_v / jnp.sum(top_v, axis=-1, keepdims=True)
        sel_new = old_to_new[top_i]
        E = gate_up_proj.shape[0]
        flat_e = sel_new.reshape(-1)
        flat_w = top_v.reshape(-1)
        tok = jnp.repeat(jnp.arange(T), TOP_K)
        oh = (flat_e[:, None] == jnp.arange(E)[None, :]).astype(jnp.int32)
        pos = jnp.sum(jnp.cumsum(oh, axis=0) * oh, axis=-1) - 1
        valid = pos < CAP
        pos_c = jnp.where(valid, pos, CAP)
        xb = jnp.zeros((E, CAP + 1, H), x.dtype).at[flat_e, pos_c].set(x[tok])
        xb = xb[:, :CAP]
        gu = jnp.einsum('ech,eoh->eco', xb, gate_up_proj)
        g, u = jnp.split(gu, 2, axis=-1)
        h = jax.nn.silu(g) * u
        out = jnp.einsum('eci,ehi->ech', h, down_proj)
        y = out[flat_e, jnp.minimum(pos_c, CAP - 1)]
        w = flat_w * valid.astype(flat_w.dtype)
        final = jnp.zeros_like(x).at[tok].add(y * w[:, None])
        return final.reshape(B, S, H)
    x = _layernorm(x + _L0_attn_ref(x, L0_attn_Wq, L0_attn_Wk, L0_attn_Wv, L0_attn_Wo, L0_attn_Wg1, L0_attn_Wg2, L0_attn_norm_weight), axis=-1)
    x = _layernorm(x + _L0_xattn_ref(x, itok_BxS_13_99985, ctx_2048, ctx_2048, ctx_2048), axis=-1)
    x = _layernorm(x + _L0_ffn_ref(x, L0_ffn_gate_weight, L0_ffn_gate_up_proj, L0_ffn_down_proj, L0_ffn_old_to_new), axis=-1)
    return x

_drawn_inputs = setup_inputs


def setup_inputs(seed=0):
    import zlib

    import numpy as np

    out = dict(_drawn_inputs(seed))
    spreads = {'L0_attn_norm_weight': (1.0, 0.2)}
    factors = {'L0_attn_Wg1': 5.496,
     'L0_attn_Wg2': 5.442,
     'L0_ffn_gate_weight': 7.012,
     'L0_ffn_gate_up_proj': 6.143,
     'L0_ffn_down_proj': 6.123}
    for name, (base, spread) in spreads.items():
        noise = np.random.default_rng([zlib.crc32(name.encode()), seed]).standard_normal(out[name].shape)
        drawn = base * np.exp(spread * noise) if base else spread * noise
        out[name] = jnp.asarray(drawn.astype(out[name].dtype))
    for name, factor in factors.items():
        out[name] = (out[name] * factor).astype(out[name].dtype)
    return out
```

```python
from contextlib import ExitStack

import numpy as np
import concourse.bass as bass
from concourse import mybir

F32 = mybir.dt.float32
BF16 = mybir.dt.bfloat16
F16 = mybir.dt.float16
I32 = mybir.dt.int32
U32 = mybir.dt.uint32
ALU = mybir.AluOpType
ACT = mybir.ActivationFunctionType
AX = mybir.AxisListType

P = 128
D = 512
KC = D // P
NB, SEQ = 4, 512
CH = SEQ // P
TOK = NB * SEQ
NT = TOK // P
H, HD = 16, 32
G = D // P
HG = P // HD
RANK = 32
LN_EPS, RMS_EPS = 1e-5, 1e-6

E1 = 4
VOCAB = 25000
PER = VOCAB // E1
SLOT_T = NT + E1 - 1
SLOTS = SLOT_T * P

OLD, E2, TOPK = 128, 48, 8
FI = 192
CAP = 192
HALF = CAP // 2
NA, NBB = 12, 16
GE = 8
NG = E2 // GE
ROW = D + E2
SPARE = 2 * P
ARENA = 22 * 1024
NEG = -1e30
TAKEN = -3e38


def shape_constants():
    f = np.float32
    i = np.arange(P)
    lam = -(f(2.0) ** (f(-8.0) * (np.arange(H, dtype=f) + f(1)) / f(H))).astype(f)
    diff = (i[None, :] - i[:, None]).astype(f)
    decay = np.where(diff[:, None, :] >= 0, np.exp(lam[None, :, None] * np.maximum(diff, 0)[:, None, :]), 0).astype(f)
    dq = np.exp(lam[:, None] * (i[None, :].astype(f) + f(1)))
    dk = np.exp(lam[None, :] * (f(P - 1) - i[:, None].astype(f)))
    lam_c = np.exp(lam * f(P))
    theta = f(10000.0) ** (f(-2.0) * np.arange(HD // 2, dtype=f) / f(HD))
    ang = (np.arange(SEQ, dtype=f)[:, None] * theta[None, :].astype(f)).astype(f)
    cos, sin = np.cos(ang).astype(f), np.sin(ang).astype(f)
    cos2 = np.concatenate([cos, cos], 1).reshape(CH, P, HD).transpose(1, 0, 2)
    sin2 = np.concatenate([-sin, sin], 1).reshape(CH, P, HD).transpose(1, 0, 2)
    by_row = np.repeat(np.arange(HG), HD)
    dq_t = np.stack([dq[g * HG + by_row] for g in range(G)], 1)
    lam_t = np.stack([lam_c[g * HG + by_row] for g in range(G)], 1)
    c = {
        "eye": np.eye(P), "decay": decay, "dq": dq_t, "dk": dk, "lam": lam_t, "cos": cos2, "sin": sin2,
        "block": (by_row[:, None] == by_row[None, :]),
        "before": (i[:, None] < i[None, :]),
        "ids": (i[:, None] + P * np.arange(NT)[None, :]),
        "tile_no": np.broadcast_to(np.arange(SLOT_T), (P, SLOT_T)),
        "n_iota": np.broadcast_to(np.arange(E2), (P, E2)),
        "ab_iota": np.broadcast_to(np.concatenate([np.arange(NA), np.arange(NBB)]), (P, NA + NBB)),
        "place_no": (NBB * (np.arange(GE * NA)[:, None] % NA) + np.arange(NBB)[None, :]),
        "diag8": (np.arange(GE * NA)[:, None] // NA == np.arange(GE)[None, :]),
    }
    c = {k: np.ascontiguousarray(v, dtype=f) for k, v in c.items()}
    c["spare"] = (TOK + i[:, None] + P * (np.arange(SLOT_T)[None, :] % 2)).astype(np.int32)
    return c


def build(nc, d):
    with ExitStack() as ctx:
        def sb(name, shape, dt=F32):
            return ctx.enter_context(nc.sbuf_tensor(name, shape, dt))

        def sem(name):
            return ctx.enter_context(nc.semaphore(name))

        def sem2(name):
            return [sem(name + "_even"), sem(name + "_odd")]

        arena = sb("arena", [P, ARENA])
        cut = [0]

        def take(name, shape, dt=F32):
            words = int(np.prod(shape[1:])) * mybir.dt.size(dt) // 4
            at, cut[0] = cut[0], cut[0] + (words + 7) // 8 * 8
            assert cut[0] <= ARENA, (name, cut[0])
            part = arena[0:shape[0], at:at + words]
            if dt != F32:
                part = part.bitcast(dt)
            axes = "abcd"[:len(shape) - 1]
            if len(axes) == 1:
                return part
            return part.rearrange(f"p ({' '.join(axes)}) -> p {' '.join(axes)}", **dict(zip(axes[1:], shape[2:])))

        x1_d = nc.dram_tensor("x1_rows", (TOK + SPARE, D), F32, kind="Internal").ap()
        x2_d = nc.dram_tensor("x2_rows", (TOK + SPARE, ROW), F32, kind="Internal").ap()
        y_d = nc.dram_tensor("y_rows", (TOK + SPARE, D), F32, kind="Internal").ap()
        token_of_slot_d = nc.dram_tensor("token_of_slot", (SLOTS, 1), I32, kind="Internal").ap()
        token_of_place_d = nc.dram_tensor("token_of_place", (E2 * CAP, 1), I32, kind="Internal").ap()

        eye = sb("eye", [P, P])
        dq = sb("dq", [P, G, P])
        dk = sb("dk", [P, H])
        lam = sb("lam", [P, G])
        cos = sb("cos", [P, CH, HD])
        sin = sb("sin", [P, CH, HD])
        block_diag = sb("block_diag", [P, P])
        before = sb("before", [P, P])
        ids = sb("ids", [P, NT])
        tile_no = sb("tile_no", [P, SLOT_T])
        n_iota = sb("n_iota", [P, E2])
        ab_iota = sb("ab_iota", [P, NA + NBB])
        place_no = sb("place_no", [GE * NA, NBB])
        diag8 = sb("diag8", [GE * NA, GE])
        wqkv = sb("wqkv", [P, KC, 3, D])
        wo = sb("wo", [P, KC, D])
        wg1 = sb("wg1", [P, KC, RANK])
        wg2 = sb("wg2", [RANK, D])
        nw = sb("nw", [P, KC])
        ctxw = sb("ctxw", [P, E1, KC, D])
        gatew = sb("gatew", [OLD, D])
        o2n_i = sb("o2n_i", [OLD, 1], I32)

        ones = sb("ones", [P, P])
        zero = sb("zero", [P, D])
        minus_half = sb("minus_half", [P, H])

        decay = take("decay", [P, H, P])
        xT = take("xT", [P, CH, KC, P])
        x_res = sb("x_res", [P, CH, D])
        sig_q = take("sig_q", [P, D]); sig_k = take("sig_k", [P, D])
        q_act = take("q_act", [P, D]); k_act = take("k_act", [P, D])
        rot1_q = take("rot1_q", [P, D]); rot1_k = take("rot1_k", [P, D])
        rot2_q = take("rot2_q", [P, D]); rot2_k = take("rot2_k", [P, D])
        q_rot = take("q_rot", [P, D]); k_rot = take("k_rot", [P, D])
        k_dec = take("k_dec", [P, 2, D])
        v = take("v", [P, 2, D])
        q_blocks = take("q_blocks", [P, G, HG, P])
        q_decT = take("q_decT", [P, G, P])
        kT = take("kT", [P, G, P])
        weighted = take("weighted", [P, H, P])
        g1T = take("g1T", [RANK, P])
        sig_gate = take("sig_gate", [P, D])
        state = take("state", [P, 2, G, P])
        state_dec = take("state_dec", [P, G, P])
        state_add = take("state_add", [P, G, P])
        gated = take("gated", [P, D])
        squares = take("squares", [P, D])
        ms = take("ms", [P, H]); ms_eps = take("ms_eps", [P, H]); rms_inv = take("rms_inv", [P, H])
        normed = take("normed", [P, D])
        oT = take("oT", [P, KC, P])
        r1 = take("r1", [P, D])
        stat1 = take("stat1", [P, 6]); mv1 = take("mv1", [P, 2]); ve1 = take("ve1", [P, 1]); rstd1 = take("rstd1", [P, 1])
        x1o = sb("x1o", [P, 2, D])
        tok_i = sb("tok_i", [P, NT], I32)
        tok_f = sb("tok_f", [P, NT])
        ge = sb("ge", [P, E1 - 1, NT])
        onehot = sb("onehot", [P, E1, NT])
        total = sb("total", [P, E1, NT])
        cum = sb("cum", [P, E1, NT])
        rank = sb("rank", [P, E1, NT])
        lot = sb("lot", [P, E1, NT])
        tiles = sb("tiles", [P, E1])
        tiles_cum = sb("tiles_cum", [P, E1])
        start = sb("start", [P, E1])
        dest = sb("dest", [P, NT])
        slot_i = sb("slot_i", [P, NT], I32)
        row_i = sb("row_i", [P, NT], I32)
        dest_i = sb("dest_i", [P, NT], U32)
        ids_i = sb("ids_i", [P, NT], I32)
        spare_i = sb("spare_i", [P, SLOT_T], I32)
        eid_f = sb("eid_f", [P, SLOT_T])
        eid_i = sb("eid_i", [P, SLOT_T], I32)

        slot_token = sb("slot_token", [P, SLOT_T], I32)
        idx_g = sb("idx_g", [P, 2], I32)
        idx_s = sb("idx_s", [P, 2], I32)
        x1g = sb("x1g", [P, 2, D])
        x1gT = sb("x1gT", [P, 2, KC, P])
        sig_s = sb("sig_s", [P, D])
        s_act = sb("s_act", [P, D])
        h1 = sb("h1", [P, D])
        h1T = sb("h1T", [P, KC, P])
        r2 = sb("r2", [P, D])
        stat2 = sb("stat2", [P, 6]); mv2 = sb("mv2", [P, 2]); ve2 = sb("ve2", [P, 1]); rstd2 = sb("rstd2", [P, 1])
        x2o = sb("x2o", [P, 2, ROW])
        x2T = sb("x2T", [P, KC, P])
        router = sb("router", [P, KC, E2])
        o2n_f = sb("o2n_f", [OLD, 1])
        pick = sb("pick", [OLD, E2])
        kept_bias = sb("kept_bias", [P, E2])
        logits = sb("logits", [P, E2])
        top8 = sb("top8", [P, TOPK])
        marked = sb("marked", [P, E2])
        neg_max = sb("neg_max", [P, 1])
        es = sb("es", [P, E2]); es1 = sb("es1", [P, E2]); es_inv = sb("es_inv", [P, E2])
        expo = sb("expo", [P, E2])
        chosen = sb("chosen", [P, E2])
        w_sum = sb("w_sum", [P, 1]); w_inv = sb("w_inv", [P, 1])
        not_chosen = sb("not_chosen", [P, E2])

        cut[0] = 0
        wnat = take("wnat", [P, NT, E2])
        sel = take("sel", [P, NT, E2], BF16)
        sel_before = take("sel_before", [P, NT, E2], BF16)
        before_b = take("before_b", [P, P], BF16)
        ones_b = take("ones_b", [P, P], BF16)
        ok = take("ok", [P, NT, E2])
        place = take("place", [P, NT, E2])
        place_i = take("place_i", [P, NT, E2], I32)
        a_i = take("a_i", [P, NT, E2], I32)
        b_i = take("b_i", [P, NT, E2], I32)
        a_h = take("a_h", [P, NT, E2], F16)
        b_h = take("b_h", [P, NT, E2], F16)
        ab_h = take("ab_h", [P, NA + NBB], F16)
        ids_h = take("ids_h", [P, NT], F16)
        hot_a = take("hot_a", [P, 2, NT, GE, NA], F16)
        hot_b = take("hot_b", [P, NT, GE, NBB], F16)
        hot_id = take("hot_id", [P, 2, NT, GE, NBB], F16)
        tab = take("tab", [GE * NA, GE, NBB])
        tab_r = take("tab_r", [GE * NA, NBB])
        tab_spare = take("tab_spare", [GE * NA, NBB])
        tab_i = take("tab_i", [GE * NA, NG, NBB], I32)

        wgu = [wqkv[:, k, :, :].rearrange("p a b -> p (a b)").rearrange("p (k o) -> p k o", k=KC) for k in range(2)]
        wdn = [wqkv[:, 2 + k, 0:2, :] for k in range(2)]
        place_token = take("place_token", [HALF, E2, 2], I32)
        cidx_g = take("cidx_g", [HALF, 2, 2], I32)
        cidx_s = take("cidx_s", [HALF, 2, 2], I32)
        xg = take("xg", [HALF, 2, 2, ROW])
        xgT = take("xgT", [P, 2, KC, CAP])
        w_col = take("w_col", [HALF, 2, 2])
        sig_a = take("sig_a", [P, CAP]); sig_c = take("sig_c", [P, CAP])
        g_a = take("g_a", [P, CAP]); g_c = take("g_c", [P, CAP])
        h_a = take("h_a", [P, 2, CAP])
        h_c = take("h_c", [P, 2, CAP])
        ye = take("ye", [HALF, 2, 2, D])

        yf = [x_res[:, k, :] for k in range(2)]
        xf = [x_res[:, 2 + k, :] for k in range(2)]
        r3 = [x1o[:, k, :] for k in range(2)]
        out_t = [x1g[:, k, :] for k in range(2)]
        stat3 = sb("stat3", [P, 6]); mv3 = sb("mv3", [P, 2]); ve3 = sb("ve3", [P, 1]); rstd3 = sb("rstd3", [P, 1])

        ps = ctx.enter_context(nc.psum_tensor("ps", [P, 8, 512], F32))
        PQ, PK, PV, PT, PS0, PO, PM = 0, 1, 2, 3, 4, 6, 7

        consts_in = sem("consts_in"); gate_in = sem("gate_in"); ctx_in = sem("ctx_in"); wqkv_in = sem("wqkv_in")
        xT_in = [sem(f"xT_in{c}") for c in range(CH)]
        x_in = [sem(f"x_in{c}") for c in range(CH)]
        setup = sem("setup"); zeroed = sem("zeroed"); sort_v = sem("sort_v"); sort_p = sem("sort_p")
        slot_sorted = sem("slot_sorted"); slots_cleared = sem("slots_cleared"); slots_named = sem("slots_named")
        rows_cleared = sem("rows_cleared")
        v_made = sem("v_made"); q_made = sem("q_made"); k_made = sem("k_made")
        v_copied = sem("v_copied"); q_sig = sem("q_sig"); k_sig = sem("k_sig")
        q_silu = sem("q_silu"); k_silu = sem("k_silu")
        q_r1 = sem("q_r1"); k_r1 = sem("k_r1"); q_r2 = sem("q_r2"); k_r2 = sem("k_r2")
        q_rotated = sem("q_rotated"); k_rotated = sem("k_rotated"); k_decayed = sem("k_decayed")
        q_turned = sem("q_turned"); k_turned = sem("k_turned")
        qT_copied = sem("qT_copied"); qT_decayed = sem("qT_decayed"); kT_copied = sem("kT_copied")
        g1_made = sem("g1_made"); g1_copied = sem("g1_copied"); gate_made = sem("gate_made"); gate_sig = sem("gate_sig")
        scored = sem("scored"); masked = sem("masked")
        add_made = sem("add_made"); add_cut = sem("add_cut"); st_decayed = sem("st_decayed"); st_new = sem("st_new")
        o_made = sem("o_made"); o_gated = sem("o_gated"); squared = sem("squared"); ms_made = sem("ms_made")
        ms_plus = sem("ms_plus"); rms_made = sem("rms_made"); o_normed = sem("o_normed")
        o_turned = sem("o_turned"); oT_copied = sem("oT_copied"); wo_made = sem("wo_made")
        r1_made = sem("r1_made"); stat1_made = sem("stat1_made"); mv1_made = sem("mv1_made")
        ve1_made = sem("ve1_made"); rstd1_made = sem("rstd1_made"); x1_made = sem("x1_made"); x1_kept = sem2("x1_kept")
        slot_token_in = sem("slot_token_in"); idx_g_set = sem("idx_g_set"); idx_s_set = sem("idx_s_set"); x1_got = sem2("x1_got")
        xg1_turned = sem("xg1_turned"); xg1_copied = sem("xg1_copied"); s_made = sem("s_made"); s_sig = sem("s_sig")
        s_silu = sem("s_silu"); h1_made = sem2("h1_made"); h1_turned = sem("h1_turned"); h1_copied = sem("h1_copied")
        y1_made = sem("y1_made"); r2_made = sem2("r2_made"); stat2_made = sem("stat2_made"); mv2_made = sem("mv2_made")
        ve2_made = sem("ve2_made"); rstd2_made = sem("rstd2_made"); x2_made = sem("x2_made")
        x2_turned = sem("x2_turned"); x2T_copied = sem("x2T_copied"); lg_made = sem("lg_made")
        router_v = sem("router_v"); rstep = sem("weights_v"); w_inverted = sem("w_inverted"); es_made = sem("es_made"); routed = sem("routed"); x2_kept = sem2("x2_kept")
        pick_v = sem("pick_v"); pick_p = sem("pick_p")
        wnat_in = sem("wnat_in"); tab_v = sem("tab_v"); pos_made = sem("pos_made"); hot_made = sem("hot_made")
        tab_made = sem("tab_made"); tab_cut = sem("tab_cut"); places_kept = sem("places_kept")
        c_half = sem("c_half"); tstep = sem("place_v"); hot_b_made = sem("hot_b_made")
        tab_masked = sem("tab_masked"); tab_summed = sem("tab_summed"); tab_spared = sem("tab_spared"); passed = sem("passed")
        gu_in = sem2("gu_in"); dn_in = sem2("dn_in"); place_token_in = sem("place_token_in"); cg_set = sem("cg_set"); cs_set = sem("cs_set")
        got = sem2("got"); c_turned = sem2("c_turned"); c_copied = sem("c_copied"); w_copied = sem2("w_copied")
        gu_made = sem2("gu_made"); c_sig = sem("c_sig"); g_made = sem("g_made"); h_made = sem("h_made")
        dn_made = sem2("dn_made"); y_scaled = sem2("y_scaled"); y_added = sem2("y_added"); y_cleared = sem("y_cleared")
        yf_in = sem2("yf_in"); r3_made = sem("r3_made"); stat3_made = sem("stat3_made"); mv3_made = sem("mv3_made")
        ve3_made = sem("ve3_made"); rstd3_made = sem("rstd3_made"); out_made = sem2("out_made"); out_kept = sem2("out_kept")

        CONSTS = [(eye, "eye"), (decay, "decay"), (dq, "dq"), (dk, "dk"), (lam, "lam"), (cos, "cos"), (sin, "sin"),
                  (block_diag, "block"), (before, "before"), (ids, "ids"), (tile_no, "tile_no"),
                  (n_iota, "n_iota"), (ab_iota, "ab_iota"), (diag8, "diag8"), (place_no, "place_no"), (spare_i, "spare"), (wg1, "wg1"), (wg2, "wg2"),
                  (nw, "nw"), (tok_i, "tok"), (wo, "wo")]
        CONSTS_IN = 16 * len(CONSTS)

        def whole(t):
            return t[(slice(None),) * len(t.shape)]

        def batches(eng, step):
            with eng.Fori(0, NB - 1) as b:
                step(b, False)
            step(NB - 1, True)

        def at_least(eng, s, n):
            if not (isinstance(n, int) and n <= 0):
                eng.wait_ge(s, n)

        def settle(eng):
            eng.sem_inc(passed, 1)

        def is_first(n):
            return isinstance(n, int) and n == 0

        def tails_before(b, c):
            return 4 * b + (c if c == 0 else c - 1)

        def units(eng, count, step):
            pairs = (count - 3) // 2
            step(0, 0, 0, 2)
            with eng.Fori(0, pairs) as i:
                step(2 * i + 1, 1, i, 2)
                step(2 * i + 2, 0, i + 1, 2)
            for n in range(2 * pairs + 1, count):
                step(n, n % 2, n // 2, min(count - 1 - n, 2))

        def before_it(p, k):
            return 1 - p, k - (1 - p)

        def after_it(p, k):
            return 1 - p, k + p

        block = ctx.enter_context(nc.Block())

        @block.sync
        def _(sp):
            for c in range(CH):
                sp.dma_start(xT[:, c], d["xT"][c]).then_inc(xT_in[c], 16)
                if c == 0:
                    for n in (2, 0, 1):
                        sp.dma_start(wqkv[:, :, n, :], d["wqkv"][:, :, n, :]).then_inc(wqkv_in, 16)
                    for t, name in CONSTS:
                        sp.dma_start(whole(t), d[name]).then_inc(consts_in, 16)
            for c in range(CH):
                sp.dma_start(x_res[:, c, :], d["x"][c * P:(c + 1) * P, :]).then_inc(x_in[c], 16)
            sp.dma_start(gatew[:, :], d["gate_weight"]).then_inc(gate_in, 16)
            sp.dma_start(o2n_i[:, :], d["o2n"]).then_inc(gate_in, 16)
            sp.dma_start(whole(ctxw), d["ctxw"]).then_inc(ctx_in, 16)

            sp.wait_ge(zeroed, 2)
            sp.wait_ge(consts_in, CONSTS_IN)
            for r in range(TOK, TOK + SPARE, P):
                sp.dma_start(x1_d[r:r + P, :], zero[:, :]).then_inc(rows_cleared, 16)
                sp.dma_start(x2_d[r:r + P, 0:D], zero[:, :]).then_inc(rows_cleared, 16)
                sp.dma_start(x2_d[r:r + P, D:ROW], zero[:, 0:E2]).then_inc(rows_cleared, 16)
                sp.dma_start(y_d[r:r + P, :], zero[:, :]).then_inc(rows_cleared, 16)
            sp.dma_start(token_of_slot_d.rearrange("(p j) a -> p (j a)", p=P), spare_i[:, :]).then_inc(slots_cleared, 16)
            for t in range(NT):
                sp.dma_start(y_d[t * P:(t + 1) * P, :], zero[:, :]).then_inc(y_cleared, 16)

            def a_batch(b, last):
                for c in range(CH):
                    t = 4 * b + c
                    if not last:
                        sp.wait_ge(g1_made, t + 1)
                        sp.dma_start(xT[:, c], d["xT"][bass.ds(t + CH, 1)].rearrange("a p k t -> (a p) k t")).then_inc(xT_in[c], 16)
                    for cc in ([c - 1] if c else []) + ([c] if c == CH - 1 else []):
                        tt = 4 * b + cc
                        sp.wait_ge(x1_made, tt + 1)
                        sp.dma_start(x1_d[bass.ds(P * tt, P), :], x1o[:, cc % 2, :]).then_inc(x1_kept[cc % 2], 16)
                        if not last:
                            sp.dma_start(x_res[:, cc, :], d["x"][bass.ds(P * (tt + CH), P), :]).then_inc(x_in[cc], 16)

            batches(sp, a_batch)

            sp.wait_ge(slots_named, 16 * NT)
            sp.dma_start(slot_token[:, :], token_of_slot_d.rearrange("(p j) a -> p (j a)", p=P)).then_inc(slot_token_in, 16)

            sp.wait_ge(x2_kept[0], 16 * (SLOT_T - SLOT_T // 2))
            sp.wait_ge(x2_kept[1], 16 * (SLOT_T // 2))
            sp.dma_start(whole(wnat), x2_d[0:TOK, D:ROW].rearrange("(j p) n -> p j n", p=P)).then_inc(wnat_in, 16)
            for g in range(NG):
                rows = slice(g * GE * CAP, (g + 1) * GE * CAP)
                sp.wait_ge(tab_cut, g + 1)
                sp.dma_start(token_of_place_d[rows, :].rearrange("(r b) a -> r (b a)", b=NBB), tab_i[:, g, :]).then_inc(places_kept, 16)
                sp.wait_ge(places_kept, 16 * (g + 1))
                sp.dma_start(place_token[:, g * GE:(g + 1) * GE, :],
                             token_of_place_d[rows, :].rearrange("(n p h) a -> p n (h a)", n=GE, h=2)).then_inc(place_token_in, 16)

            for p in range(2):
                sp.wait_ge(y_added[p], 32 * (E2 // 2))
            with sp.Fori(0, NT // 2) as i:
                for p in range(2):
                    t = 2 * i + p
                    sp.wait_ge(out_made[p], i)
                    sp.dma_start(yf[p], y_d[bass.ds(P * t, P), :]).then_inc(yf_in[p], 16)
                    sp.dma_start(xf[p], x2_d[bass.ds(P * t, P), 0:D]).then_inc(yf_in[p], 16)

        @block.tensor
        def _(pe):
            def project(n, bank, made, done, b, c):
                t = 4 * b + c
                pe.wait_ge(xT_in[c], 16 * (b + 1))
                at_least(pe, done, t)
                for k in range(KC):
                    m = pe.matmul(ps[:, bank, :], xT[:, c, k, :], wqkv[:, k, n, :], start=(k == 0), stop=(k == KC - 1))
                m.then_inc(made, 1)

            def project_q(b, c):
                project(0, PQ, q_made, q_silu, b, c)

            def project_k(b, c):
                project(1, PK, k_made, k_silu, b, c)

            def project_v(b, c):
                project(2, PV, v_made, v_copied, b, c)

            def gate_low(b, c):
                at_least(pe, r1_made, tails_before(b, c))
                at_least(pe, add_cut, 3 * b + min(c, 3))
                for k in range(KC):
                    m = pe.matmul(ps[0:RANK, PM, 0:P], wg1[:, k, :], xT[:, c, k, :], start=(k == 0), stop=(k == KC - 1))
                m.then_inc(g1_made, 1)

            def tail(b, c, now):
                t = 4 * b + c
                pe.wait_ge(o_normed, t + 1)
                pe.wait_ge(kT_copied, now + 1)
                for k in range(KC):
                    m = pe.transpose(ps[:, PT, k * P:(k + 1) * P], normed[:, k * P:(k + 1) * P], eye[:, :])
                m.then_inc(o_turned, 1)
                pe.wait_ge(oT_copied, t + 1)
                pe.wait_ge(gate_sig, now + 1)
                nc_ = c + 1 if c < CH - 1 else CH - 1
                pe.wait_ge(add_cut, 3 * b + min(nc_ + 1, 3))
                at_least(pe, r1_made, t)
                for k in range(KC):
                    m = pe.matmul(ps[:, PM, :], oT[:, k, :], wo[:, k, :], start=(k == 0), stop=(k == KC - 1))
                m.then_inc(wo_made, 1)

            def main(b, c, last):
                t = 4 * b + c
                pe.wait_ge(q_rotated, t + 1)
                at_least(pe, oT_copied, tails_before(b, c))
                for g in range(G):
                    m = pe.transpose(ps[:, PT, g * P:(g + 1) * P], q_rot[:, g * P:(g + 1) * P], eye[:, :])
                m.then_inc(q_turned, 1)
                gate_low(b, c)
                if c < CH - 1:
                    project_v(b, c + 1)
                pe.wait_ge(g1_copied, t + 1)
                pe.matmul(ps[:, PM, :], g1T[:, :], wg2[:, :], start=True, stop=True).then_inc(gate_made, 1)
                pe.wait_ge(k_rotated, t + 1)
                pe.wait_ge(qT_copied, t + 1)
                pe.wait_ge(qT_decayed, t + 1)
                for g in range(G):
                    m = pe.transpose(ps[:, PT, g * P:(g + 1) * P], k_rot[:, g * P:(g + 1) * P], eye[:, :])
                m.then_inc(k_turned, 1)
                if c < CH - 1:
                    project_q(b, c + 1)
                pe.wait_ge(kT_copied, t + 1)
                for g in range(G):
                    at_least(pe, masked, 4 * t + max(g - 1, 0))
                    pe.matmul(ps[:, PS0 + g % 2, :], kT[:, g, :], q_blocks[:, g, :, :].rearrange("p a b -> p (a b)"),
                              start=True, stop=True).then_inc(scored, 1)
                if c < CH - 1:
                    pe.wait_ge(k_decayed, 3 * b + c + 1)
                    pe.wait_ge(v_copied, t + 1)
                    pe.wait_ge(gate_sig, t + 1)
                    for g in range(G):
                        m = pe.matmul(ps[:, PM, g * P:(g + 1) * P], k_dec[:, c % 2, g * P:(g + 1) * P],
                                      v[:, c % 2, g * P:(g + 1) * P], start=True, stop=True)
                    m.then_inc(add_made, 1)
                    project_k(b, c + 1)
                if c:
                    tail(b, c - 1, t)
                pe.wait_ge(v_copied, t + 1)
                pe.wait_ge(masked, 4 * t + G)
                at_least(pe, o_gated, t)
                first = True
                if c:
                    pe.wait_ge(st_new, 3 * b + c)
                    for g in range(G):
                        pe.matmul(ps[:, PO, g * P:(g + 1) * P], q_decT[:, g, :], state[:, (c - 1) % 2, g, :],
                                  start=first, stop=False, skip_group_check=True)
                        first = False
                for h in range(H):
                    m = pe.matmul(ps[:, PO, h * HD:(h + 1) * HD], weighted[:, h, :], v[:, c % 2, h * HD:(h + 1) * HD],
                                  start=first, stop=(h == H - 1), skip_group_check=True)
                    first = False
                m.then_inc(o_made, 1)
                if c == CH - 1:
                    if not last:
                        project_v(b + 1, 0)
                        project_q(b + 1, 0)
                        project_k(b + 1, 0)
                    tail(b, c, t)

            pe.wait_ge(sort_v, 3)
            pe.wait_ge(setup, 2)
            flat = onehot[:, :, :].rearrange("p e j -> p (e j)")
            pe.matmul(ps[:, PO, 0:E1 * NT], before[:, :], flat, start=True, stop=True)
            pe.matmul(ps[:, PO, 64:64 + E1 * NT], ones[:, :], flat, start=True, stop=True).then_inc(sort_p, 1)
            pe.wait_ge(pick_v, 2)
            for k in range(KC):
                pe.matmul(ps[:, PS0, k * E2:(k + 1) * E2], gatew[:, k * P:(k + 1) * P], pick[:, :], start=True, stop=True)
            pe.matmul(ps[:, PS0, KC * E2:(KC + 1) * E2], ones[:, :], pick[:, :], start=True, stop=True).then_inc(pick_p, 1)

            pe.wait_ge(wqkv_in, 48)
            project_v(0, 0)
            project_q(0, 0)
            project_k(0, 0)
            pe.wait_ge(pick_v, 4)
            pe.wait_ge(sort_v, 5)

            def a_batch(b, last):
                for c in range(CH):
                    main(b, c, last)

            batches(pe, a_batch)

            BT, BS, BH, BY, BX, BL = 0, 1, 3, 4, 6, 7

            def expert_of(j):
                return pe.value_load(eid_i[0:1, bass.ds(j, 1)], min_val=0, max_val=E1 - 1)

            def turn_x(p, k):
                pe.wait_ge(x1_got[p], 16 * (k + 1))
                at_least(pe, xg1_copied, 2 * k + p)
                for q in range(KC):
                    m = pe.transpose(ps[:, BT, q * P:(q + 1) * P], x1g[:, p, q * P:(q + 1) * P], eye[:, :])
                m.then_inc(xg1_turned, 1)

            def up(j, p, k):
                e = expert_of(j)
                pe.wait_ge(xg1_copied, 2 * k + p + 1)
                at_least(pe, h1_made[p], k)
                for q in range(KC):
                    m = pe.matmul(ps[:, BS + p, :], x1gT[:, p, q, :], ctxw[:, bass.ds(e, 1), q, :].rearrange("p a n -> p (a n)"),
                                  start=(q == 0), stop=(q == KC - 1))
                m.then_inc(s_made, 1)

            def route(p, k):
                pe.wait_ge(x2_made, 2 * k + p + 1)
                at_least(pe, x2T_copied, 2 * k + p)
                for q in range(KC):
                    m = pe.transpose(ps[:, BX, q * P:(q + 1) * P], x2o[:, p, q * P:(q + 1) * P], eye[:, :])
                m.then_inc(x2_turned, 1)
                pe.wait_ge(x2T_copied, 2 * k + p + 1)
                at_least(pe, routed, 2 * k + p)
                for q in range(KC):
                    m = pe.matmul(ps[:, BL, 0:E2], x2T[:, q, :], router[:, q, :], start=(q == 0), stop=(q == KC - 1))
                m.then_inc(lg_made, 1)

            def b_tile(j, p, k, left):
                if not is_first(j):
                    route(*before_it(p, k))
                e = expert_of(j)
                pe.wait_ge(h1_made[p], k + 1)
                for q in range(KC):
                    m = pe.transpose(ps[:, BH, q * P:(q + 1) * P], h1[:, q * P:(q + 1) * P], eye[:, :])
                m.then_inc(h1_turned, 1)
                if left:
                    turn_x(*after_it(p, k))
                pe.wait_ge(h1_copied, 2 * k + p + 1)
                at_least(pe, r2_made[p], k)
                for q in range(KC):
                    m = pe.matmul(ps[:, BY + p, :], h1T[:, q, :], ctxw[:, bass.ds(e, 1), q, :].rearrange("p a n -> p (a n)"),
                                  start=(q == 0), stop=(q == KC - 1))
                m.then_inc(y1_made, 1)
                if left:
                    up(j + 1, *after_it(p, k))

            pe.wait_ge(r1_made, NT)
            pe.wait_ge(o_gated, NT)
            pe.wait_ge(slot_sorted, 1)
            pe.wait_ge(ctx_in, 16)
            turn_x(0, 0)
            up(0, 0, 0)
            units(pe, SLOT_T, b_tile)
            route((SLOT_T - 1) % 2, (SLOT_T - 1) // 2)

            pe.wait_ge(tab_v, 17)
            pe.wait_ge(c_half, 2)
            for half in range(2):
                js = slice(half * NT // 2, (half + 1) * NT // 2)
                out = ps[:, half, 0:NT // 2 * E2]
                pe.matmul(out, before_b[:, :], sel[:, js, :].rearrange("p j n -> p (j n)"), start=True, stop=False)
                pe.matmul(out, ones_b[:, :], sel_before[:, js, :].rearrange("p j n -> p (j n)"),
                          start=False, stop=True).then_inc(pos_made, 1)
            for g in range(NG):
                pe.wait_ge(hot_made, g + 1)
                at_least(pe, tab_cut, g - 1)
                for j in range(NT):
                    m = pe.matmul(ps[0:GE * NA, 2 + g % 2, 0:GE * NBB], hot_a[:, g % 2, j].rearrange("p n a -> p (n a)"),
                                  hot_id[:, g % 2, j].rearrange("p n b -> p (n b)"), start=(j == 0), stop=(j == NT - 1))
                m.then_inc(tab_made, 1)

            CT, CG, CY = 0, 2, 4

            def c_turn(p, k):
                pe.wait_ge(got[p], 32 * (k + 1))
                at_least(pe, c_copied, 2 * (2 * k + p))
                for q in range(KC):
                    for h in range(2):
                        o = (q % 2) * CAP + h * HALF
                        m = pe.transpose(ps[:, CT + q // 2, o:o + HALF], xg[:, p, h, q * P:(q + 1) * P], eye[0:HALF, 0:HALF])
                m.then_inc(c_turned[p], 1)

            def c_up(p, k):
                pe.wait_ge(gu_in[p], 16 * (k + 1))
                pe.wait_ge(c_copied, 2 * (2 * k + p + 1))
                at_least(pe, h_made, 2 * (2 * k + p))
                for part in range(3):
                    out = ps[:, CG, part * CAP:(part + 1) * CAP] if part < 2 else ps[:, CG + 1, 0:CAP]
                    for q in range(KC):
                        m = pe.matmul(out, wgu[p][:, q, part * P:(part + 1) * P], xgT[:, p, q, :], start=(q == 0), stop=(q == KC - 1))
                m.then_inc(gu_made[p], 1)

            def c_down(p, k):
                pe.wait_ge(dn_in[p], 32 * (k + 1))
                pe.wait_ge(h_made, 2 * (2 * k + p + 1))
                at_least(pe, y_scaled[1 - p], 2 * (k + p))
                for h in range(2):
                    cols = slice(h * HALF, (h + 1) * HALF)
                    pe.matmul(ps[0:HALF, CY + h, :], h_a[:, p, cols], wdn[p][:, 0, :], start=True, stop=False)
                    m = pe.matmul(ps[0:HALF, CY + h, :], h_c[P - FI + P:P, p, cols], wdn[p][P - FI + P:P, 1, :], start=False, stop=True)
                m.then_inc(dn_made[p], 1)

            def c_expert(n, p, k, left):
                first, last = is_first(n), left == 0
                c_up(p, k)
                if not first:
                    c_down(1 - p, k - (1 - p))
                if not last:
                    c_turn(1 - p, k + p)

            pe.wait_ge(tab_cut, NG)
            c_turn(0, 0)
            units(pe, E2, c_expert)
            c_down(1, E2 // 2 - 1)

        @block.scalar
        def _(act):
            def copy_v(b, c):
                t = 4 * b + c
                act.wait_ge(v_made, t + 1)
                if not (isinstance(t, int) and t < 2):
                    act.wait_ge(o_made, t - 1)
                act.activation(v[:, c % 2, :], ps[:, PV, :], ACT.Copy).then_inc(v_copied, 1)

            def sigmoids(b, c, which):
                t = 4 * b + c
                bank, buf, made, done, free = ((PQ, sig_q, q_made, q_sig, q_silu), (PK, sig_k, k_made, k_sig, k_silu))[which]
                act.wait_ge(made, t + 1)
                at_least(act, free, t)
                act.activation(buf[:, :], ps[:, bank, :], ACT.Sigmoid).then_inc(done, 1)

            def main(b, c, last):
                t = 4 * b + c
                act.wait_ge(q_turned, t + 1)
                for j in range(HG):
                    rows = slice(j * HD, (j + 1) * HD)
                    m = act.activation(q_blocks[rows, :, j, :], ps[rows, PT, :].rearrange("p (g t) -> p g t", g=G), ACT.Copy)
                m.then_inc(qT_copied, 1)
                act.wait_ge(g1_made, t + 1)
                act.activation(g1T[:, :], ps[0:RANK, PM, 0:P], ACT.Copy).then_inc(g1_copied, 1)
                if c < CH - 1:
                    copy_v(b, c + 1)
                act.wait_ge(gate_made, t + 1)
                at_least(act, o_gated, t)
                act.activation(sig_gate[:, :], ps[:, PM, :], ACT.Sigmoid).then_inc(gate_sig, 1)
                act.wait_ge(k_turned, t + 1)
                act.activation(whole(kT), ps[:, PT, :].rearrange("p (g t) -> p g t", g=G), ACT.Copy).then_inc(kT_copied, 1)
                if c < CH - 1:
                    sigmoids(b, c + 1, 0)
                    sigmoids(b, c + 1, 1)
                elif not last:
                    copy_v(b + 1, 0)
                    sigmoids(b + 1, 0, 0)
                    sigmoids(b + 1, 0, 1)

            copy_v(0, 0)
            sigmoids(0, 0, 0)
            sigmoids(0, 0, 1)
            act.wait_ge(zeroed, 2)

            def a_batch(b, last):
                for c in range(CH):
                    main(b, c, last)

            batches(act, a_batch)

            BT, BS, BH, BX = 0, 1, 3, 6

            def front(p, k):
                act.wait_ge(xg1_turned, 2 * k + p + 1)
                act.activation(x1gT[:, p].rearrange("p k t -> p (k t)"), ps[:, BT, :], ACT.Copy).then_inc(xg1_copied, 1)
                act.wait_ge(s_made, 2 * k + p + 1)
                at_least(act, s_silu, 2 * k + p)
                act.activation(sig_s[:, :], ps[:, BS + p, :], ACT.Sigmoid).then_inc(s_sig, 1)

            def copy_x2(p, k):
                act.wait_ge(x2_turned, 2 * k + p + 1)
                act.activation(whole(x2T).rearrange("p k t -> p (k t)"), ps[:, BX, :], ACT.Copy).then_inc(x2T_copied, 1)

            def exps(p, k):
                act.wait_ge(router_v, 4 * (2 * k + p) + 4)
                act.activation(es[:, :], logits[:, :], ACT.Sigmoid, bias=neg_max[:, 0:1]).then_inc(es_made, 1)

            def b_tile(j, p, k, left):
                if not is_first(j):
                    copy_x2(*before_it(p, k))
                act.wait_ge(h1_turned, 2 * k + p + 1)
                act.activation(whole(h1T).rearrange("p k t -> p (k t)"), ps[:, BH, :], ACT.Copy).then_inc(h1_copied, 1)
                if not is_first(j):
                    exps(*before_it(p, k))
                if left:
                    front(*after_it(p, k))

            front(0, 0)
            units(act, SLOT_T, b_tile)
            copy_x2((SLOT_T - 1) % 2, (SLOT_T - 1) // 2)
            exps((SLOT_T - 1) % 2, (SLOT_T - 1) // 2)

            CT, CG, CY = 0, 2, 4

            def load_up(n, p, k):
                at_least(act, gu_made[p], k)
                act.dma_start(wgu[p], d["gu"][bass.ds(n, 1)].rearrange("a p k o -> (a p) k o")).then_inc(gu_in[p], 16)

            def load_down(n, p, k):
                at_least(act, dn_made[p], k)
                act.dma_start(wdn[p][:, 0, :], d["dn"][bass.ds(n, 1), 0:P, :].rearrange("a p h -> (a p) h")).then_inc(dn_in[p], 16)
                act.dma_start(wdn[p][P // 2:P, 1, :], d["dn"][bass.ds(n, 1), P:FI, :].rearrange("a p h -> (a p) h")).then_inc(dn_in[p], 16)

            def copy_x(p, k):
                act.wait_ge(c_turned[p], k + 1)
                act.activation(xgT[:, p, 0:2, :], ps[:, CT, 0:2 * CAP].rearrange("p (q s) -> p q s", q=2), ACT.Copy)\
                   .then_inc(c_copied, 1)

            def scale_y(p, k):
                act.wait_ge(dn_made[p], k + 1)
                act.wait_ge(w_copied[p], k + 1)
                at_least(act, y_added[p], 32 * k)
                act.activation(ye[:, p, 0, :], ps[0:HALF, CY, :], ACT.Copy, scale=w_col[:, p, 0:1]).then_inc(y_scaled[p], 1)

            def c_expert(n, p, k, left):
                first, last = is_first(n), left == 0
                act.wait_ge(gu_made[p], k + 1)
                at_least(act, h_made, 2 * (2 * k + p))
                act.activation(sig_a[:, :], ps[:, CG, 0:CAP], ACT.Sigmoid)
                act.activation(sig_c[0:P // 2, :], ps[0:P // 2, CG + 1, 0:CAP], ACT.Sigmoid).then_inc(c_sig, 1)
                if left == 2:
                    load_up(n + 2, p, k + 1)
                if not first:
                    scale_y(1 - p, k - (1 - p))
                if not last:
                    load_down(n + 1, 1 - p, k + p)
                if not last:
                    copy_x(1 - p, k + p)

            act.wait_ge(o_made, NT)
            load_up(0, 0, 0)
            load_down(0, 0, 0)
            load_up(1, 1, 0)
            copy_x(0, 0)
            units(act, E2, c_expert)
            scale_y(1, E2 // 2 - 1)

            with act.Fori(0, NT // 2) as i:
                for p in range(2):
                    act.wait_ge(out_made[p], i + 1)
                    act.dma_start(d["out"][bass.ds(P * (2 * i + p), P), :], out_t[p]).then_inc(out_kept[p], 16)
            for p in range(2):
                act.wait_ge(out_kept[p], 16 * (NT // 2))

        @block.vector
        def _(dve):
            dve.memset(ones[:, :], 1.0).then_inc(setup, 1)
            dve.memset(zero[:, :], 0.0).then_inc(zeroed, 1)
            dve.wait_ge(consts_in, CONSTS_IN)
            dve.tensor_copy(tok_f[:, :], tok_i[:, :]).then_inc(sort_v, 1)
            dve.wait_ge(sort_v, 1)
            for e in range(E1 - 1):
                m = dve.tensor_scalar(ge[:, e, :], tok_f[:, :], float(PER * (e + 1)), None, ALU.is_ge)
            m.then_inc(sort_v, 1)
            dve.wait_ge(sort_v, 2)
            dve.tensor_scalar(onehot[:, 0, :], ge[:, 0, :], -1.0, 1.0, ALU.mult, ALU.add)
            dve.tensor_tensor(onehot[:, 1:E1 - 1, :], ge[:, 0:E1 - 2, :], ge[:, 1:E1 - 1, :], ALU.subtract)
            dve.tensor_copy(onehot[:, E1 - 1, :], ge[:, E1 - 2, :]).then_inc(sort_v, 1)
            dve.wait_ge(gate_in, 32)
            dve.tensor_copy(o2n_f[:, :], o2n_i[:, :]).then_inc(pick_v, 1)
            dve.wait_ge(pick_v, 1)
            dve.tensor_scalar(pick[:, :], n_iota[:, :], o2n_f[:, 0:1], None, ALU.is_equal).then_inc(pick_v, 1)
            dve.wait_ge(sort_p, 1)
            dve.tensor_copy(whole(total).rearrange("p e j -> p (e j)"), ps[:, PO, 64:64 + E1 * NT]).then_inc(sort_v, 1)
            dve.tensor_copy(whole(rank).rearrange("p e j -> p (e j)"), ps[:, PO, 0:E1 * NT]).then_inc(sort_v, 1)
            dve.wait_ge(sort_v, 5)
            for e in range(E1):
                m = dve.tensor_tensor_scan(cum[:, e, :], ones[:, 0:NT], total[:, e, :], 0.0, ALU.mult, ALU.add)
            m.then_inc(sort_v, 1)
            dve.wait_ge(sort_v, 6)
            for e in range(E1):
                m = dve.tensor_scalar(lot[:, e, :], tile_no[:, 0:NT], float(P), cum[:, e, NT - 1:NT], ALU.mult, ALU.is_lt)
            m.then_inc(sort_v, 1)
            dve.tensor_tensor(whole(rank), whole(rank), whole(cum), ALU.add).then_inc(sort_v, 1)
            dve.wait_ge(sort_v, 8)
            dve.tensor_reduce(tiles[:, :], whole(lot), AX.X, ALU.add).then_inc(sort_v, 1)
            dve.tensor_tensor(whole(rank), whole(rank), whole(total), ALU.subtract).then_inc(sort_v, 1)
            dve.wait_ge(sort_v, 10)
            dve.tensor_tensor_scan(tiles_cum[:, :], ones[:, 0:E1], tiles[:, :], 0.0, ALU.mult, ALU.add).then_inc(sort_v, 1)
            dve.wait_ge(sort_v, 11)
            dve.tensor_tensor(start[:, :], tiles_cum[:, :], tiles[:, :], ALU.subtract).then_inc(sort_v, 1)
            dve.tensor_scalar(eid_f[:, :], tile_no[:, :], tiles_cum[:, 0:1], None, ALU.is_ge).then_inc(sort_v, 1)
            dve.wait_ge(sort_v, 13)
            dve.tensor_scalar(start[:, :], start[:, :], float(P), None, ALU.mult).then_inc(sort_v, 1)
            for e in range(1, E1 - 1):
                dve.wait_ge(sort_v, 13 + (e > 1))
                dve.scalar_tensor_tensor(eid_f[:, :], tile_no[:, :], tiles_cum[:, e:e + 1], eid_f[:, :], ALU.is_ge, ALU.add)\
                   .then_inc(sort_v, 1)
                dve.wait_ge(sort_v, 14 + e)
            dve.tensor_copy(eid_i[:, :], eid_f[:, :]).then_inc(slot_sorted, 1)
            for e in range(E1):
                m = dve.scalar_tensor_tensor(rank[:, e, :], rank[:, e, :], start[:, e:e + 1], onehot[:, e, :], ALU.add, ALU.mult)
            m.then_inc(sort_v, 1)
            dve.wait_ge(sort_v, 17)
            dve.tensor_reduce(dest[:, :], whole(rank).rearrange("p e j -> p j e"), AX.X, ALU.add).then_inc(sort_v, 1)
            dve.wait_ge(sort_v, 18)
            dve.tensor_copy(slot_i[:, :], dest[:, :]).then_inc(sort_v, 1)
            dve.wait_ge(sort_v, 19)
            dve.tensor_single_scalar(row_i[:, :], slot_i[:, :], P - 1, ALU.bitwise_and)
            dve.tensor_single_scalar(slot_i[:, :], slot_i[:, :], 7, ALU.arith_shift_right).then_inc(sort_v, 1)
            dve.wait_ge(sort_v, 20)
            dve.scalar_tensor_tensor(dest_i[:, :], row_i[:, :], float(SLOT_T), slot_i[:, :], ALU.mult, ALU.add).then_inc(sort_v, 1)
            dve.tensor_copy(ids_i[:, :], ids[:, :]).then_inc(sort_v, 1)
            dve.wait_ge(pick_p, 1)
            dve.tensor_copy(whole(router).rearrange("p k n -> p (k n)"), ps[:, PS0, 0:KC * E2]).then_inc(pick_v, 1)
            dve.tensor_scalar(kept_bias[:, :], ps[:, PS0, KC * E2:(KC + 1) * E2], -1.0, -NEG, ALU.add, ALU.mult).then_inc(pick_v, 1)

            def silu(b, c, which):
                t = 4 * b + c
                bank, sg, x, r2_, sig, done, second, rotated = (
                    (PQ, sig_q, q_act, rot2_q, q_sig, q_silu, q_r2, q_rotated),
                    (PK, sig_k, k_act, rot2_k, k_sig, k_silu, k_r2, k_rotated))[which]
                dve.wait_ge(sig, t + 1)
                at_least(dve, rotated, t)
                dve.tensor_tensor(x[:, :], ps[:, bank, :], sg[:, :], ALU.mult).then_inc(done, 1)
                dve.wait_ge(done, t + 1)
                xv = x[:, :].rearrange("p (h a i) -> p h a i", a=2, i=HD // 2)
                rv = r2_[:, :].rearrange("p (h a i) -> p h a i", a=2, i=HD // 2)
                for a in range(2):
                    s = sin[:, c, a * HD // 2:(a + 1) * HD // 2].unsqueeze(1).to_broadcast([P, H, HD // 2])
                    m = dve.tensor_tensor(rv[:, :, a, :], xv[:, :, 1 - a, :], s, ALU.mult)
                m.then_inc(second, 1)

            def tail(b, c):
                t = 4 * b + c
                dve.wait_ge(o_turned, t + 1)
                at_least(dve, wo_made, t)
                dve.tensor_tensor(whole(oT), ps[:, PT, :].rearrange("p (k t) -> p k t", k=KC),
                                  nw[:, :].unsqueeze(2).to_broadcast([P, KC, P]), ALU.mult).then_inc(oT_copied, 1)
                dve.wait_ge(wo_made, t + 1)
                dve.wait_ge(x_in[c], 16 * (b + 1))
                at_least(dve, x1_made, t)
                dve.tensor_tensor(r1[:, :], ps[:, PM, :], x_res[:, c, :], ALU.add).then_inc(r1_made, 1)
                dve.wait_ge(r1_made, t + 1)
                dve.bn_stats(stat1[:, :], r1[:, :]).then_inc(stat1_made, 1)
                dve.wait_ge(stat1_made, t + 1)
                at_least(dve, rstd1_made, t)
                settle(dve)
                dve.bn_aggr(mv1[:, :], stat1[:, :]).then_inc(mv1_made, 1)

            def tail_norm(b, c):
                t = 4 * b + c
                dve.wait_ge(rstd1_made, t + 1)
                at_least(dve, x1_kept[c % 2], 16 * (2 * b + c // 2))
                dve.tensor_scalar(x1o[:, c % 2, :], r1[:, :], mv1[:, 0:1], rstd1[:, 0:1], ALU.subtract, ALU.mult).then_inc(x1_made, 1)

            def main(b, c, last):
                t = 4 * b + c
                dve.wait_ge(qT_copied, t + 1)
                dve.tensor_tensor(whole(q_decT), ps[:, PT, :].rearrange("p (g t) -> p g t", g=G), whole(dq), ALU.mult)\
                   .then_inc(qT_decayed, 1)
                for g in range(G):
                    dve.wait_ge(scored, 4 * t + g + 1)
                    dve.tensor_tensor(weighted[:, g * HG:(g + 1) * HG, :], ps[:, PS0 + g % 2, :].rearrange("p (h t) -> p h t", h=HG),
                                      decay[:, g * HG:(g + 1) * HG, :], ALU.mult).then_inc(masked, 1)
                if c < CH - 1:
                    silu(b, c + 1, 0)
                    n = 3 * b + c
                    dve.wait_ge(add_made, n + 1)
                    at_least(dve, st_new, n)
                    dve.tensor_tensor(whole(state_add), ps[:, PM, :].rearrange("p (g t) -> p g t", g=G),
                                      block_diag[:, :].unsqueeze(1).to_broadcast([P, G, P]), ALU.mult).then_inc(add_cut, 1)
                    dve.wait_ge(add_cut, n + 1)
                    at_least(dve, o_made, t)
                    if c:
                        dve.wait_ge(st_decayed, 2 * b + c)
                        dve.tensor_tensor(state[:, c % 2], whole(state_add), whole(state_dec), ALU.add).then_inc(st_new, 1)
                    else:
                        dve.tensor_copy(state[:, c % 2], whole(state_add)).then_inc(st_new, 1)
                if c:
                    tail(b, c - 1)
                if c < CH - 1:
                    silu(b, c + 1, 1)
                if c:
                    tail_norm(b, c - 1)
                dve.wait_ge(o_made, t + 1)
                dve.wait_ge(gate_sig, t + 1)
                at_least(dve, o_normed, t)
                dve.tensor_tensor(gated[:, :], ps[:, PO, :], sig_gate[:, :], ALU.mult).then_inc(o_gated, 1)
                dve.wait_ge(squared, t + 1)
                at_least(dve, rms_made, t)
                dve.tensor_reduce(ms[:, :], squares[:, :].rearrange("p (h i) -> p h i", h=H), AX.X, ALU.add).then_inc(ms_made, 1)
                dve.wait_ge(rms_made, t + 1)
                at_least(dve, o_turned, t)
                dve.tensor_tensor(normed[:, :].rearrange("p (h i) -> p h i", h=H), gated[:, :].rearrange("p (h i) -> p h i", h=H),
                                  rms_inv[:, :].unsqueeze(2).to_broadcast([P, H, HD]), ALU.mult).then_inc(o_normed, 1)
                if c == CH - 1:
                    if not last:
                        silu(b + 1, 0, 0)
                        silu(b + 1, 0, 1)
                    tail(b, c)
                    tail_norm(b, c)

            silu(0, 0, 0)
            silu(0, 0, 1)

            def a_batch(b, last):
                for c in range(CH):
                    main(b, c, last)

            batches(dve, a_batch)

            BS, BY, BL = 1, 4, 7

            def hidden(p, k):
                dve.wait_ge(s_sig, 2 * k + p + 1)
                at_least(dve, h1_made[1 - p], k + p)
                dve.tensor_tensor(s_act[:, :], ps[:, BS + p, :], sig_s[:, :], ALU.mult).then_inc(s_silu, 1)
                dve.wait_ge(s_silu, 2 * k + p + 1)
                at_least(dve, h1_turned, 2 * k + p)
                dve.tensor_tensor(h1[:, :], ps[:, BS + p, :], s_act[:, :], ALU.mult).then_inc(h1_made[p], 1)

            def route(p, k):
                j = 2 * k + p
                v0 = 4 * j
                dve.wait_ge(lg_made, 2 * k + p + 1)
                dve.tensor_tensor(logits[:, :], ps[:, BL, 0:E2], kept_bias[:, :], ALU.add).then_inc(router_v, 1)
                dve.wait_ge(router_v, v0 + 1)
                settle(dve)
                dve.max(top8[:, :], logits[:, :]).then_inc(router_v, 1)
                dve.wait_ge(router_v, v0 + 2)
                settle(dve)
                dve.match_replace(marked[:, :], top8[:, :], logits[:, :], TAKEN).then_inc(router_v, 1)
                dve.tensor_scalar(neg_max[:, :], top8[:, 0:1], -1.0, None, ALU.mult).then_inc(router_v, 1)
                dve.wait_ge(router_v, v0 + 4)
                dve.tensor_scalar(not_chosen[:, :], marked[:, :], TAKEN / 2, -1.0, ALU.is_le, ALU.add).then_inc(rstep, 1)
                dve.wait_ge(es_made, 2 * k + p + 1)
                r0 = 5 * j
                dve.tensor_scalar(es1[:, :], es[:, :], -1.0, 1.0, ALU.mult, ALU.add).then_inc(rstep, 1)
                dve.wait_ge(rstep, r0 + 2)
                dve.reciprocal(es_inv[:, :], es1[:, :]).then_inc(rstep, 1)
                dve.wait_ge(rstep, r0 + 3)
                dve.tensor_tensor(expo[:, :], es[:, :], es_inv[:, :], ALU.mult).then_inc(rstep, 1)
                dve.wait_ge(rstep, r0 + 4)
                dve.scalar_tensor_tensor(chosen[:, :], marked[:, :], TAKEN / 2, expo[:, :], ALU.is_le, ALU.mult,
                                         accum_out=w_sum[:, :]).then_inc(rstep, 1)
                dve.wait_ge(rstep, r0 + 5)
                dve.reciprocal(w_inv[:, :], w_sum[:, :]).then_inc(w_inverted, 1)
                dve.wait_ge(w_inverted, j + 1)
                dve.scalar_tensor_tensor(x2o[:, p, D:ROW], chosen[:, :], w_inv[:, 0:1], not_chosen[:, :], ALU.mult, ALU.add)\
                   .then_inc(routed, 1)

            def b_tile(j, p, k, left):
                if not is_first(j):
                    route(*before_it(p, k))
                dve.wait_ge(y1_made, 2 * k + p + 1)
                at_least(dve, x2_made, 2 * k + p)
                dve.tensor_tensor(r2[:, :], ps[:, BY + p, :], x1g[:, p, :], ALU.add).then_inc(r2_made[p], 1)
                dve.wait_ge(r2_made[p], k + 1)
                dve.bn_stats(stat2[:, :], r2[:, :]).then_inc(stat2_made, 1)
                dve.wait_ge(stat2_made, 2 * k + p + 1)
                settle(dve)
                dve.bn_aggr(mv2[:, :], stat2[:, :]).then_inc(mv2_made, 1)
                dve.wait_ge(rstd2_made, 2 * k + p + 1)
                at_least(dve, x2_kept[p], 16 * k)
                dve.tensor_scalar(x2o[:, p, 0:D], r2[:, :], mv2[:, 0:1], rstd2[:, 0:1], ALU.subtract, ALU.mult).then_inc(x2_made, 1)
                if left:
                    hidden(*after_it(p, k))

            hidden(0, 0)
            units(dve, SLOT_T, b_tile)
            route((SLOT_T - 1) % 2, (SLOT_T - 1) // 2)

            def cut_table(g):
                dve.wait_ge(tab_made, g + 1)
                at_least(dve, tab_summed, g)
                dve.tensor_tensor(whole(tab), ps[0:GE * NA, 2 + g % 2, 0:GE * NBB].rearrange("r (n b) -> r n b", n=GE),
                                  diag8[:, :].unsqueeze(2).to_broadcast([GE * NA, GE, NBB]), ALU.mult).then_inc(tab_masked, 1)
                dve.wait_ge(tab_masked, g + 1)
                at_least(dve, tab_cut, g)
                dve.tensor_reduce(tab_r[:, :], whole(tab).rearrange("r n b -> r b n"), AX.X, ALU.add).then_inc(tab_summed, 1)
                dve.wait_ge(tab_summed, g + 1)
                dve.scalar_tensor_tensor(tab_spare[:, :], tab_r[:, :], 0.0, place_no[:, :], ALU.is_equal, ALU.mult).then_inc(tab_spared, 1)
                dve.wait_ge(tab_spared, g + 1)
                dve.scalar_tensor_tensor(tab_i[:, g, :], tab_r[:, :], float(TOK), tab_spare[:, :], ALU.add, ALU.add).then_inc(tab_cut, 1)

            dve.memset(before_b[:, :], 0.0).then_inc(c_half, 1)
            dve.wait_ge(c_half, 1)
            dve.tensor_copy(before_b[:, :], before[:, :])
            dve.tensor_copy(ab_h[:, :], ab_iota[:, :])
            dve.tensor_scalar(ids_h[:, :], ids[:, :], -float(TOK), None, ALU.add)
            dve.tensor_copy(ones_b[:, :], ones[:, :]).then_inc(c_half, 1)
            dve.wait_ge(wnat_in, 16)
            dve.tensor_scalar(whole(sel), whole(wnat), 0.0, None, ALU.is_ge).then_inc(tab_v, 1)
            dve.memset(sel_before[:, 0, :], 0.0).then_inc(tab_v, 1)
            for j in range(1, NT):
                dve.wait_ge(tab_v, j + 1)
                dve.tensor_tensor(sel_before[:, j, :], sel_before[:, j - 1, :], sel[:, j - 1, :], ALU.add).then_inc(tab_v, 1)
            for half in range(2):
                js = slice(half * NT // 2, (half + 1) * NT // 2)
                out = ps[:, half, 0:NT // 2 * E2].rearrange("p (j n) -> p j n", n=E2)
                dve.wait_ge(pos_made, half + 1)
                dve.scalar_tensor_tensor(ok[:, js, :], out, float(CAP), sel[:, js, :], ALU.is_lt, ALU.mult).then_inc(tstep, 1)
                dve.wait_ge(tstep, 2 * half + 1)
                dve.scalar_tensor_tensor(place[:, js, :], out, 1.0, ok[:, js, :], ALU.add, ALU.mult).then_inc(tstep, 1)
            dve.wait_ge(tstep, 4)
            dve.tensor_scalar(whole(place_i), whole(place), -1.0, None, ALU.add).then_inc(tstep, 1)
            dve.wait_ge(tstep, 5)
            dve.tensor_single_scalar(whole(a_i), whole(place_i), 4, ALU.arith_shift_right)
            dve.tensor_single_scalar(whole(b_i), whole(place_i), NBB - 1, ALU.bitwise_and).then_inc(tstep, 1)
            dve.wait_ge(tstep, 6)
            dve.tensor_copy(whole(a_h), whole(a_i))
            dve.tensor_copy(whole(b_h), whole(b_i)).then_inc(tstep, 1)
            dve.wait_ge(tstep, 7)
            dve.wait_ge(c_half, 2)
            for g in range(NG):
                ns = slice(g * GE, (g + 1) * GE)
                at_least(dve, tab_made, g - 1)
                if g:
                    dve.wait_ge(hot_made, g)
                dve.tensor_tensor(hot_a[:, g % 2], a_h[:, :, ns].unsqueeze(3).to_broadcast([P, NT, GE, NA]),
                                  ab_h[:, 0:NA].unsqueeze(1).unsqueeze(1).to_broadcast([P, NT, GE, NA]), ALU.is_equal)
                dve.tensor_tensor(whole(hot_b), b_h[:, :, ns].unsqueeze(3).to_broadcast([P, NT, GE, NBB]),
                                  ab_h[:, NA:NA + NBB].unsqueeze(1).unsqueeze(1).to_broadcast([P, NT, GE, NBB]), ALU.is_equal)\
                    .then_inc(hot_b_made, 1)
                dve.wait_ge(hot_b_made, g + 1)
                dve.tensor_tensor(hot_id[:, g % 2].rearrange("p j n b -> p j (n b)"), whole(hot_b).rearrange("p j n b -> p j (n b)"),
                                  ids_h[:, :].unsqueeze(2).to_broadcast([P, NT, GE * NBB]), ALU.mult).then_inc(hot_made, 1)
                if g:
                    cut_table(g - 1)
            cut_table(NG - 1)

            CT, CG, CY = 0, 2, 4
            LO, HI = slice(0, P // 2), slice(P // 2, P)

            def copy_x(n, p, k):
                dve.wait_ge(c_turned[p], k + 1)
                dve.tensor_copy(xgT[:, p, 2:4, :], ps[:, CT + 1, 0:2 * CAP].rearrange("p (q s) -> p q s", q=2))\
                   .then_inc(c_copied, 1)
                at_least(dve, y_scaled[p], 2 * k)
                dve.tensor_copy(w_col[:, p, :], xg[:, p, :, bass.ds(n + D, 1)].rearrange("p h a -> p (h a)")).then_inc(w_copied[p], 1)

            def scale_y(p, k):
                dve.wait_ge(dn_made[p], k + 1)
                dve.wait_ge(w_copied[p], k + 1)
                at_least(dve, y_added[p], 32 * k)
                dve.tensor_scalar(ye[:, p, 1, :], ps[0:HALF, CY + 1, :], w_col[:, p, 1:2], None, ALU.mult).then_inc(y_scaled[p], 1)

            def c_expert(n, p, k, left):
                first, last = is_first(n), left == 0
                dve.wait_ge(c_sig, 2 * k + p + 1)
                at_least(dve, h_made, 2 * (2 * k + p))
                dve.tensor_tensor(g_a[:, :], ps[:, CG, 0:CAP], sig_a[:, :], ALU.mult).then_inc(g_made, 1)
                dve.tensor_tensor(g_c[HI, :], ps[LO, CG + 1, 0:CAP], sig_c[LO, :], ALU.mult).then_inc(g_made, 1)
                dve.wait_ge(g_made, 2 * (2 * k + p) + 1)
                at_least(dve, dn_made[p], k)
                dve.tensor_tensor(h_a[:, p, :], ps[:, CG, CAP:2 * CAP], g_a[:, :], ALU.mult).then_inc(h_made, 1)
                dve.wait_ge(g_made, 2 * (2 * k + p) + 2)
                dve.tensor_tensor(h_c[HI, p, :], ps[HI, CG + 1, 0:CAP], g_c[HI, :], ALU.mult).then_inc(h_made, 1)
                if not first:
                    scale_y(1 - p, k - (1 - p))
                if not last:
                    copy_x(n + 1, 1 - p, k + p)

            copy_x(0, 0, 0)
            units(dve, E2, c_expert)
            scale_y(1, E2 // 2 - 1)

            with dve.Fori(0, NT // 2) as i:
                for p in range(2):
                    t = 2 * i + p
                    dve.wait_ge(yf_in[p], 32 * (i + 1))
                    dve.tensor_tensor(r3[p], yf[p], xf[p], ALU.add).then_inc(r3_made, 1)
                    dve.wait_ge(r3_made, t + 1)
                    dve.bn_stats(stat3[:, :], r3[p]).then_inc(stat3_made, 1)
                    dve.wait_ge(stat3_made, t + 1)
                    settle(dve)
                    dve.bn_aggr(mv3[:, :], stat3[:, :]).then_inc(mv3_made, 1)
                    dve.wait_ge(rstd3_made, t + 1)
                    dve.wait_ge(out_kept[p], 16 * i)
                    dve.tensor_scalar(out_t[p], r3[p], mv3[:, 0:1], rstd3[:, 0:1], ALU.subtract, ALU.mult).then_inc(out_made[p], 1)

        @block.gpsimd
        def _(pool):
            pool.memset(minus_half[:, :], -0.5).then_inc(setup, 1)
            pool.memset(whole(q_blocks), 0.0).then_inc(zeroed, 1)

            def rotate(b, c, which):
                t = 4 * b + c
                x, r1_, r2_, out, silu_, one, two, done, turned = (
                    (q_act, rot1_q, rot2_q, q_rot, q_silu, q_r1, q_r2, q_rotated, q_turned),
                    (k_act, rot1_k, rot2_k, k_rot, k_silu, k_r1, k_r2, k_rotated, k_turned))[which]
                heads = lambda z: z[:, :].rearrange("p (h i) -> p h i", h=H)
                pool.wait_ge(silu_, t + 1)
                pool.tensor_tensor(heads(r1_), heads(x), cos[:, c, :].unsqueeze(1).to_broadcast([P, H, HD]), ALU.mult).then_inc(one, 1)
                pool.wait_ge(one, t + 1)
                pool.wait_ge(two, t + 1)
                at_least(pool, turned, t)
                if which:
                    at_least(pool, k_decayed, 3 * b + c)
                pool.tensor_tensor(out[:, :], r1_[:, :], r2_[:, :], ALU.add).then_inc(done, 1)
                if which and c < CH - 1:
                    pool.wait_ge(done, t + 1)
                    at_least(pool, add_made, 3 * b + (c - 1 if c else 0))
                    pool.tensor_tensor(k_dec[:, c % 2, :].rearrange("p (h i) -> p h i", h=H),
                                       heads(out), dk[:, :].unsqueeze(2).to_broadcast([P, H, HD]), ALU.mult).then_inc(k_decayed, 1)

            def rstd1_of(t):
                pool.wait_ge(mv1_made, t + 1)
                settle(pool)
                pool.tensor_scalar(ve1[:, :], mv1[:, 1:2], 1.0, LN_EPS, ALU.mult, ALU.add).then_inc(ve1_made, 1)
                pool.wait_ge(ve1_made, t + 1)
                at_least(pool, x1_made, t)
                pool.tensor_tensor(rstd1[:, :], ve1[:, :], minus_half[:, 0:1], ALU.pow).then_inc(rstd1_made, 1)

            def main(b, c, last):
                t = 4 * b + c
                if c < CH - 1:
                    rotate(b, c + 1, 0)
                    if c:
                        pool.wait_ge(st_new, 3 * b + c)
                        pool.tensor_tensor(whole(state_dec), state[:, (c - 1) % 2], lam[:, :].unsqueeze(2).to_broadcast([P, G, P]),
                                           ALU.mult).then_inc(st_decayed, 1)
                if c:
                    rstd1_of(t - 1)
                if c < CH - 1:
                    rotate(b, c + 1, 1)
                pool.wait_ge(o_gated, t + 1)
                pool.tensor_tensor(squares[:, :], gated[:, :], gated[:, :], ALU.mult).then_inc(squared, 1)
                pool.wait_ge(ms_made, t + 1)
                settle(pool)
                pool.tensor_scalar(ms_eps[:, :], ms[:, :], 1.0 / HD, RMS_EPS, ALU.mult, ALU.add).then_inc(ms_plus, 1)
                pool.wait_ge(ms_plus, t + 1)
                at_least(pool, o_normed, t)
                pool.tensor_tensor(rms_inv[:, :], ms_eps[:, :], minus_half[:, :], ALU.pow).then_inc(rms_made, 1)
                if c == CH - 1:
                    if not last:
                        rotate(b + 1, 0, 0)
                        rotate(b + 1, 0, 1)
                    rstd1_of(t)

            pool.wait_ge(sort_v, 22)
            pool.wait_ge(slots_cleared, 16)
            for j in range(NT):
                pool.indirect_dma_start(out=token_of_slot_d, out_offset=bass.IndirectOffsetOnAxis(ap=dest_i[:, j:j + 1], axis=0),
                                        in_=ids_i[:, j:j + 1], in_offset=None).then_inc(slots_named, 16)
            pool.wait_ge(setup, 2)
            rotate(0, 0, 0)
            rotate(0, 0, 1)

            def a_batch(b, last):
                for c in range(CH):
                    main(b, c, last)

            batches(pool, a_batch)

            def gather(j, p, k):
                at_least(pool, r2_made[p], k)
                at_least(pool, x1_got[p], 16 * k)
                pool.tensor_copy(idx_g[:, p:p + 1], slot_token[:, bass.ds(j, 1)]).then_inc(idx_g_set, 1)
                pool.wait_ge(idx_g_set, 2 * k + p + 1)
                settle(pool)
                pool.indirect_dma_start(out=x1g[:, p, :], out_offset=None, in_=x1_d,
                                        in_offset=bass.IndirectOffsetOnAxis(ap=idx_g[:, p:p + 1].bitcast(U32), axis=0)).then_inc(x1_got[p], 16)

            def scatter(j, p, k):
                at_least(pool, x2_kept[p], 16 * k)
                pool.tensor_copy(idx_s[:, p:p + 1], slot_token[:, bass.ds(j, 1)]).then_inc(idx_s_set, 1)
                pool.wait_ge(idx_s_set, 2 * k + p + 1)
                pool.wait_ge(routed, 2 * k + p + 1)
                settle(pool)
                pool.indirect_dma_start(out=x2_d, out_offset=bass.IndirectOffsetOnAxis(ap=idx_s[:, p:p + 1].bitcast(U32), axis=0),
                                        in_=x2o[:, p, :], in_offset=None).then_inc(x2_kept[p], 16)

            def b_tile(j, p, k, left):
                if not is_first(j):
                    scatter(j - 1, *before_it(p, k))
                pool.wait_ge(mv2_made, 2 * k + p + 1)
                settle(pool)
                pool.tensor_scalar(ve2[:, :], mv2[:, 1:2], 1.0, LN_EPS, ALU.mult, ALU.add).then_inc(ve2_made, 1)
                pool.wait_ge(ve2_made, 2 * k + p + 1)
                pool.tensor_tensor(rstd2[:, :], ve2[:, :], minus_half[:, 0:1], ALU.pow).then_inc(rstd2_made, 1)
                if left == 2:
                    gather(j + 2, p, k + 1)

            pool.wait_ge(slot_token_in, 16)
            pool.wait_ge(rows_cleared, 4 * 16 * SPARE // P)
            pool.wait_ge(x1_kept[0], 16 * NT // 2)
            pool.wait_ge(x1_kept[1], 16 * NT // 2)
            gather(0, 0, 0)
            gather(1, 1, 0)
            units(pool, SLOT_T, b_tile)
            scatter(SLOT_T - 1, (SLOT_T - 1) % 2, (SLOT_T - 1) // 2)

            def c_gather(n, p, k):
                at_least(pool, w_copied[p], k)
                at_least(pool, c_turned[p], k)
                at_least(pool, got[p], 32 * k)
                pool.tensor_copy(cidx_g[:, p, :], place_token[:, bass.ds(n, 1), :].rearrange("p a h -> p (a h)")).then_inc(cg_set, 1)
                pool.wait_ge(cg_set, 2 * k + p + 1)
                settle(pool)
                for h in range(2):
                    pool.indirect_dma_start(out=xg[:, p, h, :], out_offset=None, in_=x2_d,
                                            in_offset=bass.IndirectOffsetOnAxis(ap=cidx_g[:, p, h:h + 1].bitcast(U32), axis=0))\
                        .then_inc(got[p], 16)

            def c_scatter(n, p, k):
                at_least(pool, y_added[p], 32 * k)
                pool.tensor_copy(cidx_s[:, p, :], place_token[:, bass.ds(n, 1), :].rearrange("p a h -> p (a h)")).then_inc(cs_set, 1)
                pool.wait_ge(cs_set, 2 * k + p + 1)
                pool.wait_ge(y_scaled[p], 2 * (k + 1))
                at_least(pool, y_added[1 - p], 32 * (k + p))
                settle(pool)
                for h in range(2):
                    pool.indirect_dma_start(out=y_d, out_offset=bass.IndirectOffsetOnAxis(ap=cidx_s[:, p, h:h + 1].bitcast(U32), axis=0),
                                            in_=ye[:, p, h, :], in_offset=None, compute_op=ALU.add).then_inc(y_added[p], 16)

            def c_expert(n, p, k, left):
                if left:
                    c_gather(n + 1, *after_it(p, k))
                if not is_first(n):
                    c_scatter(n - 1, *before_it(p, k))

            pool.wait_ge(place_token_in, 16 * NG)
            pool.wait_ge(y_cleared, 16 * NT)
            c_gather(0, 0, 0)
            units(pool, E2, c_expert)
            c_scatter(E2 - 1, 1, E2 // 2 - 1)

            with pool.Fori(0, NT) as t:
                pool.wait_ge(mv3_made, t + 1)
                settle(pool)
                pool.tensor_scalar(ve3[:, :], mv3[:, 1:2], 1.0, LN_EPS, ALU.mult, ALU.add).then_inc(ve3_made, 1)
                pool.wait_ge(ve3_made, t + 1)
                pool.tensor_tensor(rstd3[:, :], ve3[:, :], minus_half[:, 0:1], ALU.pow).then_inc(rstd3_made, 1)


def kernel(**inputs):
    import concourse.bacc as bacc
    from concourse.bass_utils import run_bass_kernel_spmd as run

    a = {k: np.asarray(v) for k, v in inputs.items()}
    x = a["x"].reshape(TOK, D)

    def rows(w):
        return w.reshape(KC, P, -1).transpose(1, 0, 2)

    gu = a["L0_ffn_gate_up_proj"]
    gu = np.concatenate([gu[:, 0:P], gu[:, FI:FI + P], gu[:, P:FI], gu[:, FI + P:]], 1)
    arrays = {
        "x": x,
        "xT": x.reshape(NT, P, KC, P).transpose(0, 3, 2, 1),
        "wqkv": np.stack([rows(a["L0_attn_W" + n]) for n in "qkv"], 2),
        "wo": rows(a["L0_attn_Wo"]),
        "wg1": rows(a["L0_attn_Wg1"]),
        "wg2": a["L0_attn_Wg2"],
        "nw": a["L0_attn_norm_weight"].reshape(KC, P).T,
        "ctxw": a["ctx_2048"].reshape(E1, D, KC, P).transpose(3, 0, 2, 1),
        "tok": a["itok_BxS_13_99985"].reshape(NT, P).T,
        "gate_weight": a["L0_ffn_gate_weight"],
        "o2n": a["L0_ffn_old_to_new"].reshape(OLD, 1),
        "gu": gu.reshape(E2, 2 * FI, KC, P).transpose(0, 3, 2, 1),
        "dn": a["L0_ffn_down_proj"].transpose(0, 2, 1),
        **shape_constants(),
    }
    arrays = {"in_" + k: np.ascontiguousarray(v) for k, v in arrays.items()}
    nc = bacc.Bacc("TRN2", target_bir_lowering=False, num_devices=1)
    d = {k[3:]: nc.dram_tensor(k, v.shape, mybir.dt.from_np(v.dtype), kind="ExternalInput").ap() for k, v in arrays.items()}
    d["out"] = nc.dram_tensor("out", (TOK, D), F32, kind="ExternalOutput").ap()
    build(nc, d)
    r = run(nc, [arrays], core_ids=[0])
    return np.asarray(r.results[0]["out"]).reshape(a["x"].shape)
```

```python
from contextlib import ExitStack

import numpy as np
import concourse.bass as bass
from concourse import mybir

F32 = mybir.dt.float32
BF16 = mybir.dt.bfloat16
F16 = mybir.dt.float16
I32 = mybir.dt.int32
U32 = mybir.dt.uint32
ALU = mybir.AluOpType
ACT = mybir.ActivationFunctionType
AX = mybir.AxisListType

P = 128
D = 512
KC = D // P
NB, SEQ = 4, 512
CH = SEQ // P
TOK = NB * SEQ
NT = TOK // P
H, HD = 16, 32
G = D // P
HG = P // HD
RANK = 32
LN_EPS, RMS_EPS = 1e-5, 1e-6

E1 = 4
VOCAB = 25000
PER = VOCAB // E1
SLOT_T = NT + E1 - 1
SLOTS = SLOT_T * P

OLD, E2, TOPK = 128, 48, 8
FI = 192
CAP = 192
HALF = CAP // 2
NA, NBB = 12, 16
GE = 8
NG = E2 // GE
PART = (NT - 1) // (NG - 1)
assert PART * (NG - 1) == NT - 1
ROW = D + E2
SPARE = 2 * P
ARENA = 22 * 1024
NEG = -1e30
TAKEN = -3e38


ATTN_PACK = [("eye", P, (P,)), ("cos", P, (CH, HD)), ("sin", P, (CH, HD)), ("dk", P, (H,)), ("lam", P, (G,)), ("nw", P, (KC,)),
             ("dq", P, (G, P)), ("block", P, (P,)), ("wg1", P, (KC, RANK))]
SORT_PACK = [("before", P, (P,)), ("ids", P, (NT,)), ("tile_no", P, (SLOT_T,)), ("n_iota", P, (E2,)),
             ("ab_iota", P, (NA + NBB,)), ("place_no", GE * NA, (NBB,)), ("diag8", GE * NA, (GE,))]


def pack_rows(arrays, parts):
    out = np.zeros((P, sum(int(np.prod(shape)) for _, _, shape in parts)), np.float32)
    at = 0
    for name, rows, shape in parts:
        n = int(np.prod(shape))
        out[0:rows, at:at + n] = arrays.pop(name).reshape(rows, n)
        at += n
    return out


def shape_constants():
    f = np.float32
    i = np.arange(P)
    lam = -(f(2.0) ** (f(-8.0) * (np.arange(H, dtype=f) + f(1)) / f(H))).astype(f)
    diff = (i[None, :] - i[:, None]).astype(f)
    decay = np.where(diff[:, None, :] >= 0, np.exp(lam[None, :, None] * np.maximum(diff, 0)[:, None, :]), 0).astype(f)
    dq = np.exp(lam[:, None] * (i[None, :].astype(f) + f(1)))
    dk = np.exp(lam[None, :] * (f(P - 1) - i[:, None].astype(f)))
    lam_c = np.exp(lam * f(P))
    theta = f(10000.0) ** (f(-2.0) * np.arange(HD // 2, dtype=f) / f(HD))
    ang = (np.arange(SEQ, dtype=f)[:, None] * theta[None, :].astype(f)).astype(f)
    cos, sin = np.cos(ang).astype(f), np.sin(ang).astype(f)
    cos2 = np.concatenate([cos, cos], 1).reshape(CH, P, HD).transpose(1, 0, 2)
    sin2 = np.concatenate([-sin, sin], 1).reshape(CH, P, HD).transpose(1, 0, 2)
    by_row = np.repeat(np.arange(HG), HD)
    dq_t = np.stack([dq[g * HG + by_row] for g in range(G)], 1)
    lam_t = np.stack([lam_c[g * HG + by_row] for g in range(G)], 1)
    c = {
        "eye": np.eye(P), "decay": decay, "dq": dq_t, "dk": dk, "lam": lam_t, "cos": cos2, "sin": sin2,
        "block": (by_row[:, None] == by_row[None, :]),
        "before": (i[:, None] < i[None, :]),
        "ids": (i[:, None] + P * np.arange(NT)[None, :]),
        "tile_no": np.broadcast_to(np.arange(SLOT_T), (P, SLOT_T)),
        "n_iota": np.broadcast_to(np.arange(E2), (P, E2)),
        "ab_iota": np.broadcast_to(np.concatenate([np.arange(NA), np.arange(NBB)]), (P, NA + NBB)),
        "place_no": (NBB * (np.arange(GE * NA)[:, None] % NA) + np.arange(NBB)[None, :]),
        "diag8": (np.arange(GE * NA)[:, None] // NA == np.arange(GE)[None, :]),
    }
    c = {k: np.ascontiguousarray(v, dtype=f) for k, v in c.items()}
    c["spare"] = (TOK + i[:, None] + P * (np.arange(SLOT_T)[None, :] % 2)).astype(np.int32)
    return c


def build(nc, d):
    with ExitStack() as ctx:
        def sb(name, shape, dt=F32):
            return ctx.enter_context(nc.sbuf_tensor(name, shape, dt))

        def sem(name):
            return ctx.enter_context(nc.semaphore(name))

        def sem2(name):
            return [sem(name + "_even"), sem(name + "_odd")]

        def unpack(name, parts):
            pack = sb(name, [P, sum(int(np.prod(shape)) for _, _, shape in parts)])
            packs[name] = pack
            views, at = [], 0
            for _, rows, shape in parts:
                n = int(np.prod(shape))
                part = pack[0:rows, at:at + n]
                if len(shape) == 2:
                    part = part.rearrange("p (a b) -> p a b", b=shape[1])
                views.append(part)
                at += n
            return views

        packs = {}

        def whole(t):
            return t[(slice(None),) * len(t.shape)]

        arena = sb("arena", [P, ARENA])
        cut = [0]

        def take(name, shape, dt=F32):
            words = int(np.prod(shape[1:])) * mybir.dt.size(dt) // 4
            at, cut[0] = cut[0], cut[0] + (words + 7) // 8 * 8
            assert cut[0] <= ARENA, (name, cut[0])
            part = arena[0:shape[0], at:at + words]
            if dt != F32:
                part = part.bitcast(dt)
            axes = "abcd"[:len(shape) - 1]
            if len(axes) == 1:
                return part
            return part.rearrange(f"p ({' '.join(axes)}) -> p {' '.join(axes)}", **dict(zip(axes[1:], shape[2:])))

        x1_d = nc.dram_tensor("x1_rows", (TOK + SPARE, D), F32, kind="Internal").ap()
        x2_d = nc.dram_tensor("x2_rows", (TOK + SPARE, ROW), F32, kind="Internal").ap()
        y_d = nc.dram_tensor("y_rows", (TOK + SPARE, D), F32, kind="Internal").ap()
        token_of_slot_d = nc.dram_tensor("token_of_slot", (SLOTS, 1), I32, kind="Internal").ap()
        token_of_place_d = nc.dram_tensor("token_of_place", (E2 * CAP, 1), I32, kind="Internal").ap()

        eye, cos, sin, dk, lam, nw, dq, block_diag, wg1 = unpack("attn_pack", ATTN_PACK)
        before, ids, tile_no, n_iota, ab_iota, place_no, diag8 = unpack("sort_pack", SORT_PACK)
        wqkv = sb("wqkv", [P, KC, 3, D])
        wo = sb("wo", [P, KC, D])
        wg2 = sb("wg2", [RANK, D])
        ctxw = sb("ctxw", [P, E1, KC, D])
        gatew = sb("gatew", [OLD, D])
        o2n_i = sb("o2n_i", [OLD, 1], I32)

        ones = sb("ones", [P, P])
        zero = sb("zero", [P, D])
        minus_half = sb("minus_half", [P, H])

        decay = take("decay", [P, H, P])
        xT = take("xT", [P, CH, KC, P])
        x_res = sb("x_res", [P, CH, D])
        sig_q = take("sig_q", [P, D]); sig_k = take("sig_k", [P, D])
        q_act = take("q_act", [P, D]); k_act = take("k_act", [P, D])
        rot1_q = take("rot1_q", [P, D]); rot1_k = take("rot1_k", [P, D])
        rot2_q = take("rot2_q", [P, D]); rot2_k = take("rot2_k", [P, D])
        q_rot = take("q_rot", [P, D]); k_rot = take("k_rot", [P, D])
        k_dec = take("k_dec", [P, 2, D])
        v = take("v", [P, 2, D])
        q_blocks = take("q_blocks", [P, G, HG, P])
        q_decT = take("q_decT", [P, G, P])
        kT = take("kT", [P, G, P])
        weighted = take("weighted", [P, H, P])
        g1T = take("g1T", [RANK, P])
        sig_gate = take("sig_gate", [P, D])
        state = take("state", [P, 2, G, P])
        state_dec = take("state_dec", [P, G, P])
        state_add = take("state_add", [P, G, P])
        gated = take("gated", [P, D])
        squares = take("squares", [P, D])
        ms = take("ms", [P, H]); ms_eps = take("ms_eps", [P, H]); rms_inv = take("rms_inv", [P, H])
        normed = take("normed", [P, D])
        oT = take("oT", [P, KC, P])
        r1 = take("r1", [P, D])
        stat1 = take("stat1", [P, 6]); mv1 = take("mv1", [P, 2]); ve1 = take("ve1", [P, 1]); rstd1 = take("rstd1", [P, 1])
        x1o = sb("x1o", [P, 2, D])
        tok_i = sb("tok_i", [P, NT], I32)
        tok_f = sb("tok_f", [P, NT])
        ge = sb("ge", [P, E1 - 1, NT])
        onehot = sb("onehot", [P, E1, NT])
        total = sb("total", [P, E1, NT])
        cum = sb("cum", [P, E1, NT])
        rank = sb("rank", [P, E1, NT])
        lot = sb("lot", [P, E1, NT])
        tiles = sb("tiles", [P, E1])
        tiles_cum = sb("tiles_cum", [P, E1])
        start = sb("start", [P, E1])
        dest = sb("dest", [P, NT])
        slot_i = sb("slot_i", [P, NT], I32)
        row_i = sb("row_i", [P, NT], I32)
        dest_i = sb("dest_i", [P, NT], U32)
        ids_i = sb("ids_i", [P, NT], I32)
        spare_i = sb("spare_i", [P, SLOT_T], I32)
        name_to = sb("name_to", [P, 1], U32)
        name_of = sb("name_of", [P, 1], I32)
        eid_f = sb("eid_f", [P, SLOT_T])
        eid_i = sb("eid_i", [P, SLOT_T], I32)

        slot_token = sb("slot_token", [P, SLOT_T], I32)
        idx_g = sb("idx_g", [P, 2], I32)
        idx_s = sb("idx_s", [P, 2], I32)
        x1g = sb("x1g", [P, 2, D])
        x1gT = sb("x1gT", [P, 2, KC, P])
        sig_s = sb("sig_s", [P, D])
        s_act = sb("s_act", [P, D])
        h1 = sb("h1", [P, D])
        h1T = sb("h1T", [P, KC, P])
        r2 = sb("r2", [P, D])
        stat2 = sb("stat2", [P, 6]); mv2 = sb("mv2", [P, 2]); ve2 = sb("ve2", [P, 1]); rstd2 = sb("rstd2", [P, 1])
        x2o = sb("x2o", [P, 2, ROW])
        x2T = sb("x2T", [P, KC, P])
        router = sb("router", [P, KC, E2])
        o2n_f = sb("o2n_f", [OLD, 1])
        pick = sb("pick", [OLD, E2])
        kept_bias = sb("kept_bias", [P, E2])
        logits = sb("logits", [P, E2])
        top8 = sb("top8", [P, TOPK])
        marked = sb("marked", [P, E2])
        neg_max = sb("neg_max", [P, 1])
        es = sb("es", [P, E2]); es1 = sb("es1", [P, E2]); es_inv = sb("es_inv", [P, E2])
        expo = sb("expo", [P, E2])
        chosen = sb("chosen", [P, E2])
        w_sum = sb("w_sum", [P, 1]); w_inv = sb("w_inv", [P, 1])
        not_chosen = sb("not_chosen", [P, E2])

        cut[0] = 0
        wnat = take("wnat", [P, NT, E2])
        sel = take("sel", [P, NT, E2], BF16)
        sel_before = take("sel_before", [P, NT, E2], BF16)
        before_b = take("before_b", [P, P], BF16)
        ones_b = take("ones_b", [P, P], BF16)
        ok = take("ok", [P, NT, E2])
        place = take("place", [P, NT, E2])
        place_i = take("place_i", [P, NT, E2], I32)
        a_i = take("a_i", [P, NT, E2], I32)
        b_i = take("b_i", [P, NT, E2], I32)
        a_h = take("a_h", [P, NT, E2], F16)
        b_h = take("b_h", [P, NT, E2], F16)
        ab_h = take("ab_h", [P, NA + NBB], F16)
        ids_h = take("ids_h", [P, NT], F16)
        hot_a = take("hot_a", [P, NT, GE, NA], F16)
        hot_b = take("hot_b", [P, NT, GE, NBB], F16)
        hot_id = take("hot_id", [P, NT, GE, NBB], F16)
        tab = take("tab", [GE * NA, GE, NBB])
        tab_r = take("tab_r", [GE * NA, NBB])
        tab_spare = take("tab_spare", [GE * NA, NBB])
        tab_i = take("tab_i", [GE * NA, NBB], I32)

        wgu = [wqkv[:, k, :, :].rearrange("p a b -> p (a b)").rearrange("p (k o) -> p k o", k=KC) for k in range(2)]
        wdn = [wqkv[:, 2 + k, 0:2, :] for k in range(2)]
        place_token = take("place_token", [HALF, E2, 2], I32)
        cidx_g = take("cidx_g", [HALF, 2, 2], I32)
        cidx_s = take("cidx_s", [HALF, 2, 2], I32)
        xg = take("xg", [HALF, 2, 2, ROW])
        xgT = take("xgT", [P, 2, KC, CAP])
        w_col = take("w_col", [HALF, 2, 2])
        sig_a = take("sig_a", [P, CAP]); sig_c = take("sig_c", [P, CAP])
        g_a = take("g_a", [P, CAP]); g_c = take("g_c", [P, CAP])
        h_a = take("h_a", [P, 2, CAP])
        h_c = take("h_c", [P, 2, CAP])
        ye = take("ye", [HALF, 2, 2, D])

        cut[0] = 0
        y_all = take("y_all", [P, NT, D])
        x2_all = whole(ctxw).rearrange("p e k n -> p (e k) n")
        stat3 = sb("stat3", [P, NT, 6]); mv3 = sb("mv3", [P, NT, 2]); ve3 = sb("ve3", [P, NT]); rstd3 = sb("rstd3", [P, NT])
        shift3 = sb("shift3", [P, NT])

        ps = ctx.enter_context(nc.psum_tensor("ps", [P, 8, 512], F32))
        PQ, PK, PV, PT, PS0, PO, PM = 0, 1, 2, 3, 4, 6, 7

        attn_in = sem("attn_in"); late_in = sem("late_in"); sort_in = sem("sort_in"); gate_in = sem("gate_in"); ctx_in = sem("ctx_in"); wqk_in = sem("wqk_in"); wv_in = sem("wv_in")
        xT_in = [sem(f"xT_in{c}") for c in range(CH)]
        x_in = [sem(f"x_in{c}") for c in range(CH)]
        setup = sem("setup"); zeroed = sem("zeroed"); sort_v = sem("sort_v"); sort_p = sem("sort_p")
        slot_sorted = sem("slot_sorted"); slots_cleared = sem("slots_cleared"); slots_named = sem("slots_named"); name_set = sem("name_set")
        rows_cleared = sem("rows_cleared")
        v_made = sem("v_made"); q_made = sem("q_made"); k_made = sem("k_made")
        v_copied = sem("v_copied"); q_sig = sem("q_sig"); k_sig = sem("k_sig")
        q_silu = sem("q_silu"); k_silu = sem("k_silu")
        q_r1 = sem("q_r1"); k_r1 = sem("k_r1"); q_r2 = sem("q_r2"); k_r2 = sem("k_r2")
        q_rotated = sem("q_rotated"); k_rotated = sem("k_rotated"); k_decayed = sem("k_decayed")
        q_turned = sem("q_turned"); k_turned = sem("k_turned")
        qT_copied = sem("qT_copied"); qT_decayed = sem("qT_decayed"); kT_copied = sem("kT_copied")
        g1_made = sem("g1_made"); g1_copied = sem("g1_copied"); gate_made = sem("gate_made"); gate_sig = sem("gate_sig")
        scored = sem("scored"); masked = sem("masked")
        add_made = sem("add_made"); add_cut = sem("add_cut"); st_decayed = sem("st_decayed"); st_new = sem("st_new")
        o_made = sem("o_made"); o_gated = sem("o_gated"); squared = sem("squared"); ms_made = sem("ms_made")
        ms_plus = sem("ms_plus"); rms_made = sem("rms_made"); o_normed = sem("o_normed")
        o_turned = sem("o_turned"); oT_copied = sem("oT_copied"); wo_made = sem("wo_made")
        r1_made = sem("r1_made"); stat1_made = sem("stat1_made"); mv1_made = sem("mv1_made")
        ve1_made = sem("ve1_made"); rstd1_made = sem("rstd1_made"); x1_made = sem("x1_made"); x1_kept = sem2("x1_kept")
        slot_token_in = sem("slot_token_in"); idx_g_set = sem("idx_g_set"); idx_s_set = sem("idx_s_set"); x1_got = sem2("x1_got")
        xg1_turned = sem("xg1_turned"); xg1_copied = sem("xg1_copied"); s_made = sem("s_made"); s_sig = sem("s_sig")
        s_silu = sem("s_silu"); h1_made = sem2("h1_made"); h1_turned = sem("h1_turned"); h1_copied = sem("h1_copied")
        y1_made = sem("y1_made"); r2_made = sem2("r2_made"); stat2_made = sem("stat2_made"); mv2_made = sem("mv2_made")
        ve2_made = sem("ve2_made"); rstd2_made = sem("rstd2_made"); x2_made = sem("x2_made")
        x2_turned = sem("x2_turned"); x2T_copied = sem("x2T_copied"); lg_made = sem("lg_made")
        router_v = sem("router_v"); rstep = sem("weights_v"); w_inverted = sem("w_inverted"); es_made = sem("es_made"); routed = sem("routed"); x2_kept = sem2("x2_kept")
        pick_v = sem("pick_v"); pick_p = sem("pick_p")
        wnat_in = sem("wnat_in"); tab_v = sem("tab_v"); pos_made = sem("pos_made"); hot_made = sem("hot_made")
        tab_made = sem("tab_made"); tab_cut = sem("tab_cut"); places_kept = sem("places_kept")
        c_half = sem("c_half"); tstep = sem("place_v"); hot_b_made = sem("hot_b_made")
        tab_masked = sem("tab_masked"); tab_summed = sem("tab_summed"); tab_spared = sem("tab_spared"); passed = sem("passed")
        gu_in = sem2("gu_in"); dn_in = sem2("dn_in"); place_token_in = sem("place_token_in"); cg_set = sem("cg_set"); cs_set = sem("cs_set")
        got = sem2("got"); c_turned = sem2("c_turned"); c_copied = sem("c_copied"); w_copied = sem2("w_copied")
        gu_made = sem2("gu_made"); c_sig = sem("c_sig"); g_made = sem("g_made"); h_made = sem("h_made")
        dn_made = sem2("dn_made"); y_scaled = sem2("y_scaled"); y_added = sem2("y_added"); y_cleared = sem("y_cleared")
        y_in = sem2("y_in"); x2_in = sem("x2_in"); shift_made = sem("shift_made"); r3_made = sem("r3_made"); stat3_made = sem("stat3_made"); mv3_made = sem("mv3_made")
        ve3_made = sem("ve3_made"); rstd3_made = sem("rstd3_made"); out_made = sem("out_made"); out_kept = sem("out_kept")

        def tiles_of_a(eng, step):
            for c in range(CH - 1):
                step(0, c, c == 0, False)
            with eng.Fori(0, NB - 1) as i:
                step(i, CH - 1, False, False)
                for c in range(CH - 1):
                    step(i + 1, c, False, False)
            step(NB - 1, CH - 1, False, True)

        def next_of(b, c):
            return (b, c + 1) if c < CH - 1 else (b + 1, 0)

        def last_of(b, c):
            return (b, c - 1) if c else (b - 1, CH - 1)

        def at_least(eng, s, n):
            if not (isinstance(n, int) and n <= 0):
                eng.wait_ge(s, n)

        def settle(eng):
            eng.sem_inc(passed, 1)

        def is_first(n):
            return isinstance(n, int) and n == 0

        def slot_tiles(eng, step):
            pairs = (SLOT_T - 5) // 2
            for n in range(3):
                step(n, n % 2, n // 2, 2)
            with eng.Fori(0, pairs) as i:
                step(2 * i + 3, 1, i + 1, 2)
                step(2 * i + 4, 0, i + 2, 2)
            for n in range(2 * pairs + 3, SLOT_T):
                step(n, n % 2, n // 2, min(SLOT_T - 1 - n, 2))

        def experts(eng, step, between=None):
            for n in range(3):
                step(n, n % 2, n // 2, 2)
            with eng.Fori(0, NG - 1) as g:
                for m in range(GE):
                    if between:
                        between(g, m)
                    step(GE * g + 3 + m, (3 + m) % 2, (GE // 2) * g + (3 + m) // 2, 2)
            for n in range(E2 - 5, E2):
                step(n, n % 2, n // 2, min(E2 - 1 - n, 2))

        def before_it(p, k):
            return 1 - p, k - (1 - p)

        def after_it(p, k):
            return 1 - p, k + p

        block = ctx.enter_context(nc.Block())

        @block.sync
        def _(sp):
            sp.dma_start(whole(packs["sort_pack"]), d["sort_pack"]).then_inc(sort_in, 16)
            sp.dma_start(tok_i[:, :], d["tok"]).then_inc(sort_in, 16)
            sp.dma_start(xT[:, 0], d["xT"][0]).then_inc(xT_in[0], 16)
            sp.dma_start(wqkv[:, :, 2, :], d["wqkv"][:, :, 2, :]).then_inc(wv_in, 16)
            sp.dma_start(gatew[:, :], d["gate_weight"]).then_inc(gate_in, 16)
            sp.dma_start(o2n_i[:, :], d["o2n"]).then_inc(gate_in, 16)
            for n in range(2):
                sp.dma_start(wqkv[:, :, n, :], d["wqkv"][:, :, n, :]).then_inc(wqk_in, 16)
            sp.dma_start(whole(packs["attn_pack"]), d["attn_pack"]).then_inc(attn_in, 16)
            sp.dma_start(xT[:, 1], d["xT"][1]).then_inc(xT_in[1], 16)
            sp.dma_start(wg2[:, :], d["wg2"]).then_inc(late_in, 16)
            sp.dma_start(whole(decay), d["decay"]).then_inc(late_in, 16)
            sp.dma_start(whole(wo), d["wo"]).then_inc(late_in, 16)
            sp.dma_start(spare_i[:, :], d["spare"]).then_inc(late_in, 16)
            for c in range(2, CH):
                sp.dma_start(xT[:, c], d["xT"][c]).then_inc(xT_in[c], 16)
            for c in range(CH):
                sp.dma_start(x_res[:, c, :], d["x"][c * P:(c + 1) * P, :]).then_inc(x_in[c], 16)
            sp.wait_ge(late_in, 64)
            sp.dma_start(token_of_slot_d.rearrange("(p j) a -> p (j a)", p=P), spare_i[:, :]).then_inc(slots_cleared, 16)
            sp.dma_start(whole(ctxw), d["ctxw"]).then_inc(ctx_in, 16)

            sp.wait_ge(zeroed, 2)
            for r in range(TOK, TOK + SPARE, P):
                sp.dma_start(x1_d[r:r + P, :], zero[:, :]).then_inc(rows_cleared, 16)
                sp.dma_start(x2_d[r:r + P, 0:D], zero[:, :]).then_inc(rows_cleared, 16)
                sp.dma_start(x2_d[r:r + P, D:ROW], zero[:, 0:E2]).then_inc(rows_cleared, 16)
                sp.dma_start(y_d[r:r + P, :], zero[:, :]).then_inc(rows_cleared, 16)
            for t in range(NT):
                sp.dma_start(y_d[t * P:(t + 1) * P, :], zero[:, :]).then_inc(y_cleared, 16)

            def store_x1(b, c):
                t = 4 * b + c
                sp.wait_ge(x1_made, t + 1)
                sp.dma_start(x1_d[bass.ds(P * t, P), :], x1o[:, c % 2, :]).then_inc(x1_kept[c % 2], 16)

            def a_tile(b, c, first, last):
                t = 4 * b + c
                if not first:
                    if not (isinstance(b, int)):
                        ahead = (c + 1) % CH
                        sp.wait_ge(g1_made, t - 2)
                        sp.dma_start(xT[:, ahead], d["xT"][bass.ds(t + 1, 1)].rearrange("a p k t -> (a p) k t")).then_inc(xT_in[ahead], 16)
                        sp.dma_start(x_res[:, ahead, :], d["x"][bass.ds(P * (t + 1), P), :]).then_inc(x_in[ahead], 16)
                if not (isinstance(t, int) and t < 2):
                    store_x1(*last_of(*last_of(b, c)))

            tiles_of_a(sp, a_tile)
            store_x1(NB - 1, CH - 2)
            store_x1(NB - 1, CH - 1)

            sp.wait_ge(slots_named, 16 * NT)
            sp.dma_start(slot_token[:, :], token_of_slot_d.rearrange("(p j) a -> p (j a)", p=P)).then_inc(slot_token_in, 16)

            def load_up(n, p, k):
                at_least(sp, gu_made[p], k)
                sp.dma_start(wgu[p], d["gu"][bass.ds(n, 1)].rearrange("a p k o -> (a p) k o")).then_inc(gu_in[p], 16)

            def load_down(n, p, k):
                at_least(sp, dn_made[p], k)
                sp.dma_start(wdn[p][:, 0, :], d["dn"][bass.ds(n, 1), 0:P, :].rearrange("a p h -> (a p) h")).then_inc(dn_in[p], 16)
                sp.dma_start(wdn[p][P // 2:P, 1, :], d["dn"][bass.ds(n, 1), P:FI, :].rearrange("a p h -> (a p) h")).then_inc(dn_in[p], 16)

            def load_expert(n, p, k, left):
                if left == 2:
                    load_up(n + 2, p, k + 1)
                if left:
                    load_down(n + 1, *after_it(p, k))

            sp.wait_ge(o_made, NT)
            load_up(0, 0, 0)
            load_down(0, 0, 0)
            load_up(1, 1, 0)

            sp.wait_ge(x2_kept[0], 16 * (SLOT_T - SLOT_T // 2))
            sp.wait_ge(x2_kept[1], 16 * (SLOT_T // 2))
            sp.dma_start(whole(wnat), x2_d[0:TOK, D:ROW].rearrange("(j p) n -> p j n", p=P)).then_inc(wnat_in, 16)
            def keep_places(g):
                rows = token_of_place_d[bass.ds(g * GE * CAP, GE * CAP), :]
                sp.wait_ge(tab_cut, g + 1)
                sp.dma_start(rows.rearrange("(r b) a -> r (b a)", b=NBB), tab_i[:, :]).then_inc(places_kept, 16)
                sp.wait_ge(places_kept, 16 * (g + 1))
                sp.dma_start(place_token[:, bass.ds(g * GE, GE), :], rows.rearrange("(n p h) a -> p n (h a)", n=GE, h=2))\
                  .then_inc(place_token_in, 16)

            def between(g, m):
                if m == 3:
                    keep_places(g + 1)
                if m == 5:
                    js = bass.ds(PART * g, PART)
                    sp.dma_start(x2_all[:, js, :], x2_d[bass.ds(PART * P * g, PART * P), 0:D].rearrange("(j p) n -> p j n", p=P))\
                      .then_inc(x2_in, 16)

            keep_places(0)
            sp.dma_start(x2_all[:, NT - 1, :], x2_d[(NT - 1) * P:TOK, 0:D]).then_inc(x2_in, 16)
            experts(sp, load_expert, between)

            for p in range(2):
                sp.wait_ge(y_added[p], 32 * (E2 // 2))
            for q in range(4):
                at_least(sp, y_in[q % 2], 16 * (q // 2))
                sp.dma_start(y_all[:, 4 * q:4 * q + 4, :], y_d[4 * q * P:4 * (q + 1) * P, :].rearrange("(j p) n -> p j n", p=P))\
                  .then_inc(y_in[q % 2], 16)

        @block.tensor
        def _(pe):
            def project(n, bank, made, done, b, c):
                t = 4 * b + c
                pe.wait_ge(xT_in[c], 16 * (b + 1))
                at_least(pe, done, t)
                for k in range(KC):
                    m = pe.matmul(ps[:, bank, :], xT[:, c, k, :], wqkv[:, k, n, :], start=(k == 0), stop=(k == KC - 1))
                m.then_inc(made, 1)

            def project_q(b, c):
                project(0, PQ, q_made, q_silu, b, c)

            def project_k(b, c):
                project(1, PK, k_made, k_silu, b, c)

            def project_v(b, c):
                project(2, PV, v_made, v_copied, b, c)

            def gate_low(b, c):
                t = 4 * b + c
                at_least(pe, r1_made, t - 1)
                at_least(pe, add_cut, 3 * b + c)
                for k in range(KC):
                    m = pe.matmul(ps[0:RANK, PM, 0:P], wg1[:, k, :], xT[:, c, k, :], start=(k == 0), stop=(k == KC - 1))
                m.then_inc(g1_made, 1)

            def turn_o(b, c):
                t = 4 * b + c
                pe.wait_ge(o_normed, t + 1)
                at_least(pe, kT_copied, t + 2 if not isinstance(t, int) or t < NT - 1 else NT)
                for k in range(KC):
                    m = pe.transpose(ps[:, PT, k * P:(k + 1) * P], normed[:, k * P:(k + 1) * P], eye[:, :])
                m.then_inc(o_turned, 1)

            def project_o(b, c, now, cuts):
                t = 4 * b + c
                pe.wait_ge(oT_copied, t + 1)
                pe.wait_ge(gate_sig, now + 1)
                pe.wait_ge(add_cut, cuts)
                at_least(pe, r1_made, t)
                for k in range(KC):
                    m = pe.matmul(ps[:, PM, :], oT[:, k, :], wo[:, k, :], start=(k == 0), stop=(k == KC - 1))
                m.then_inc(wo_made, 1)

            def a_tile(b, c, first, last):
                t = 4 * b + c
                bn, cn = next_of(b, c)
                pe.wait_ge(q_rotated, t + 1)
                at_least(pe, oT_copied, t - 1)
                at_least(pe, kT_copied, t)
                for g in range(G):
                    m = pe.transpose(ps[:, PT, g * P:(g + 1) * P], q_rot[:, g * P:(g + 1) * P], eye[:, :])
                m.then_inc(q_turned, 1)
                gate_low(b, c)
                if not last:
                    project_v(bn, cn)
                pe.wait_ge(g1_copied, t + 1)
                pe.matmul(ps[:, PM, :], g1T[:, :], wg2[:, :], start=True, stop=True).then_inc(gate_made, 1)
                pe.wait_ge(k_rotated, t + 1)
                pe.wait_ge(qT_copied, t + 1)
                pe.wait_ge(qT_decayed, t + 1)
                for g in range(G):
                    m = pe.transpose(ps[:, PT, g * P:(g + 1) * P], k_rot[:, g * P:(g + 1) * P], eye[:, :])
                m.then_inc(k_turned, 1)
                if not last:
                    project_q(bn, cn)
                pe.wait_ge(kT_copied, t + 1)
                for g in range(G):
                    at_least(pe, masked, 4 * t + max(g - 1, 0))
                    pe.matmul(ps[:, PS0 + g % 2, :], kT[:, g, :], q_blocks[:, g, :, :].rearrange("p a b -> p (a b)"),
                              start=True, stop=True).then_inc(scored, 1)
                if not first:
                    turn_o(*last_of(b, c))
                if c < CH - 1:
                    pe.wait_ge(k_decayed, 3 * b + c + 1)
                    pe.wait_ge(v_copied, t + 1)
                    pe.wait_ge(gate_sig, t + 1)
                    for g in range(G):
                        m = pe.matmul(ps[:, PM, g * P:(g + 1) * P], k_dec[:, c % 2, g * P:(g + 1) * P],
                                      v[:, c % 2, g * P:(g + 1) * P], start=True, stop=True)
                    m.then_inc(add_made, 1)
                if not last:
                    project_k(bn, cn)
                if not first:
                    project_o(*last_of(b, c), t, 3 * b + min(c + 1, 3))
                pe.wait_ge(v_copied, t + 1)
                pe.wait_ge(masked, 4 * t + G)
                at_least(pe, o_gated, t)
                start = True
                if c:
                    pe.wait_ge(st_new, 3 * b + c)
                    for g in range(G):
                        pe.matmul(ps[:, PO, g * P:(g + 1) * P], q_decT[:, g, :], state[:, (c - 1) % 2, g, :],
                                  start=start, stop=False, skip_group_check=True)
                        start = False
                for h in range(H):
                    m = pe.matmul(ps[:, PO, h * HD:(h + 1) * HD], weighted[:, h, :], v[:, c % 2, h * HD:(h + 1) * HD],
                                  start=start, stop=(h == H - 1), skip_group_check=True)
                    start = False
                m.then_inc(o_made, 1)

            pe.wait_ge(sort_v, 3)
            pe.wait_ge(setup, 2)
            flat = onehot[:, :, :].rearrange("p e j -> p (e j)")
            pe.matmul(ps[:, PO, 0:E1 * NT], before, flat, start=True, stop=True)
            pe.matmul(ps[:, PO, 64:64 + E1 * NT], ones[:, :], flat, start=True, stop=True).then_inc(sort_p, 1)

            pe.wait_ge(wv_in, 16)
            project_v(0, 0)
            pe.wait_ge(pick_v, 2)
            for k in range(KC):
                pe.matmul(ps[:, PS0, k * E2:(k + 1) * E2], gatew[:, k * P:(k + 1) * P], pick[:, :], start=True, stop=True)
            pe.matmul(ps[:, PS0, KC * E2:(KC + 1) * E2], ones[:, :], pick[:, :], start=True, stop=True).then_inc(pick_p, 1)
            pe.wait_ge(wqk_in, 32)
            project_q(0, 0)
            project_k(0, 0)
            pe.wait_ge(pick_v, 4)
            pe.wait_ge(sort_v, 5)
            pe.wait_ge(attn_in, 16)
            pe.wait_ge(late_in, 64)
            tiles_of_a(pe, a_tile)
            turn_o(NB - 1, CH - 1)
            project_o(NB - 1, CH - 1, NT - 1, 3 * NB)

            BT, BS, BH, BY, BX, BL = 0, 1, 3, 4, 6, 7

            def expert_of(j):
                return pe.value_load(eid_i[0:1, bass.ds(j, 1)], min_val=0, max_val=E1 - 1)

            def turn_x(p, k):
                pe.wait_ge(x1_got[p], 16 * (k + 1))
                at_least(pe, xg1_copied, 2 * k + p)
                for q in range(KC):
                    m = pe.transpose(ps[:, BT, q * P:(q + 1) * P], x1g[:, p, q * P:(q + 1) * P], eye[:, :])
                m.then_inc(xg1_turned, 1)

            def up(j, p, k):
                e = expert_of(j)
                pe.wait_ge(xg1_copied, 2 * k + p + 1)
                at_least(pe, h1_made[p], k)
                for q in range(KC):
                    m = pe.matmul(ps[:, BS + p, :], x1gT[:, p, q, :], ctxw[:, bass.ds(e, 1), q, :].rearrange("p a n -> p (a n)"),
                                  start=(q == 0), stop=(q == KC - 1))
                m.then_inc(s_made, 1)

            def route(p, k):
                pe.wait_ge(x2_made, 2 * k + p + 1)
                at_least(pe, x2T_copied, 2 * k + p)
                for q in range(KC):
                    m = pe.transpose(ps[:, BX, q * P:(q + 1) * P], x2o[:, p, q * P:(q + 1) * P], eye[:, :])
                m.then_inc(x2_turned, 1)
                pe.wait_ge(x2T_copied, 2 * k + p + 1)
                at_least(pe, routed, 2 * k + p)
                for q in range(KC):
                    m = pe.matmul(ps[:, BL, 0:E2], x2T[:, q, :], router[:, q, :], start=(q == 0), stop=(q == KC - 1))
                m.then_inc(lg_made, 1)

            def b_tile(j, p, k, left):
                if not is_first(j):
                    route(*before_it(p, k))
                e = expert_of(j)
                pe.wait_ge(h1_made[p], k + 1)
                for q in range(KC):
                    m = pe.transpose(ps[:, BH, q * P:(q + 1) * P], h1[:, q * P:(q + 1) * P], eye[:, :])
                m.then_inc(h1_turned, 1)
                if left:
                    turn_x(*after_it(p, k))
                pe.wait_ge(h1_copied, 2 * k + p + 1)
                at_least(pe, r2_made[p], k)
                for q in range(KC):
                    m = pe.matmul(ps[:, BY + p, :], h1T[:, q, :], ctxw[:, bass.ds(e, 1), q, :].rearrange("p a n -> p (a n)"),
                                  start=(q == 0), stop=(q == KC - 1))
                m.then_inc(y1_made, 1)
                if left:
                    up(j + 1, *after_it(p, k))

            pe.wait_ge(r1_made, NT)
            pe.wait_ge(o_gated, NT)
            pe.wait_ge(slot_sorted, 1)
            pe.wait_ge(ctx_in, 16)
            turn_x(0, 0)
            up(0, 0, 0)
            slot_tiles(pe, b_tile)
            route((SLOT_T - 1) % 2, (SLOT_T - 1) // 2)

            pe.wait_ge(tab_v, 17)
            pe.wait_ge(c_half, 2)
            for half in range(2):
                js = slice(half * NT // 2, (half + 1) * NT // 2)
                out = ps[:, half, 0:NT // 2 * E2]
                pe.matmul(out, before_b[:, :], sel[:, js, :].rearrange("p j n -> p (j n)"), start=True, stop=False)
                pe.matmul(out, ones_b[:, :], sel_before[:, js, :].rearrange("p j n -> p (j n)"),
                          start=False, stop=True).then_inc(pos_made, 1)

            def table(g):
                pe.wait_ge(hot_made, g + 1)
                at_least(pe, tab_masked, g)
                for j in range(NT):
                    m = pe.matmul(ps[0:GE * NA, 6, 0:GE * NBB], hot_a[:, j].rearrange("p n a -> p (n a)"),
                                  hot_id[:, j].rearrange("p n b -> p (n b)"), start=(j == 0), stop=(j == NT - 1))
                m.then_inc(tab_made, 1)

            def between(g, m):
                if m == 2:
                    table(g + 1)

            table(0)

            CT, CG, CY = 0, 2, 4

            def c_turn(p, k):
                pe.wait_ge(got[p], 32 * (k + 1))
                at_least(pe, c_copied, 2 * (2 * k + p))
                for q in range(KC):
                    for h in range(2):
                        o = (q % 2) * CAP + h * HALF
                        m = pe.transpose(ps[:, CT + q // 2, o:o + HALF], xg[:, p, h, q * P:(q + 1) * P], eye[0:HALF, 0:HALF])
                m.then_inc(c_turned[p], 1)

            def c_up(p, k):
                pe.wait_ge(gu_in[p], 16 * (k + 1))
                pe.wait_ge(c_copied, 2 * (2 * k + p + 1))
                at_least(pe, h_made, 2 * (2 * k + p))
                for part in range(3):
                    out = ps[:, CG, part * CAP:(part + 1) * CAP] if part < 2 else ps[:, CG + 1, 0:CAP]
                    for q in range(KC):
                        m = pe.matmul(out, wgu[p][:, q, part * P:(part + 1) * P], xgT[:, p, q, :], start=(q == 0), stop=(q == KC - 1))
                m.then_inc(gu_made[p], 1)

            def c_down(p, k):
                pe.wait_ge(dn_in[p], 32 * (k + 1))
                pe.wait_ge(h_made, 2 * (2 * k + p + 1))
                at_least(pe, y_scaled[1 - p], 2 * (k + p))
                for h in range(2):
                    cols = slice(h * HALF, (h + 1) * HALF)
                    pe.matmul(ps[0:HALF, CY + h, :], h_a[:, p, cols], wdn[p][:, 0, :], start=True, stop=False)
                    m = pe.matmul(ps[0:HALF, CY + h, :], h_c[P - FI + P:P, p, cols], wdn[p][P - FI + P:P, 1, :], start=False, stop=True)
                m.then_inc(dn_made[p], 1)

            def c_expert(n, p, k, left):
                first, last = is_first(n), left == 0
                c_up(p, k)
                if not last:
                    c_turn(1 - p, k + p)
                if not first:
                    c_down(1 - p, k - (1 - p))

            c_turn(0, 0)
            experts(pe, c_expert, between)
            c_down(1, E2 // 2 - 1)

        @block.scalar
        def _(act):
            def copy_v(b, c):
                t = 4 * b + c
                act.wait_ge(v_made, t + 1)
                if not (isinstance(t, int) and t < 2):
                    act.wait_ge(o_made, t - 1)
                act.activation(v[:, c % 2, :], ps[:, PV, :], ACT.Copy).then_inc(v_copied, 1)

            def sigmoids(b, c, which):
                t = 4 * b + c
                bank, buf, made, done, free = ((PQ, sig_q, q_made, q_sig, q_silu), (PK, sig_k, k_made, k_sig, k_silu))[which]
                act.wait_ge(made, t + 1)
                at_least(act, free, t)
                act.activation(buf[:, :], ps[:, bank, :], ACT.Sigmoid).then_inc(done, 1)

            def a_tile(b, c, first, last):
                t = 4 * b + c
                bn, cn = next_of(b, c)
                act.wait_ge(q_turned, t + 1)
                for j in range(HG):
                    rows = slice(j * HD, (j + 1) * HD)
                    m = act.activation(q_blocks[rows, :, j, :], ps[rows, PT, :].rearrange("p (g t) -> p g t", g=G), ACT.Copy)
                m.then_inc(qT_copied, 1)
                act.wait_ge(g1_made, t + 1)
                act.activation(g1T[:, :], ps[0:RANK, PM, 0:P], ACT.Copy).then_inc(g1_copied, 1)
                if not last:
                    copy_v(bn, cn)
                act.wait_ge(gate_made, t + 1)
                at_least(act, o_gated, t)
                act.activation(sig_gate[:, :], ps[:, PM, :], ACT.Sigmoid).then_inc(gate_sig, 1)
                act.wait_ge(k_turned, t + 1)
                act.activation(whole(kT), ps[:, PT, :].rearrange("p (g t) -> p g t", g=G), ACT.Copy).then_inc(kT_copied, 1)
                if not last:
                    sigmoids(bn, cn, 0)
                    sigmoids(bn, cn, 1)
                act.wait_ge(o_gated, t + 1)
                act.activation(squares[:, :], gated[:, :], ACT.Square).then_inc(squared, 1)

            copy_v(0, 0)
            sigmoids(0, 0, 0)
            sigmoids(0, 0, 1)
            act.wait_ge(zeroed, 2)
            tiles_of_a(act, a_tile)

            BT, BS, BH, BX = 0, 1, 3, 6

            def front(p, k):
                act.wait_ge(xg1_turned, 2 * k + p + 1)
                act.activation(x1gT[:, p].rearrange("p k t -> p (k t)"), ps[:, BT, :], ACT.Copy).then_inc(xg1_copied, 1)
                act.wait_ge(s_made, 2 * k + p + 1)
                at_least(act, s_silu, 2 * k + p)
                act.activation(sig_s[:, :], ps[:, BS + p, :], ACT.Sigmoid).then_inc(s_sig, 1)

            def copy_x2(p, k):
                act.wait_ge(x2_turned, 2 * k + p + 1)
                act.activation(whole(x2T).rearrange("p k t -> p (k t)"), ps[:, BX, :], ACT.Copy).then_inc(x2T_copied, 1)

            def exps(p, k):
                act.wait_ge(router_v, 4 * (2 * k + p) + 4)
                act.activation(es[:, :], logits[:, :], ACT.Sigmoid, bias=neg_max[:, 0:1]).then_inc(es_made, 1)

            def b_tile(j, p, k, left):
                if not is_first(j):
                    copy_x2(*before_it(p, k))
                act.wait_ge(h1_turned, 2 * k + p + 1)
                act.activation(whole(h1T).rearrange("p k t -> p (k t)"), ps[:, BH, :], ACT.Copy).then_inc(h1_copied, 1)
                if not is_first(j):
                    exps(*before_it(p, k))
                if left:
                    front(*after_it(p, k))

            front(0, 0)
            slot_tiles(act, b_tile)
            copy_x2((SLOT_T - 1) % 2, (SLOT_T - 1) // 2)
            exps((SLOT_T - 1) % 2, (SLOT_T - 1) // 2)

            CT, CG, CY = 0, 2, 4

            def copy_x(p, k):
                act.wait_ge(c_turned[p], k + 1)
                act.activation(xgT[:, p, 0:2, :], ps[:, CT, 0:2 * CAP].rearrange("p (q s) -> p q s", q=2), ACT.Copy)\
                   .then_inc(c_copied, 1)

            def scale_y(p, k):
                act.wait_ge(dn_made[p], k + 1)
                act.wait_ge(w_copied[p], k + 1)
                at_least(act, y_added[p], 32 * k)
                act.activation(ye[:, p, 0, :], ps[0:HALF, CY, :], ACT.Copy, scale=w_col[:, p, 0:1]).then_inc(y_scaled[p], 1)

            def c_expert(n, p, k, left):
                first, last = is_first(n), left == 0
                act.wait_ge(gu_made[p], k + 1)
                at_least(act, h_made, 2 * (2 * k + p))
                act.activation(sig_a[:, :], ps[:, CG, 0:CAP], ACT.Sigmoid)
                act.activation(sig_c[0:P // 2, :], ps[0:P // 2, CG + 1, 0:CAP], ACT.Sigmoid).then_inc(c_sig, 1)
                if not last:
                    copy_x(1 - p, k + p)
                if not first:
                    scale_y(1 - p, k - (1 - p))

            copy_x(0, 0)
            experts(act, c_expert)
            scale_y(1, E2 // 2 - 1)

            for q in range(4):
                act.wait_ge(shift_made, 2 * q + 2)
                for j in range(4 * q, 4 * q + 4):
                    m = act.activation(x2_all[:, j, :], y_all[:, j, :], ACT.Identity, bias=shift3[:, j:j + 1], scale=rstd3[:, j:j + 1])
                m.then_inc(out_made, 1)
                act.wait_ge(out_made, q + 1)
                act.dma_start(d["out"][4 * q * P:4 * (q + 1) * P, :].rearrange("(j p) n -> p j n", p=P), x2_all[:, 4 * q:4 * q + 4, :])\
                   .then_inc(out_kept, 16)
            act.wait_ge(out_kept, 64)

        @block.vector
        def _(dve):
            dve.memset(ones[:, :], 1.0).then_inc(setup, 1)
            dve.memset(zero[:, :], 0.0).then_inc(zeroed, 1)
            dve.wait_ge(sort_in, 32)
            dve.tensor_copy(tok_f[:, :], tok_i[:, :]).then_inc(sort_v, 1)
            dve.wait_ge(sort_v, 1)
            for e in range(E1 - 1):
                m = dve.tensor_scalar(ge[:, e, :], tok_f[:, :], float(PER * (e + 1)), None, ALU.is_ge)
            m.then_inc(sort_v, 1)
            dve.wait_ge(sort_v, 2)
            dve.tensor_scalar(onehot[:, 0, :], ge[:, 0, :], -1.0, 1.0, ALU.mult, ALU.add)
            dve.tensor_tensor(onehot[:, 1:E1 - 1, :], ge[:, 0:E1 - 2, :], ge[:, 1:E1 - 1, :], ALU.subtract)
            dve.tensor_copy(onehot[:, E1 - 1, :], ge[:, E1 - 2, :]).then_inc(sort_v, 1)
            dve.wait_ge(gate_in, 32)
            dve.tensor_copy(o2n_f[:, :], o2n_i[:, :]).then_inc(pick_v, 1)
            dve.wait_ge(pick_v, 1)
            dve.tensor_scalar(pick[:, :], n_iota[:, :], o2n_f[:, 0:1], None, ALU.is_equal).then_inc(pick_v, 1)
            dve.wait_ge(sort_p, 1)
            dve.tensor_copy(whole(total).rearrange("p e j -> p (e j)"), ps[:, PO, 64:64 + E1 * NT]).then_inc(sort_v, 1)
            dve.tensor_copy(whole(rank).rearrange("p e j -> p (e j)"), ps[:, PO, 0:E1 * NT]).then_inc(sort_v, 1)
            dve.wait_ge(sort_v, 5)
            for e in range(E1):
                m = dve.tensor_tensor_scan(cum[:, e, :], ones[:, 0:NT], total[:, e, :], 0.0, ALU.mult, ALU.add)
            m.then_inc(sort_v, 1)
            dve.wait_ge(sort_v, 6)
            for e in range(E1):
                m = dve.tensor_scalar(lot[:, e, :], tile_no[:, 0:NT], float(P), cum[:, e, NT - 1:NT], ALU.mult, ALU.is_lt)
            m.then_inc(sort_v, 1)
            dve.tensor_tensor(whole(rank), whole(rank), whole(cum), ALU.add).then_inc(sort_v, 1)
            dve.wait_ge(sort_v, 8)
            dve.tensor_reduce(tiles[:, :], whole(lot), AX.X, ALU.add).then_inc(sort_v, 1)
            dve.tensor_tensor(whole(rank), whole(rank), whole(total), ALU.subtract).then_inc(sort_v, 1)
            dve.wait_ge(sort_v, 10)
            dve.tensor_tensor_scan(tiles_cum[:, :], ones[:, 0:E1], tiles[:, :], 0.0, ALU.mult, ALU.add).then_inc(sort_v, 1)
            dve.wait_ge(sort_v, 11)
            dve.tensor_tensor(start[:, :], tiles_cum[:, :], tiles[:, :], ALU.subtract).then_inc(sort_v, 1)
            dve.tensor_scalar(eid_f[:, :], tile_no[:, :], tiles_cum[:, 0:1], None, ALU.is_ge).then_inc(sort_v, 1)
            dve.wait_ge(sort_v, 13)
            dve.tensor_scalar(start[:, :], start[:, :], float(P), None, ALU.mult).then_inc(sort_v, 1)
            for e in range(1, E1 - 1):
                dve.wait_ge(sort_v, 13 + (e > 1))
                dve.scalar_tensor_tensor(eid_f[:, :], tile_no[:, :], tiles_cum[:, e:e + 1], eid_f[:, :], ALU.is_ge, ALU.add)\
                   .then_inc(sort_v, 1)
                dve.wait_ge(sort_v, 14 + e)
            dve.tensor_copy(eid_i[:, :], eid_f[:, :]).then_inc(slot_sorted, 1)
            for e in range(E1):
                m = dve.scalar_tensor_tensor(rank[:, e, :], rank[:, e, :], start[:, e:e + 1], onehot[:, e, :], ALU.add, ALU.mult)
            m.then_inc(sort_v, 1)
            dve.wait_ge(sort_v, 17)
            dve.tensor_reduce(dest[:, :], whole(rank).rearrange("p e j -> p j e"), AX.X, ALU.add).then_inc(sort_v, 1)
            dve.wait_ge(sort_v, 18)
            dve.tensor_copy(slot_i[:, :], dest[:, :]).then_inc(sort_v, 1)
            dve.wait_ge(sort_v, 19)
            dve.tensor_single_scalar(row_i[:, :], slot_i[:, :], P - 1, ALU.bitwise_and)
            dve.tensor_single_scalar(slot_i[:, :], slot_i[:, :], 7, ALU.arith_shift_right).then_inc(sort_v, 1)
            dve.wait_ge(sort_v, 20)
            dve.scalar_tensor_tensor(dest_i[:, :], row_i[:, :], float(SLOT_T), slot_i[:, :], ALU.mult, ALU.add).then_inc(sort_v, 1)
            dve.tensor_copy(ids_i[:, :], ids[:, :]).then_inc(sort_v, 1)

            def keep_router():
                dve.wait_ge(pick_p, 1)
                dve.tensor_copy(whole(router).rearrange("p k n -> p (k n)"), ps[:, PS0, 0:KC * E2]).then_inc(pick_v, 1)
                dve.tensor_scalar(kept_bias[:, :], ps[:, PS0, KC * E2:(KC + 1) * E2], -1.0, -NEG, ALU.add, ALU.mult).then_inc(pick_v, 1)

            def silu(b, c, which):
                t = 4 * b + c
                bank, sg, x, r2_, sig, done, second, rotated = (
                    (PQ, sig_q, q_act, rot2_q, q_sig, q_silu, q_r2, q_rotated),
                    (PK, sig_k, k_act, rot2_k, k_sig, k_silu, k_r2, k_rotated))[which]
                dve.wait_ge(sig, t + 1)
                at_least(dve, rotated, t)
                dve.tensor_tensor(x[:, :], ps[:, bank, :], sg[:, :], ALU.mult).then_inc(done, 1)
                dve.wait_ge(done, t + 1)
                xv = x[:, :].rearrange("p (h a i) -> p h a i", a=2, i=HD // 2)
                rv = r2_[:, :].rearrange("p (h a i) -> p h a i", a=2, i=HD // 2)
                for a in range(2):
                    s = sin[:, c, a * HD // 2:(a + 1) * HD // 2].unsqueeze(1).to_broadcast([P, H, HD // 2])
                    m = dve.tensor_tensor(rv[:, :, a, :], xv[:, :, 1 - a, :], s, ALU.mult)
                m.then_inc(second, 1)

            def rotated_sum(b, c, which):
                t = 4 * b + c
                r1_, r2_, out, one, two, done, turned = (
                    (rot1_q, rot2_q, q_rot, q_r1, q_r2, q_rotated, q_turned),
                    (rot1_k, rot2_k, k_rot, k_r1, k_r2, k_rotated, k_turned))[which]
                dve.wait_ge(one, t + 1)
                dve.wait_ge(two, t + 1)
                at_least(dve, turned, t)
                if which:
                    at_least(dve, k_decayed, 3 * b + c)
                dve.tensor_tensor(out[:, :], r1_[:, :], r2_[:, :], ALU.add).then_inc(done, 1)

            def norm_o(b, c):
                t = 4 * b + c
                dve.wait_ge(rms_made, t + 1)
                at_least(dve, o_turned, t)
                dve.tensor_tensor(normed[:, :].rearrange("p (h i) -> p h i", h=H), gated[:, :].rearrange("p (h i) -> p h i", h=H),
                                  rms_inv[:, :].unsqueeze(2).to_broadcast([P, H, HD]), ALU.mult).then_inc(o_normed, 1)

            def copy_o(b, c):
                t = 4 * b + c
                dve.wait_ge(o_turned, t + 1)
                at_least(dve, wo_made, t)
                dve.tensor_tensor(whole(oT), ps[:, PT, :].rearrange("p (k t) -> p k t", k=KC),
                                  nw[:, :].unsqueeze(2).to_broadcast([P, KC, P]), ALU.mult).then_inc(oT_copied, 1)

            def layer_norm1(b, c):
                t = 4 * b + c
                dve.wait_ge(wo_made, t + 1)
                dve.wait_ge(x_in[c], 16 * (b + 1))
                at_least(dve, x1_made, t)
                dve.tensor_tensor(r1[:, :], ps[:, PM, :], x_res[:, c, :], ALU.add).then_inc(r1_made, 1)
                dve.wait_ge(r1_made, t + 1)
                dve.bn_stats(stat1[:, :], r1[:, :]).then_inc(stat1_made, 1)
                dve.wait_ge(stat1_made, t + 1)
                at_least(dve, rstd1_made, t)
                settle(dve)
                dve.bn_aggr(mv1[:, :], stat1[:, :]).then_inc(mv1_made, 1)
                dve.wait_ge(rstd1_made, t + 1)
                at_least(dve, x1_kept[c % 2], 16 * (2 * b + c // 2))
                dve.tensor_scalar(x1o[:, c % 2, :], r1[:, :], mv1[:, 0:1], rstd1[:, 0:1], ALU.subtract, ALU.mult).then_inc(x1_made, 1)

            def a_tile(b, c, first, last):
                t = 4 * b + c
                bn, cn = next_of(b, c)
                dve.wait_ge(qT_copied, t + 1)
                dve.tensor_tensor(whole(q_decT), ps[:, PT, :].rearrange("p (g t) -> p g t", g=G), dq, ALU.mult)\
                   .then_inc(qT_decayed, 1)
                if not first:
                    norm_o(*last_of(b, c))
                if not last:
                    silu(bn, cn, 0)
                for g in range(G):
                    dve.wait_ge(scored, 4 * t + g + 1)
                    dve.tensor_tensor(weighted[:, g * HG:(g + 1) * HG, :], ps[:, PS0 + g % 2, :].rearrange("p (h t) -> p h t", h=HG),
                                      decay[:, g * HG:(g + 1) * HG, :], ALU.mult).then_inc(masked, 1)
                if not first:
                    copy_o(*last_of(b, c))
                if not last:
                    rotated_sum(bn, cn, 0)
                if c < CH - 1:
                    n = 3 * b + c
                    dve.wait_ge(add_made, n + 1)
                    at_least(dve, st_new, n)
                    dve.tensor_tensor(whole(state_add), ps[:, PM, :].rearrange("p (g t) -> p g t", g=G),
                                      block_diag[:, :].unsqueeze(1).to_broadcast([P, G, P]), ALU.mult).then_inc(add_cut, 1)
                    dve.wait_ge(add_cut, n + 1)
                    at_least(dve, o_made, t)
                    if c:
                        dve.wait_ge(st_decayed, 2 * b + c)
                        dve.tensor_tensor(state[:, c % 2], whole(state_add), whole(state_dec), ALU.add).then_inc(st_new, 1)
                    else:
                        dve.tensor_copy(state[:, c % 2], whole(state_add)).then_inc(st_new, 1)
                if not last:
                    silu(bn, cn, 1)
                    rotated_sum(bn, cn, 1)
                if not first:
                    layer_norm1(*last_of(b, c))
                dve.wait_ge(o_made, t + 1)
                dve.wait_ge(gate_sig, t + 1)
                at_least(dve, o_normed, t)
                dve.tensor_tensor(gated[:, :], ps[:, PO, :], sig_gate[:, :], ALU.mult).then_inc(o_gated, 1)
                dve.wait_ge(squared, t + 1)
                at_least(dve, rms_made, t)
                dve.tensor_reduce(ms[:, :], squares[:, :].rearrange("p (h i) -> p h i", h=H), AX.X, ALU.add).then_inc(ms_made, 1)

            dve.wait_ge(attn_in, 16)
            silu(0, 0, 0)
            rotated_sum(0, 0, 0)
            silu(0, 0, 1)
            rotated_sum(0, 0, 1)
            keep_router()
            dve.wait_ge(late_in, 64)
            tiles_of_a(dve, a_tile)
            norm_o(NB - 1, CH - 1)
            copy_o(NB - 1, CH - 1)
            layer_norm1(NB - 1, CH - 1)

            BS, BY, BL = 1, 4, 7

            def hidden(p, k):
                dve.wait_ge(s_sig, 2 * k + p + 1)
                at_least(dve, h1_made[1 - p], k + p)
                dve.tensor_tensor(s_act[:, :], ps[:, BS + p, :], sig_s[:, :], ALU.mult).then_inc(s_silu, 1)
                dve.wait_ge(s_silu, 2 * k + p + 1)
                at_least(dve, h1_turned, 2 * k + p)
                dve.tensor_tensor(h1[:, :], ps[:, BS + p, :], s_act[:, :], ALU.mult).then_inc(h1_made[p], 1)

            def route(p, k):
                j = 2 * k + p
                v0 = 4 * j
                dve.wait_ge(lg_made, 2 * k + p + 1)
                dve.tensor_tensor(logits[:, :], ps[:, BL, 0:E2], kept_bias[:, :], ALU.add).then_inc(router_v, 1)
                dve.wait_ge(router_v, v0 + 1)
                settle(dve)
                dve.max(top8[:, :], logits[:, :]).then_inc(router_v, 1)
                dve.wait_ge(router_v, v0 + 2)
                settle(dve)
                dve.match_replace(marked[:, :], top8[:, :], logits[:, :], TAKEN).then_inc(router_v, 1)
                dve.tensor_scalar(neg_max[:, :], top8[:, 0:1], -1.0, None, ALU.mult).then_inc(router_v, 1)
                dve.wait_ge(router_v, v0 + 4)
                dve.tensor_scalar(not_chosen[:, :], marked[:, :], TAKEN / 2, -1.0, ALU.is_le, ALU.add).then_inc(rstep, 1)
                dve.wait_ge(es_made, 2 * k + p + 1)
                r0 = 5 * j
                dve.tensor_scalar(es1[:, :], es[:, :], -1.0, 1.0, ALU.mult, ALU.add).then_inc(rstep, 1)
                dve.wait_ge(rstep, r0 + 2)
                dve.reciprocal(es_inv[:, :], es1[:, :]).then_inc(rstep, 1)
                dve.wait_ge(rstep, r0 + 3)
                dve.tensor_tensor(expo[:, :], es[:, :], es_inv[:, :], ALU.mult).then_inc(rstep, 1)
                dve.wait_ge(rstep, r0 + 4)
                dve.scalar_tensor_tensor(chosen[:, :], marked[:, :], TAKEN / 2, expo[:, :], ALU.is_le, ALU.mult,
                                         accum_out=w_sum[:, :]).then_inc(rstep, 1)
                dve.wait_ge(rstep, r0 + 5)
                dve.reciprocal(w_inv[:, :], w_sum[:, :]).then_inc(w_inverted, 1)
                dve.wait_ge(w_inverted, j + 1)
                dve.scalar_tensor_tensor(x2o[:, p, D:ROW], chosen[:, :], w_inv[:, 0:1], not_chosen[:, :], ALU.mult, ALU.add)\
                   .then_inc(routed, 1)

            def b_tile(j, p, k, left):
                if not is_first(j):
                    route(*before_it(p, k))
                dve.wait_ge(y1_made, 2 * k + p + 1)
                at_least(dve, x2_made, 2 * k + p)
                dve.tensor_tensor(r2[:, :], ps[:, BY + p, :], x1g[:, p, :], ALU.add).then_inc(r2_made[p], 1)
                dve.wait_ge(r2_made[p], k + 1)
                dve.bn_stats(stat2[:, :], r2[:, :]).then_inc(stat2_made, 1)
                dve.wait_ge(stat2_made, 2 * k + p + 1)
                settle(dve)
                dve.bn_aggr(mv2[:, :], stat2[:, :]).then_inc(mv2_made, 1)
                dve.wait_ge(rstd2_made, 2 * k + p + 1)
                at_least(dve, x2_kept[p], 16 * k)
                dve.tensor_scalar(x2o[:, p, 0:D], r2[:, :], mv2[:, 0:1], rstd2[:, 0:1], ALU.subtract, ALU.mult).then_inc(x2_made, 1)
                if left:
                    hidden(*after_it(p, k))

            hidden(0, 0)
            slot_tiles(dve, b_tile)
            route((SLOT_T - 1) % 2, (SLOT_T - 1) // 2)

            def cut_table(g):
                dve.wait_ge(tab_made, g + 1)
                at_least(dve, tab_summed, g)
                dve.tensor_tensor(whole(tab), ps[0:GE * NA, 6, 0:GE * NBB].rearrange("r (n b) -> r n b", n=GE),
                                  diag8[:, :].unsqueeze(2).to_broadcast([GE * NA, GE, NBB]), ALU.mult).then_inc(tab_masked, 1)
                dve.wait_ge(tab_masked, g + 1)
                at_least(dve, tab_cut, g)
                dve.tensor_reduce(tab_r[:, :], whole(tab).rearrange("r n b -> r b n"), AX.X, ALU.add).then_inc(tab_summed, 1)
                dve.wait_ge(tab_summed, g + 1)
                dve.scalar_tensor_tensor(tab_spare[:, :], tab_r[:, :], 0.0, place_no[:, :], ALU.is_equal, ALU.mult).then_inc(tab_spared, 1)
                dve.wait_ge(tab_spared, g + 1)
                at_least(dve, places_kept, 16 * g)
                dve.scalar_tensor_tensor(tab_i[:, :], tab_r[:, :], float(TOK), tab_spare[:, :], ALU.add, ALU.add).then_inc(tab_cut, 1)

            dve.memset(before_b[:, :], 0.0).then_inc(c_half, 1)
            dve.wait_ge(c_half, 1)
            dve.tensor_copy(before_b[:, :], before[:, :])
            dve.tensor_copy(ab_h[:, :], ab_iota[:, :])
            dve.tensor_scalar(ids_h[:, :], ids[:, :], -float(TOK), None, ALU.add)
            dve.tensor_copy(ones_b[:, :], ones[:, :]).then_inc(c_half, 1)
            dve.wait_ge(wnat_in, 16)
            dve.tensor_scalar(whole(sel), whole(wnat), 0.0, None, ALU.is_ge).then_inc(tab_v, 1)
            dve.memset(sel_before[:, 0, :], 0.0).then_inc(tab_v, 1)
            for j in range(1, NT):
                dve.wait_ge(tab_v, j + 1)
                dve.tensor_tensor(sel_before[:, j, :], sel_before[:, j - 1, :], sel[:, j - 1, :], ALU.add).then_inc(tab_v, 1)
            for half in range(2):
                js = slice(half * NT // 2, (half + 1) * NT // 2)
                out = ps[:, half, 0:NT // 2 * E2].rearrange("p (j n) -> p j n", n=E2)
                dve.wait_ge(pos_made, half + 1)
                dve.scalar_tensor_tensor(ok[:, js, :], out, float(CAP), sel[:, js, :], ALU.is_lt, ALU.mult).then_inc(tstep, 1)
                dve.wait_ge(tstep, 2 * half + 1)
                dve.scalar_tensor_tensor(place[:, js, :], out, 1.0, ok[:, js, :], ALU.add, ALU.mult).then_inc(tstep, 1)
            dve.wait_ge(tstep, 4)
            dve.tensor_scalar(whole(place_i), whole(place), -1.0, None, ALU.add).then_inc(tstep, 1)
            dve.wait_ge(tstep, 5)
            dve.tensor_single_scalar(whole(a_i), whole(place_i), 4, ALU.arith_shift_right)
            dve.tensor_single_scalar(whole(b_i), whole(place_i), NBB - 1, ALU.bitwise_and).then_inc(tstep, 1)
            dve.wait_ge(tstep, 6)
            dve.tensor_copy(whole(a_h), whole(a_i))
            dve.tensor_copy(whole(b_h), whole(b_i)).then_inc(tstep, 1)
            dve.wait_ge(tstep, 7)
            dve.wait_ge(c_half, 2)

            def one_hots(g):
                ns = bass.ds(g * GE, GE)
                at_least(dve, tab_made, g)
                dve.tensor_tensor(whole(hot_a), a_h[:, :, ns].unsqueeze(3).to_broadcast([P, NT, GE, NA]),
                                  ab_h[:, 0:NA].unsqueeze(1).unsqueeze(1).to_broadcast([P, NT, GE, NA]), ALU.is_equal)
                dve.tensor_tensor(whole(hot_b), b_h[:, :, ns].unsqueeze(3).to_broadcast([P, NT, GE, NBB]),
                                  ab_h[:, NA:NA + NBB].unsqueeze(1).unsqueeze(1).to_broadcast([P, NT, GE, NBB]), ALU.is_equal)\
                    .then_inc(hot_b_made, 1)

            def hot_ids(g):
                dve.wait_ge(hot_b_made, g + 1)
                dve.tensor_tensor(whole(hot_id).rearrange("p j n b -> p j (n b)"), whole(hot_b).rearrange("p j n b -> p j (n b)"),
                                  ids_h[:, :].unsqueeze(2).to_broadcast([P, NT, GE * NBB]), ALU.mult).then_inc(hot_made, 1)

            def between(g, m):
                if m == 0:
                    one_hots(g + 1)
                if m == 1:
                    hot_ids(g + 1)
                if m == 2:
                    cut_table(g + 1)

            one_hots(0)
            hot_ids(0)
            cut_table(0)

            CT, CG, CY = 0, 2, 4
            LO, HI = slice(0, P // 2), slice(P // 2, P)

            def copy_x(p, k):
                dve.wait_ge(c_turned[p], k + 1)
                dve.tensor_copy(xgT[:, p, 2:4, :], ps[:, CT + 1, 0:2 * CAP].rearrange("p (q s) -> p q s", q=2))\
                   .then_inc(c_copied, 1)

            def keep_w(n, p, k):
                dve.wait_ge(c_turned[p], k + 1)
                at_least(dve, y_scaled[p], 2 * k)
                dve.tensor_copy(w_col[:, p, :], xg[:, p, :, bass.ds(n + D, 1)].rearrange("p h a -> p (h a)")).then_inc(w_copied[p], 1)

            def scale_y(p, k):
                dve.wait_ge(dn_made[p], k + 1)
                dve.wait_ge(w_copied[p], k + 1)
                at_least(dve, y_added[p], 32 * k)
                dve.tensor_scalar(ye[:, p, 1, :], ps[0:HALF, CY + 1, :], w_col[:, p, 1:2], None, ALU.mult).then_inc(y_scaled[p], 1)

            def c_expert(n, p, k, left):
                first, last = is_first(n), left == 0
                dve.wait_ge(c_sig, 2 * k + p + 1)
                at_least(dve, h_made, 2 * (2 * k + p))
                dve.tensor_tensor(g_a[:, :], ps[:, CG, 0:CAP], sig_a[:, :], ALU.mult).then_inc(g_made, 1)
                dve.tensor_tensor(g_c[HI, :], ps[LO, CG + 1, 0:CAP], sig_c[LO, :], ALU.mult).then_inc(g_made, 1)
                dve.wait_ge(g_made, 2 * (2 * k + p) + 1)
                at_least(dve, dn_made[p], k)
                dve.tensor_tensor(h_a[:, p, :], ps[:, CG, CAP:2 * CAP], g_a[:, :], ALU.mult).then_inc(h_made, 1)
                dve.wait_ge(g_made, 2 * (2 * k + p) + 2)
                dve.tensor_tensor(h_c[HI, p, :], ps[HI, CG + 1, 0:CAP], g_c[HI, :], ALU.mult).then_inc(h_made, 1)
                if not last:
                    copy_x(1 - p, k + p)
                if not first:
                    scale_y(1 - p, k - (1 - p))
                if not last:
                    keep_w(n + 1, 1 - p, k + p)

            copy_x(0, 0)
            keep_w(0, 0, 0)
            experts(dve, c_expert, between)
            scale_y(1, E2 // 2 - 1)

            dve.wait_ge(x2_in, 16 * NG)
            for q in range(4):
                js = slice(4 * q, 4 * q + 4)
                dve.wait_ge(y_in[q % 2], 16 * (q // 2 + 1))
                dve.tensor_tensor(y_all[:, js, :], y_all[:, js, :], x2_all[:, js, :], ALU.add).then_inc(r3_made, 1)
                dve.wait_ge(r3_made, q + 1)
                for j in range(4 * q, 4 * q + 4):
                    m = dve.bn_stats(stat3[:, j, :], y_all[:, j, :])
                m.then_inc(stat3_made, 1)
                dve.wait_ge(stat3_made, q + 1)
                for j in range(4 * q, 4 * q + 4):
                    m = dve.bn_aggr(mv3[:, j, :], stat3[:, j, :])
                m.then_inc(mv3_made, 1)

        @block.gpsimd
        def _(pool):
            pool.memset(minus_half[:, :], -0.5).then_inc(setup, 1)
            pool.memset(whole(q_blocks), 0.0).then_inc(zeroed, 1)

            def cosines(b, c, which):
                t = 4 * b + c
                x, r1_, silu_, one = ((q_act, rot1_q, q_silu, q_r1), (k_act, rot1_k, k_silu, k_r1))[which]
                pool.wait_ge(silu_, t + 1)
                pool.tensor_tensor(r1_[:, :].rearrange("p (h i) -> p h i", h=H), x[:, :].rearrange("p (h i) -> p h i", h=H),
                                   cos[:, c, :].unsqueeze(1).to_broadcast([P, H, HD]), ALU.mult).then_inc(one, 1)

            def decay_k(b, c):
                pool.wait_ge(k_rotated, 4 * b + c + 1)
                at_least(pool, add_made, 3 * b + max(c - 1, 0))
                pool.tensor_tensor(k_dec[:, c % 2, :].rearrange("p (h i) -> p h i", h=H), k_rot[:, :].rearrange("p (h i) -> p h i", h=H),
                                   dk[:, :].unsqueeze(2).to_broadcast([P, H, HD]), ALU.mult).then_inc(k_decayed, 1)

            def rstd1_of(b, c):
                t = 4 * b + c
                pool.wait_ge(mv1_made, t + 1)
                settle(pool)
                pool.tensor_scalar(ve1[:, :], mv1[:, 1:2], 1.0, LN_EPS, ALU.mult, ALU.add).then_inc(ve1_made, 1)
                pool.wait_ge(ve1_made, t + 1)
                at_least(pool, x1_made, t)
                pool.tensor_tensor(rstd1[:, :], ve1[:, :], minus_half[:, 0:1], ALU.pow).then_inc(rstd1_made, 1)

            def name_slots(t):
                at_least(pool, slots_named, 16 * t)
                settle(pool)
                pool.tensor_copy(name_to[:, :], dest_i[:, bass.ds(t, 1)])
                pool.tensor_copy(name_of[:, :], ids_i[:, bass.ds(t, 1)]).then_inc(name_set, 1)
                pool.wait_ge(name_set, t + 1)
                settle(pool)
                pool.indirect_dma_start(out=token_of_slot_d, out_offset=bass.IndirectOffsetOnAxis(ap=name_to[:, :], axis=0),
                                        in_=name_of[:, :], in_offset=None).then_inc(slots_named, 16)

            def a_tile(b, c, first, last):
                t = 4 * b + c
                bn, cn = next_of(b, c)
                if 0 < c < CH - 1:
                    pool.wait_ge(st_new, 3 * b + c)
                    pool.tensor_tensor(whole(state_dec), state[:, (c - 1) % 2], lam[:, :].unsqueeze(2).to_broadcast([P, G, P]),
                                       ALU.mult).then_inc(st_decayed, 1)
                if not last:
                    cosines(bn, cn, 0)
                name_slots(t)
                if not last:
                    cosines(bn, cn, 1)
                    if cn < CH - 1:
                        decay_k(bn, cn)
                if not first:
                    rstd1_of(*last_of(b, c))
                pool.wait_ge(ms_made, t + 1)
                settle(pool)
                pool.tensor_scalar(ms_eps[:, :], ms[:, :], 1.0 / HD, RMS_EPS, ALU.mult, ALU.add).then_inc(ms_plus, 1)
                pool.wait_ge(ms_plus, t + 1)
                at_least(pool, o_normed, t)
                pool.tensor_tensor(rms_inv[:, :], ms_eps[:, :], minus_half[:, :], ALU.pow).then_inc(rms_made, 1)

            pool.wait_ge(setup, 2)
            pool.wait_ge(attn_in, 16)
            cosines(0, 0, 0)
            cosines(0, 0, 1)
            decay_k(0, 0)
            pool.wait_ge(sort_v, 22)
            pool.wait_ge(slots_cleared, 16)
            tiles_of_a(pool, a_tile)
            rstd1_of(NB - 1, CH - 1)

            def gather(j, p, k):
                at_least(pool, r2_made[p], k)
                at_least(pool, x1_got[p], 16 * k)
                settle(pool)
                pool.tensor_copy(idx_g[:, p:p + 1], slot_token[:, bass.ds(j, 1)]).then_inc(idx_g_set, 1)
                pool.wait_ge(idx_g_set, 2 * k + p + 1)
                settle(pool)
                pool.indirect_dma_start(out=x1g[:, p, :], out_offset=None, in_=x1_d,
                                        in_offset=bass.IndirectOffsetOnAxis(ap=idx_g[:, p:p + 1].bitcast(U32), axis=0)).then_inc(x1_got[p], 16)

            def scatter(j, p, k):
                at_least(pool, x2_kept[p], 16 * k)
                settle(pool)
                pool.tensor_copy(idx_s[:, p:p + 1], slot_token[:, bass.ds(j, 1)]).then_inc(idx_s_set, 1)
                pool.wait_ge(idx_s_set, 2 * k + p + 1)
                pool.wait_ge(routed, 2 * k + p + 1)
                settle(pool)
                pool.indirect_dma_start(out=x2_d, out_offset=bass.IndirectOffsetOnAxis(ap=idx_s[:, p:p + 1].bitcast(U32), axis=0),
                                        in_=x2o[:, p, :], in_offset=None).then_inc(x2_kept[p], 16)

            def b_tile(j, p, k, left):
                if not is_first(j):
                    scatter(j - 1, *before_it(p, k))
                pool.wait_ge(mv2_made, 2 * k + p + 1)
                settle(pool)
                pool.tensor_scalar(ve2[:, :], mv2[:, 1:2], 1.0, LN_EPS, ALU.mult, ALU.add).then_inc(ve2_made, 1)
                pool.wait_ge(ve2_made, 2 * k + p + 1)
                pool.tensor_tensor(rstd2[:, :], ve2[:, :], minus_half[:, 0:1], ALU.pow).then_inc(rstd2_made, 1)
                if left == 2:
                    gather(j + 2, p, k + 1)

            pool.wait_ge(slot_token_in, 16)
            pool.wait_ge(rows_cleared, 4 * 16 * SPARE // P)
            pool.wait_ge(x1_kept[0], 16 * NT // 2)
            pool.wait_ge(x1_kept[1], 16 * NT // 2)
            gather(0, 0, 0)
            gather(1, 1, 0)
            slot_tiles(pool, b_tile)
            scatter(SLOT_T - 1, (SLOT_T - 1) % 2, (SLOT_T - 1) // 2)

            def c_gather(n, p, k):
                at_least(pool, w_copied[p], k)
                at_least(pool, c_turned[p], k)
                at_least(pool, got[p], 32 * k)
                settle(pool)
                pool.tensor_copy(cidx_g[:, p, :], place_token[:, bass.ds(n, 1), :].rearrange("p a h -> p (a h)")).then_inc(cg_set, 1)
                pool.wait_ge(cg_set, 2 * k + p + 1)
                settle(pool)
                for h in range(2):
                    pool.indirect_dma_start(out=xg[:, p, h, :], out_offset=None, in_=x2_d,
                                            in_offset=bass.IndirectOffsetOnAxis(ap=cidx_g[:, p, h:h + 1].bitcast(U32), axis=0))\
                        .then_inc(got[p], 16)

            def c_scatter(n, p, k):
                at_least(pool, y_added[p], 32 * k)
                settle(pool)
                pool.tensor_copy(cidx_s[:, p, :], place_token[:, bass.ds(n, 1), :].rearrange("p a h -> p (a h)")).then_inc(cs_set, 1)
                pool.wait_ge(cs_set, 2 * k + p + 1)
                pool.wait_ge(y_scaled[p], 2 * (k + 1))
                at_least(pool, y_added[1 - p], 32 * (k + p))
                settle(pool)
                for h in range(2):
                    pool.indirect_dma_start(out=y_d, out_offset=bass.IndirectOffsetOnAxis(ap=cidx_s[:, p, h:h + 1].bitcast(U32), axis=0),
                                            in_=ye[:, p, h, :], in_offset=None, compute_op=ALU.add).then_inc(y_added[p], 16)

            def c_expert(n, p, k, left):
                if left == 2:
                    c_gather(n + 2, p, k + 1)
                if not is_first(n):
                    c_scatter(n - 1, *before_it(p, k))

            def between(g, m):
                if m == 3:
                    pool.wait_ge(place_token_in, 16 * (g + 2))

            pool.wait_ge(place_token_in, 16)
            pool.wait_ge(y_cleared, 16 * NT)
            c_gather(0, 0, 0)
            c_gather(1, 1, 0)
            experts(pool, c_expert, between)
            c_scatter(E2 - 1, 1, E2 // 2 - 1)

            for q in range(4):
                js = slice(4 * q, 4 * q + 4)
                pool.wait_ge(mv3_made, q + 1)
                pool.tensor_scalar(ve3[:, js], mv3[:, js, 1], 1.0, LN_EPS, ALU.mult, ALU.add).then_inc(ve3_made, 1)
                pool.wait_ge(ve3_made, q + 1)
                pool.tensor_tensor(rstd3[:, js], ve3[:, js], minus_half[:, 0:4], ALU.pow).then_inc(rstd3_made, 1)
                pool.wait_ge(rstd3_made, q + 1)
                pool.tensor_tensor(shift3[:, js], mv3[:, js, 0], rstd3[:, js], ALU.mult).then_inc(shift_made, 1)
                pool.wait_ge(shift_made, 2 * q + 1)
                pool.tensor_scalar(shift3[:, js], shift3[:, js], -1.0, None, ALU.mult).then_inc(shift_made, 1)


def kernel(**inputs):
    import concourse.bacc as bacc
    from concourse.bass_utils import run_bass_kernel_spmd as run

    a = {k: np.asarray(v) for k, v in inputs.items()}
    x = a["x"].reshape(TOK, D)

    def rows(w):
        return w.reshape(KC, P, -1).transpose(1, 0, 2)

    gu = a["L0_ffn_gate_up_proj"]
    gu = np.concatenate([gu[:, 0:P], gu[:, FI:FI + P], gu[:, P:FI], gu[:, FI + P:]], 1)
    arrays = {
        "x": x,
        "xT": x.reshape(NT, P, KC, P).transpose(0, 3, 2, 1),
        "wqkv": np.stack([rows(a["L0_attn_W" + n]) for n in "qkv"], 2),
        "wo": rows(a["L0_attn_Wo"]),
        "wg1": rows(a["L0_attn_Wg1"]),
        "wg2": a["L0_attn_Wg2"],
        "nw": a["L0_attn_norm_weight"].reshape(KC, P).T,
        "ctxw": a["ctx_2048"].reshape(E1, D, KC, P).transpose(3, 0, 2, 1),
        "tok": a["itok_BxS_13_99985"].reshape(NT, P).T,
        "gate_weight": a["L0_ffn_gate_weight"],
        "o2n": a["L0_ffn_old_to_new"].reshape(OLD, 1),
        "gu": gu.reshape(E2, 2 * FI, KC, P).transpose(0, 3, 2, 1),
        "dn": a["L0_ffn_down_proj"].transpose(0, 2, 1),
        **shape_constants(),
    }
    arrays["attn_pack"] = pack_rows(arrays, ATTN_PACK)
    arrays["sort_pack"] = pack_rows(arrays, SORT_PACK)
    arrays = {"in_" + k: np.ascontiguousarray(v) for k, v in arrays.items()}
    nc = bacc.Bacc("TRN2", target_bir_lowering=False, num_devices=1)
    d = {k[3:]: nc.dram_tensor(k, v.shape, mybir.dt.from_np(v.dtype), kind="ExternalInput").ap() for k, v in arrays.items()}
    d["out"] = nc.dram_tensor("out", (TOK, D), F32, kind="ExternalOutput").ap()
    build(nc, d)
    r = run(nc, [arrays], core_ids=[0])
    return np.asarray(r.results[0]["out"]).reshape(a["x"].shape)
```

```python
from contextlib import ExitStack

import numpy as np
import concourse.bass as bass
from concourse import mybir

F32 = mybir.dt.float32
F32R = mybir.dt.float32r
BF16 = mybir.dt.bfloat16
F16 = mybir.dt.float16
I32 = mybir.dt.int32
U32 = mybir.dt.uint32
ALU = mybir.AluOpType
ACT = mybir.ActivationFunctionType
AX = mybir.AxisListType

P = 128
D = 512
KC = D // P
NB, SEQ = 4, 512
CH = SEQ // P
TOK = NB * SEQ
NT = TOK // P
H, HD = 16, 32
G = D // P
HG = P // HD
RANK = 32
LN_EPS, RMS_EPS = 1e-5, 1e-6

E1 = 4
VOCAB = 25000
PER = VOCAB // E1
SLOT_T = NT + E1 - 1
SLOTS = SLOT_T * P

OLD, E2, TOPK = 128, 48, 8
HALF_D = D // 2
FI = 192
CAP = 192
HALF = CAP // 2
NA, NBB = 12, 16
GE = 8
NG = E2 // GE
PART = (NT - 1) // (NG - 1)
assert PART * (NG - 1) == NT - 1
ROW = D + E2
SPARE = 2 * P
ARENA = 75 * 256
NEG = -1e30
TAKEN = -3e38


ATTN_PACK = [("eye", P, (P,)), ("cos", P, (CH, HD)), ("sin", P, (CH, HD)), ("dk", P, (H,)), ("lam", P, (G,)), ("nw", P, (KC,)),
             ("dq", P, (G, P)), ("block", P, (P,)), ("wg1", P, (KC, RANK))]
SORT_PACK = [("before", P, (P,)), ("ids", P, (NT,)), ("tile_no", P, (SLOT_T,)), ("n_iota", P, (E2,)),
             ("ab_iota", P, (NA + NBB,)), ("place_no", GE * NA, (NBB,)), ("diag8", GE * NA, (GE,))]


def pack_rows(arrays, parts):
    out = np.zeros((P, sum(int(np.prod(shape)) for _, _, shape in parts)), np.float32)
    at = 0
    for name, rows, shape in parts:
        n = int(np.prod(shape))
        out[0:rows, at:at + n] = arrays.pop(name).reshape(rows, n)
        at += n
    return out


def shape_constants():
    f = np.float32
    i = np.arange(P)
    lam = -(f(2.0) ** (f(-8.0) * (np.arange(H, dtype=f) + f(1)) / f(H))).astype(f)
    diff = (i[None, :] - i[:, None]).astype(f)
    decay = np.where(diff[:, None, :] >= 0, np.exp(lam[None, :, None] * np.maximum(diff, 0)[:, None, :]), 0).astype(f)
    dq = np.exp(lam[:, None] * (i[None, :].astype(f) + f(1)))
    dk = np.exp(lam[None, :] * (f(P - 1) - i[:, None].astype(f)))
    lam_c = np.exp(lam * f(P))
    theta = f(10000.0) ** (f(-2.0) * np.arange(HD // 2, dtype=f) / f(HD))
    ang = (np.arange(SEQ, dtype=f)[:, None] * theta[None, :].astype(f)).astype(f)
    cos, sin = np.cos(ang).astype(f), np.sin(ang).astype(f)
    cos2 = np.concatenate([cos, cos], 1).reshape(CH, P, HD).transpose(1, 0, 2)
    sin2 = np.concatenate([-sin, sin], 1).reshape(CH, P, HD).transpose(1, 0, 2)
    by_row = np.repeat(np.arange(HG), HD)
    dq_t = np.stack([dq[g * HG + by_row] for g in range(G)], 1)
    lam_t = np.stack([lam_c[g * HG + by_row] for g in range(G)], 1)
    c = {
        "eye": np.eye(P), "decay": decay, "dq": dq_t, "dk": dk, "lam": lam_t, "cos": cos2, "sin": sin2,
        "block": (by_row[:, None] == by_row[None, :]),
        "before": (i[:, None] < i[None, :]),
        "ids": (i[:, None] + P * np.arange(NT)[None, :]),
        "tile_no": np.broadcast_to(np.arange(SLOT_T), (P, SLOT_T)),
        "n_iota": np.broadcast_to(np.arange(E2), (P, E2)),
        "ab_iota": np.broadcast_to(np.concatenate([np.arange(NA), np.arange(NBB)]), (P, NA + NBB)),
        "place_no": (NBB * (np.arange(GE * NA)[:, None] % NA) + np.arange(NBB)[None, :]),
        "diag8": (np.arange(GE * NA)[:, None] // NA == np.arange(GE)[None, :]),
    }
    c = {k: np.ascontiguousarray(v, dtype=f) for k, v in c.items()}
    c["spare"] = (TOK + i[:, None] + P * (np.arange(SLOT_T)[None, :] % 2)).astype(np.int32)
    return c


def build(nc, d):
    with ExitStack() as ctx:
        def sb(name, shape, dt=F32):
            return ctx.enter_context(nc.sbuf_tensor(name, shape, dt))

        def sem(name):
            return ctx.enter_context(nc.semaphore(name))

        def sem2(name):
            return [sem(name + "_even"), sem(name + "_odd")]

        def unpack(name, parts):
            pack = sb(name, [P, sum(int(np.prod(shape)) for _, _, shape in parts)])
            packs[name] = pack
            views, at = [], 0
            for _, rows, shape in parts:
                n = int(np.prod(shape))
                part = pack[0:rows, at:at + n]
                if len(shape) == 2:
                    part = part.rearrange("p (a b) -> p a b", b=shape[1])
                views.append(part)
                at += n
            return views

        packs = {}

        def whole(t):
            return t[(slice(None),) * len(t.shape)]

        arena = sb("arena", [P, ARENA])
        cut = [0]

        def take(name, shape, dt=F32):
            words = int(np.prod(shape[1:])) * mybir.dt.size(dt) // 4
            at, cut[0] = cut[0], cut[0] + (words + 7) // 8 * 8
            assert cut[0] <= ARENA, (name, cut[0])
            part = arena[0:shape[0], at:at + words]
            if dt != F32:
                part = part.bitcast(dt)
            axes = "abcd"[:len(shape) - 1]
            if len(axes) == 1:
                return part
            return part.rearrange(f"p ({' '.join(axes)}) -> p {' '.join(axes)}", **dict(zip(axes[1:], shape[2:])))

        x1_d = nc.dram_tensor("x1_rows", (TOK + SPARE, D), F32, kind="Internal").ap()
        x2_d = nc.dram_tensor("x2_rows", (TOK + SPARE, ROW), F32, kind="Internal").ap()
        y_d = nc.dram_tensor("y_rows", (TOK + SPARE, D), F32, kind="Internal").ap()
        token_of_slot_d = nc.dram_tensor("token_of_slot", (SLOTS, 1), I32, kind="Internal").ap()
        token_of_place_d = nc.dram_tensor("token_of_place", (E2 * CAP, 1), I32, kind="Internal").ap()

        eye, cos, sin, dk, lam, nw, dq, block_diag, wg1 = unpack("attn_pack", ATTN_PACK)
        before, ids, tile_no, n_iota, ab_iota, place_no, diag8 = unpack("sort_pack", SORT_PACK)
        raw = sb("raw", [P, 4, KC, D])
        w_hi = sb("w_hi", [P, 4, KC, D], F32R)
        w_lo = sb("w_lo", [P, 4, KC, D], F32R)
        x_hi = sb("x_hi", [P, KC, P], F32R); x_lo = sb("x_lo", [P, KC, P], F32R)
        o_hi = sb("o_hi", [P, KC, P], F32R); o_lo = sb("o_lo", [P, KC, P], F32R)
        wg2 = sb("wg2", [RANK, D])
        gatew = sb("gatew", [OLD, D])
        o2n_i = sb("o2n_i", [OLD, 1], I32)

        ones = sb("ones", [P, P])
        zero = sb("zero", [P, D])
        minus_half = sb("minus_half", [P, H])
        warm = sb("warm", [P, H])

        decay = take("decay", [P, H, P])
        xT = take("xT", [P, 2, KC, P])
        x_res = sb("x_res", [P, 2, D])
        q_act = take("q_act", [P, D]); k_act = take("k_act", [P, D])
        rot1_q = take("rot1_q", [P, D]); rot1_k = take("rot1_k", [P, D])
        rot2_q = take("rot2_q", [P, D]); rot2_k = take("rot2_k", [P, D])
        q_rot = take("q_rot", [P, D]); k_rot = take("k_rot", [P, D])
        k_dec = take("k_dec", [P, 2, D])
        v = take("v", [P, 2, D])
        q_blocks = take("q_blocks", [P, G, HG, P])
        q_decT = take("q_decT", [P, G, P])
        kT = take("kT", [P, G, P])
        weighted = take("weighted", [P, H, P])
        g1T = take("g1T", [RANK, P])
        sig_gate = take("sig_gate", [P, D])
        state = take("state", [P, 2, G, P])
        state_dec = take("state_dec", [P, G, P])
        state_add = take("state_add", [P, G, P])
        gated = take("gated", [P, D])
        squares = take("squares", [P, D])
        ms = take("ms", [P, H]); ms_eps = take("ms_eps", [P, H]); rms_inv = take("rms_inv", [P, H])
        normed = take("normed", [P, D])
        r1 = take("r1", [P, D])
        stat1 = take("stat1", [P, 6]); mv1 = take("mv1", [P, 2]); ve1 = take("ve1", [P, 1]); rstd1 = take("rstd1", [P, 1])
        x1o = sb("x1o", [P, 2, D])
        tok_i = sb("tok_i", [P, NT], I32)
        tok_f = sb("tok_f", [P, NT])
        ge = sb("ge", [P, E1 - 1, NT])
        onehot = sb("onehot", [P, E1, NT])
        total = sb("total", [P, E1, NT])
        cum = sb("cum", [P, E1, NT])
        rank = sb("rank", [P, E1, NT])
        lot = sb("lot", [P, E1, NT])
        tiles = sb("tiles", [P, E1])
        tiles_cum = sb("tiles_cum", [P, E1])
        start = sb("start", [P, E1])
        dest = sb("dest", [P, NT])
        slot_i = sb("slot_i", [P, NT], I32)
        row_i = sb("row_i", [P, NT], I32)
        dest_i = sb("dest_i", [P, NT], U32)
        ids_i = sb("ids_i", [P, NT], I32)
        spare_i = sb("spare_i", [P, SLOT_T], I32)
        name_to = sb("name_to", [P, 1], U32)
        name_of = sb("name_of", [P, 1], I32)
        eid_f = sb("eid_f", [P, SLOT_T])
        eid_i = sb("eid_i", [P, SLOT_T], I32)

        cut[0] = 0
        slot_token = sb("slot_token", [P, SLOT_T], I32)
        idx_g = sb("idx_g", [P, 2], I32)
        idx_s = sb("idx_s", [P, 2], I32)
        x1g = take("x1g", [P, 4, D])
        sig_s = take("sig_s", [P, D])
        s_act = take("s_act", [P, D])
        h1 = take("h1", [P, D])
        r2 = take("r2", [P, D])
        stat2 = take("stat2", [P, 6]); mv2 = take("mv2", [P, 2]); ve2 = take("ve2", [P, 1]); rstd2 = take("rstd2", [P, 1])
        x2o = take("x2o", [P, 4, ROW])
        x2T = take("x2T", [P, KC, P])
        router = sb("router", [P, KC, E2])
        o2n_f = sb("o2n_f", [OLD, 1])
        pick = sb("pick", [OLD, E2])
        kept_bias = sb("kept_bias", [P, E2])
        logits = take("logits", [P, E2])
        top8 = take("top8", [P, TOPK])
        marked = take("marked", [P, E2])
        neg_max = take("neg_max", [P, 1])
        es = take("es", [P, E2]); es1 = take("es1", [P, E2]); es_inv = take("es_inv", [P, E2])
        expo = take("expo", [P, E2])
        chosen = take("chosen", [P, E2])
        w_sum = take("w_sum", [P, 1]); w_inv = take("w_inv", [P, 1])
        not_chosen = take("not_chosen", [P, E2])

        before_b = sb("before_b", [P, P], BF16)
        same_expert = sb("same_expert", [P, E2, NT], BF16)
        ones_b = sb("ones_b", [P, P], BF16)
        ab_h = sb("ab_h", [P, NA + NBB], F16)
        ids_h = sb("ids_h", [P, NT], F16)
        cut[0] = 0
        wnat = take("wnat", [P, NT, E2])
        sel = take("sel", [P, NT, E2], BF16)
        sel_t = take("sel_t", [P, E2, NT], BF16)
        sel_so_far = take("sel_so_far", [P, E2, NT], BF16)
        ok = take("ok", [P, NT, E2])
        place = take("place", [P, NT, E2])
        place_i = take("place_i", [P, NT, E2], I32)
        a_i = take("a_i", [P, NT, E2], I32)
        b_i = take("b_i", [P, NT, E2], I32)
        a_h = take("a_h", [P, NT, E2 + GE], F16)
        b_h = take("b_h", [P, NT, E2 + GE], F16)
        hot_a = take("hot_a", [P, NT, GE, NA], F16)
        hot_b = take("hot_b", [P, NT, GE, NBB], F16)
        hot_id = take("hot_id", [P, NT, GE, NA], F16)
        tab = take("tab", [GE * NA, GE, NBB])
        tab_r = take("tab_r", [GE * NA, NBB])
        tab_spare = take("tab_spare", [GE * NA, NBB])
        tab_i = take("tab_i", [GE * NA, NBB], I32)

        wgu = [raw[:, k, :, :].rearrange("p a b -> p (a b)")[:, 0:KC * 2 * FI].rearrange("p (k o) -> p k o", k=KC) for k in range(2)]
        wdn = [raw[:, 2 + k, 0:2, :] for k in range(2)]
        wdn_hi = [w_hi[:, k, 0:2, :] for k in range(2)]
        wdn_lo = [w_hi[:, k, 2:4, :] for k in range(2)]
        by_parity = lambda z: z[:, :, :].rearrange("p k t -> p (k t)")[:, 0:2 * CAP].rearrange("p (a s) -> p a s", a=2)
        ha_hi, ha_lo, hc, hc_hi = by_parity(x_hi), by_parity(x_lo), by_parity(o_hi), by_parity(o_lo)
        place_token = take("place_token", [HALF, E2, 2], I32)
        cidx_g = take("cidx_g", [HALF, 2, 2], I32)
        cidx_s = take("cidx_s", [HALF, 2, 2], I32)
        xg = take("xg", [HALF, 2, 2, ROW])
        xgT = take("xgT", [P, 2, KC, CAP])
        w_col = take("w_col", [HALF, 2, 2])
        sig_a = take("sig_a", [P, CAP]); sig_c = take("sig_c", [P, CAP])
        g_a = take("g_a", [P, CAP]); g_c = take("g_c", [P, CAP])
        h_a = take("h_a", [P, 2, CAP])
        h_c = take("h_c", [P, 2, CAP])
        ye = take("ye", [HALF, 2, 2, D])

        cut[0] = 0
        y_all = take("y_all", [P, NT, D])
        x2_all = whole(w_lo).bitcast(F32).rearrange("p e k n -> p (e k) n")
        stat3 = sb("stat3", [P, NT, 6]); mv3 = sb("mv3", [P, NT, 2]); ve3 = sb("ve3", [P, NT]); rstd3 = sb("rstd3", [P, NT])
        shift3 = sb("shift3", [P, NT])

        ps = ctx.enter_context(nc.psum_tensor("ps", [P, 8, 512], F32))
        PQ, PK, PV, PT, PS0, PO, PM = 0, 1, 2, 3, 4, 6, 7

        attn_in = sem("attn_in"); late_in = sem("late_in"); sort_in = sem("sort_in"); gate_in = sem("gate_in"); ctx_in = sem("ctx_in"); wqk_in = sem("wqk_in"); wv_in = sem("wv_in"); wo_in = sem("wo_in")
        w_high = sem("w_high"); w_split = sem("w_split"); x_high = sem("x_high"); x_split = sem("x_split")
        o_high = sem("o_high")
        xT_in = sem2("xT_in")
        x_in = sem2("x_in")
        setup = sem("setup"); zeroed = sem("zeroed"); sort_v = sem("sort_v"); sort_p = sem("sort_p")
        slot_sorted = sem("slot_sorted"); slots_cleared = sem("slots_cleared"); slots_named = sem("slots_named"); name_set = sem("name_set")
        rows_cleared = sem("rows_cleared")
        v_made = sem("v_made"); q_made = sem("q_made"); k_made = sem("k_made")
        v_copied = sem("v_copied"); q_sig = sem("q_sig"); k_sig = sem("k_sig")
        q_silu = sem("q_silu"); k_silu = sem("k_silu")
        q_r1 = sem("q_r1"); k_r1 = sem("k_r1"); q_r2 = sem("q_r2"); k_r2 = sem("k_r2")
        q_rotated = sem("q_rotated"); k_rotated = sem("k_rotated"); k_decayed = sem("k_decayed")
        q_turned = sem("q_turned"); k_turned = sem("k_turned")
        qT_copied = sem("qT_copied"); qT_decayed = sem("qT_decayed"); kT_copied = sem("kT_copied")
        g1_made = sem("g1_made"); g1_copied = sem("g1_copied"); gate_made = sem("gate_made"); gate_sig = sem("gate_sig")
        scored = sem("scored"); masked = sem("masked")
        add_made = sem("add_made"); add_cut = sem("add_cut"); st_decayed = sem("st_decayed"); st_new = sem("st_new")
        o_made = sem("o_made"); o_gated = sem("o_gated"); squared = sem("squared"); ms_made = sem("ms_made")
        ms_plus = sem("ms_plus"); rms_made = sem("rms_made"); o_normed = sem("o_normed")
        o_turned = sem("o_turned"); oT_copied = sem("oT_copied"); wo_made = sem("wo_made")
        r1_made = sem("r1_made"); stat_made = sem("stat_made"); mv_made = sem("mv_made")
        ve_made = sem("ve_made"); rstd_made = sem("rstd_made"); x1_made = sem("x1_made"); x1_kept = sem2("x1_kept")
        slot_token_in = sem("slot_token_in"); idx_g_set = sem("idx_g_set"); idx_s_set = sem("idx_s_set"); x1_got = sem2("x1_got")
        xg1_turned = sem("xg1_turned"); xg1_copied = sem("xg1_copied"); s_made = sem("s_made"); s_sig = sem("s_sig")
        s_silu = sem("s_silu"); h1_made = sem("h1_made"); h1_turned = sem("h1_turned"); h1_copied = sem("h1_copied")
        y1_made = sem("y1_made"); r2_made = sem("r2_made")
        x2_made = sem("x2_made")
        x2_turned = sem("x2_turned"); x2T_copied = sem("x2T_copied"); lg_made = sem("lg_made")
        router_v = sem("router_v"); rstep = sem("weights_v"); w_inverted = sem("w_inverted"); es_made = sem("es_made"); routed = sem("routed"); x2_kept = sem2("x2_kept")
        pick_v = sem("pick_v"); wo_scaled = sem("wo_scaled")
        wnat_in = sem("wnat_in"); tab_v = sem("tab_v"); pos_made = sem("pos_made"); hot_made = sem("hot_made")
        tab_made = sem("tab_made"); tab_cut = sem("tab_cut"); places_kept = sem("places_kept")
        c_half = sem("c_half"); tstep = sem("place_v"); hot_parts = sem("hot_parts")
        tab_masked = sem("tab_masked"); tab_step = sem("tab_step"); passed = sem("passed")
        gu_in = sem2("gu_in"); dn_in = sem2("dn_in"); place_token_in = sem("place_token_in"); cg_set = sem("cg_set"); cs_set = sem("cs_set")
        got = sem2("got"); c_turned = sem2("c_turned"); c_copied = sem("c_copied"); w_copied = sem2("w_copied")
        gu_made = sem2("gu_made"); c_sig = sem("c_sig"); g_made = sem("g_made"); h_made = sem("h_made")
        dn_made = sem2("dn_made"); dn_split = sem2("dn_split"); dn_high = sem("dn_high"); h_high = sem("h_high"); h_split = sem("h_split"); y_scaled = sem2("y_scaled"); y_added = sem2("y_added"); y_cleared = sem("y_cleared")
        y_in = sem2("y_in"); x2_in = sem("x2_in"); shift_made = sem("shift_made"); r3_too = sem("r3_too"); r3_made = sem("r3_made")
        out_made = sem("out_made"); out_kept = sem("out_kept")

        def tiles_of_a(eng, step):
            for c in range(2):
                step(0, c, c == 0, False)
            with eng.Fori(0, NB - 1) as i:
                for c in range(2, CH):
                    step(i, c, False, False)
                for c in range(2):
                    step(i + 1, c, False, False)
            for c in range(2, CH):
                step(NB - 1, c, False, c == CH - 1)

        def split_ahead(b, c):
            return not (isinstance(b, int) and b == NB - 1 and c >= 2)

        def next_of(b, c):
            return (b, c + 1) if c < CH - 1 else (b + 1, 0)

        def last_of(b, c):
            return (b, c - 1) if c else (b - 1, CH - 1)

        def at_least(eng, s, n):
            if not (isinstance(n, int) and n <= 0):
                eng.wait_ge(s, n)

        def settle(eng):
            eng.sem_inc(passed, 1)

        def is_later(n):
            return not (isinstance(n, int) and n < 2)

        def is_first(n):
            return isinstance(n, int) and n == 0

        def slot_tiles(eng, step):
            for n in range(5):
                step(n, n % 2, n // 2, 2, n % 4)
            with eng.Fori(0, (SLOT_T - 7) // 4) as i:
                for m in range(5, 9):
                    step(4 * i + m, m % 2, 2 * i + m // 2, 2, m % 4)
            for n in range(SLOT_T - 2, SLOT_T):
                step(n, n % 2, n // 2, SLOT_T - 1 - n, n % 4)

        def experts(eng, step, between=None):
            for n in range(3):
                step(n, n % 2, n // 2, 2)
            with eng.Fori(0, NG - 1) as g:
                for m in range(GE):
                    if between:
                        between(g, m)
                    step(GE * g + 3 + m, (3 + m) % 2, (GE // 2) * g + (3 + m) // 2, 2)
            for n in range(E2 - 5, E2):
                step(n, n % 2, n // 2, min(E2 - 1 - n, 2))

        def before_it(p, k):
            return 1 - p, k - (1 - p)

        def after_it(p, k):
            return 1 - p, k + p

        block = ctx.enter_context(nc.Block())

        @block.sync
        def _(sp):
            sp.dma_start(whole(packs["sort_pack"]), d["sort_pack"]).then_inc(sort_in, 16)
            sp.dma_start(tok_i[:, :], d["tok"]).then_inc(sort_in, 16)
            sp.dma_start(xT[:, 0], d["xT"][0]).then_inc(xT_in[0], 16)
            sp.dma_start(raw[:, 2], d["wqkv"][:, 2]).then_inc(wv_in, 16)
            for n in range(2):
                sp.dma_start(raw[:, n], d["wqkv"][:, n]).then_inc(wqk_in, 16)
            sp.dma_start(whole(packs["attn_pack"]), d["attn_pack"]).then_inc(attn_in, 16)
            sp.dma_start(gatew[:, :], d["gate_weight"]).then_inc(gate_in, 16)
            sp.dma_start(o2n_i[:, :], d["o2n"]).then_inc(gate_in, 16)
            sp.dma_start(raw[:, 3], d["wo"]).then_inc(wo_in, 16)
            sp.dma_start(xT[:, 1], d["xT"][1]).then_inc(xT_in[1], 16)
            sp.dma_start(wg2[:, :], d["wg2"]).then_inc(late_in, 16)
            sp.dma_start(whole(decay), d["decay"]).then_inc(late_in, 16)
            sp.dma_start(spare_i[:, :], d["spare"]).then_inc(late_in, 16)
            for c in range(2):
                sp.dma_start(x_res[:, c, :], d["x"][c * P:(c + 1) * P, :]).then_inc(x_in[c % 2], 16)
            sp.wait_ge(late_in, 48)
            sp.dma_start(token_of_slot_d.rearrange("(p j) a -> p (j a)", p=P), spare_i[:, :]).then_inc(slots_cleared, 16)
            sp.wait_ge(zeroed, 2)

            def spare_rows():
                for k in range(2):
                    r = TOK + k * P
                    sp.dma_start(x1_d[r:r + P, :], zero[:, :]).then_inc(x1_kept[k], 16)
                    sp.dma_start(x2_d[r:r + P, 0:D], zero[:, :]).then_inc(rows_cleared, 16)
                    sp.dma_start(x2_d[r:r + P, D:ROW], zero[:, 0:E2]).then_inc(rows_cleared, 16)
                    sp.dma_start(y_d[r:r + P, :], zero[:, :]).then_inc(rows_cleared, 16)

            def store_x1(b, c):
                t = 4 * b + c
                sp.wait_ge(x1_made, t + 1)
                sp.dma_start(x1_d[bass.ds(P * t, P), :], x1o[:, c % 2, :]).then_inc(x1_kept[c % 2], 16)

            def a_tile(b, c, first, last):
                t = 4 * b + c
                if not first and not last:
                    bn, cn = next_of(b, c)
                    sp.wait_ge(g1_made, t)
                    sp.dma_start(xT[:, cn % 2], d["xT"][bass.ds(t + 1, 1)].rearrange("a p k t -> (a p) k t")).then_inc(xT_in[cn % 2], 16)
                sp.dma_start(y_d[bass.ds(P * t, P), :], zero[:, :]).then_inc(y_cleared, 16)
                if isinstance(t, int) and t == 1:
                    spare_rows()
                    sp.wait_ge(w_split, 4)
                    sp.dma_start(whole(raw), d["ctxw"]).then_inc(ctx_in, 16)
                if not (isinstance(t, int) and t < 2):
                    store_x1(*last_of(*last_of(b, c)))
                    sp.dma_start(x_res[:, c % 2, :], d["x"][bass.ds(P * t, P), :]).then_inc(x_in[c % 2], 16)

            tiles_of_a(sp, a_tile)
            sp.wait_ge(slots_named, 16 * NT)
            sp.dma_start(slot_token[:, :], token_of_slot_d.rearrange("(p j) a -> p (j a)", p=P)).then_inc(slot_token_in, 16)
            store_x1(NB - 1, CH - 2)
            store_x1(NB - 1, CH - 1)

            def load_up(n, p, k):
                at_least(sp, gu_made[p], k)
                sp.dma_start(wgu[p], d["gu"][bass.ds(n, 1)].rearrange("a p k o -> (a p) k o")).then_inc(gu_in[p], 16)

            def load_down(n, p, k):
                at_least(sp, dn_split[p], k)
                sp.dma_start(wdn[p][:, 0, :], d["dn"][bass.ds(n, 1), 0:P, :].rearrange("a p h -> (a p) h")).then_inc(dn_in[p], 16)
                sp.dma_start(wdn[p][P // 2:P, 1, :], d["dn"][bass.ds(n, 1), P:FI, :].rearrange("a p h -> (a p) h")).then_inc(dn_in[p], 16)

            def load_expert(n, p, k, left):
                if left == 2:
                    load_up(n + 2, p, k + 1)
                if left:
                    load_down(n + 1, *after_it(p, k))

            sp.wait_ge(x1_got[0], 32)
            sp.wait_ge(w_split, 4 + E1)
            load_up(0, 0, 0)
            load_down(0, 0, 0)
            load_up(1, 1, 0)

            sp.wait_ge(x2_kept[0], 16 * (SLOT_T - SLOT_T // 2))
            sp.wait_ge(x2_kept[1], 16 * (SLOT_T // 2))
            sp.dma_start(whole(wnat), x2_d[0:TOK, D:ROW].rearrange("(j p) n -> p j n", p=P)).then_inc(wnat_in, 16)
            def keep_places(g):
                rows = token_of_place_d[bass.ds(g * GE * CAP, GE * CAP), :]
                sp.wait_ge(tab_cut, g + 1)
                sp.dma_start(rows.rearrange("(r b) a -> r (b a)", b=NBB), tab_i[:, :]).then_inc(places_kept, 16)
                sp.wait_ge(places_kept, 16 * (g + 1))
                sp.dma_start(place_token[:, bass.ds(g * GE, GE), :], rows.rearrange("(n p h) a -> p n (h a)", n=GE, h=2))\
                  .then_inc(place_token_in, 16)

            def between(g, m):
                if m == 2:
                    keep_places(g + 1)
                if m == 5:
                    js = bass.ds(PART * g, PART)
                    sp.dma_start(x2_all[:, js, :], x2_d[bass.ds(PART * P * g, PART * P), 0:D].rearrange("(j p) n -> p j n", p=P))\
                      .then_inc(x2_in, 16)

            keep_places(0)
            sp.dma_start(x2_all[:, NT - 1, :], x2_d[(NT - 1) * P:TOK, 0:D]).then_inc(x2_in, 16)
            experts(sp, load_expert, between)

            for p in range(2):
                sp.wait_ge(y_added[p], 32 * (E2 // 2))
            for q in range(4):
                at_least(sp, y_in[q % 2], 16 * (q // 2))
                sp.dma_start(y_all[:, 4 * q:4 * q + 4, :], y_d[4 * q * P:4 * (q + 1) * P, :].rearrange("(j p) n -> p j n", p=P))\
                  .then_inc(y_in[q % 2], 16)

        @block.tensor
        def _(pe):
            def three_passes(out, a_hi, a_lo, b_hi, b_lo, low=None, between=None):
                for i, (lhs, rhs) in enumerate(((a_hi, b_hi), (a_hi, b_lo), (a_lo, b_hi))):
                    if low and i == 2:
                        pe.wait_ge(*low)
                    for k in range(KC):
                        m = pe.matmul(out, lhs[:, k, :], rhs[:, k, :], start=(i == 0 and k == 0), stop=(i == 2 and k == KC - 1))
                        if between:
                            between(i * KC + k)
                return m

            def project(n, bank, made, done, b, c):
                t = 4 * b + c
                pe.wait_ge(x_split, t + 1)
                at_least(pe, done, t)
                three_passes(ps[:, bank, :], x_hi, x_lo, w_hi[:, n], w_lo[:, n]).then_inc(made, 1)

            def project_q(b, c):
                project(0, PQ, q_made, q_silu, b, c)

            def project_k(b, c):
                project(1, PK, k_made, k_silu, b, c)

            def project_v(b, c):
                project(2, PV, v_made, v_copied, b, c)

            def gate_low(b, c):
                t = 4 * b + c
                at_least(pe, r1_made, t - 1)
                at_least(pe, add_cut, 3 * b + c)
                pe.wait_ge(xT_in[c % 2], 16 * (2 * b + c // 2 + 1))
                for k in range(KC):
                    m = pe.matmul(ps[0:RANK, PM, 0:P], wg1[:, k, :], xT[:, c % 2, k, :], start=(k == 0), stop=(k == KC - 1))
                m.then_inc(g1_made, 1)

            def turn_o(b, c):
                t = 4 * b + c
                pe.wait_ge(o_normed, t + 1)
                at_least(pe, kT_copied, t + 2 if not isinstance(t, int) or t < NT - 1 else NT)
                for k in range(KC):
                    m = pe.transpose(ps[:, PT, k * P:(k + 1) * P], normed[:, k * P:(k + 1) * P], eye[:, :])
                m.then_inc(o_turned, 1)

            def project_o(b, c, now, cuts, between=None):
                t = 4 * b + c
                pe.wait_ge(oT_copied, t + 1)
                at_least(pe, w_split, 4)
                pe.wait_ge(gate_sig, now + 1)
                pe.wait_ge(add_cut, cuts)
                at_least(pe, r1_made, t)
                three_passes(ps[:, PM, :], o_hi, o_lo, w_hi[:, 3], w_lo[:, 3], between=between).then_inc(wo_made, 1)

            def a_tile(b, c, first, last):
                t = 4 * b + c
                bn, cn = next_of(b, c)
                pe.wait_ge(q_rotated, t + 1)
                at_least(pe, oT_copied, t - 1)
                at_least(pe, kT_copied, t)
                for g in range(G):
                    m = pe.transpose(ps[:, PT, g * P:(g + 1) * P], q_rot[:, g * P:(g + 1) * P], eye[:, :])
                m.then_inc(q_turned, 1)
                if not last:
                    project_v(bn, cn)
                gate_low(b, c)
                if not last:
                    project_q(bn, cn)
                pe.wait_ge(k_rotated, t + 1)
                pe.wait_ge(qT_copied, t + 1)
                pe.wait_ge(qT_decayed, t + 1)
                for g in range(G):
                    m = pe.transpose(ps[:, PT, g * P:(g + 1) * P], k_rot[:, g * P:(g + 1) * P], eye[:, :])
                m.then_inc(k_turned, 1)
                pe.wait_ge(g1_copied, t + 1)
                pe.matmul(ps[:, PM, :], g1T[:, :], wg2[:, :], start=True, stop=True).then_inc(gate_made, 1)
                pe.wait_ge(kT_copied, t + 1)
                for g in range(G):
                    at_least(pe, masked, 4 * t + max(g - 1, 0))
                    pe.matmul(ps[:, PS0 + g % 2, :], kT[:, g, :], q_blocks[:, g, :, :].rearrange("p a b -> p (a b)"),
                              start=True, stop=True).then_inc(scored, 1)
                if not first:
                    turn_o(*last_of(b, c))
                if c < CH - 1:
                    pe.wait_ge(k_decayed, 3 * b + c + 1)
                    pe.wait_ge(v_copied, t + 1)
                    pe.wait_ge(gate_sig, t + 1)
                    for g in range(G):
                        m = pe.matmul(ps[:, PM, g * P:(g + 1) * P], k_dec[:, c % 2, g * P:(g + 1) * P],
                                      v[:, c % 2, g * P:(g + 1) * P], start=True, stop=True)
                    m.then_inc(add_made, 1)
                if not last:
                    project_k(bn, cn)
                pe.wait_ge(v_copied, t + 1)
                pe.wait_ge(masked, 4 * t + G)
                at_least(pe, o_gated, t)
                if c:
                    pe.wait_ge(st_new, 3 * b + c)

                def from_state(g):
                    pe.matmul(ps[:, PO, g * P:(g + 1) * P], q_decT[:, g, :], state[:, (c - 1) % 2, g, :],
                              start=(g == 0), stop=False, skip_group_check=True)

                def own_pairs(h):
                    m = pe.matmul(ps[:, PO, h * HD:(h + 1) * HD], weighted[:, h, :], v[:, c % 2, h * HD:(h + 1) * HD],
                                  start=(c == 0 and h == 0), stop=(h == H - 1), skip_group_check=True)
                    if h == H - 1:
                        m.then_inc(o_made, 1)

                short = [(from_state, g) for g in range(G if c else 0)] + [(own_pairs, h) for h in range(H)]
                todo = list(short)

                def some(n):
                    while todo and len(short) - len(todo) < (n + 1) * len(short) / (3 * KC):
                        step, i = todo.pop(0)
                        step(i)

                if first:
                    some(3 * KC)
                else:
                    project_o(*last_of(b, c), t, 3 * b + min(c + 1, 3), some)

            pe.wait_ge(sort_v, 3)
            pe.wait_ge(setup, 2)
            flat = onehot[:, :, :].rearrange("p e j -> p (e j)")
            pe.matmul(ps[:, PO, 0:E1 * NT], before, flat, start=True, stop=True)
            pe.matmul(ps[:, PO, 64:64 + E1 * NT], ones[:, :], flat, start=True, stop=True).then_inc(sort_p, 1)

            pe.wait_ge(w_split, 1)
            project_v(0, 0)
            pe.wait_ge(w_split, 3)
            project_q(0, 0)
            project_k(0, 0)
            pe.wait_ge(pick_v, 2)
            for k in range(KC):
                pe.matmul(ps[:, PS0, k * E2:(k + 1) * E2], gatew[:, k * P:(k + 1) * P], pick[:, :], start=True, stop=True)
            pe.matmul(ps[:, PS0, KC * E2:(KC + 1) * E2], ones[:, :], pick[:, :], start=True, stop=True).then_inc(sort_p, 1)
            pe.wait_ge(pick_v, 4)
            pe.wait_ge(sort_v, 5)
            pe.wait_ge(attn_in, 16)
            pe.wait_ge(late_in, 48)
            tiles_of_a(pe, a_tile)
            turn_o(NB - 1, CH - 1)
            project_o(NB - 1, CH - 1, NT - 1, 3 * NB)

            BT, BS, BH, BY, BX, BL = 0, 1, 3, 4, 6, 7

            def expert_of(j):
                return pe.value_load(eid_i[0:1, bass.ds(j, 1)], min_val=0, max_val=E1 - 1)

            def expert_part(w, e):
                return w[:, bass.ds(e, 1), :, :].rearrange("p a k n -> p (a k) n")

            def turn_x(p, k, place):
                pe.wait_ge(x1_got[p], 16 * (k + 1))
                at_least(pe, xg1_copied, 2 * k + p)
                for q in range(KC):
                    m = pe.transpose(ps[:, BT, q * P:(q + 1) * P], x1g[:, place, q * P:(q + 1) * P], eye[:, :])
                m.then_inc(xg1_turned, 1)

            def up(j, p, k):
                e = expert_of(j)
                pe.wait_ge(x_high, NT + 2 * k + p + 1)
                at_least(pe, h1_made, 2 * (2 * k + p))
                for half in range(2):
                    cols = slice(half * HALF_D, (half + 1) * HALF_D)
                    three_passes(ps[:, BS + half, 0:HALF_D], x_hi, x_lo, expert_part(w_hi, e)[:, :, cols], expert_part(w_lo, e)[:, :, cols],
                                 (xg1_copied, 2 * k + p + 1)).then_inc(s_made, 1)

            def turn_h(p, k, half):
                pe.wait_ge(h1_made, 2 * (2 * k + p) + half + 1)
                at_least(pe, h1_copied, 2 * k + p)
                for q in range(half * KC // 2, (half + 1) * KC // 2):
                    m = pe.transpose(ps[:, BH, q * P:(q + 1) * P], h1[:, q * P:(q + 1) * P], eye[:, :])
                if half:
                    m.then_inc(h1_turned, 1)

            def turn_x2(p, k, place):
                pe.wait_ge(x2_made, 2 * k + p + 1)
                at_least(pe, x2T_copied, 2 * k + p)
                for q in range(KC):
                    m = pe.transpose(ps[:, BX, q * P:(q + 1) * P], x2o[:, place, q * P:(q + 1) * P], eye[:, :])
                m.then_inc(x2_turned, 1)

            def route(p, k):
                pe.wait_ge(x2T_copied, 2 * k + p + 1)
                at_least(pe, routed, 2 * k + p)
                for q in range(KC):
                    m = pe.matmul(ps[:, BL, 0:E2], x2T[:, q, :], router[:, q, :], start=(q == 0), stop=(q == KC - 1))
                m.then_inc(lg_made, 1)

            def b_tile(j, p, k, left, place):
                if is_later(j):
                    route(p, k - 1)
                turn_h(p, k, 0)
                e = expert_of(j)
                if left:
                    turn_x(*after_it(p, k), (place + 1) % 4)
                turn_h(p, k, 1)
                if not is_first(j):
                    turn_x2(*before_it(p, k), (place - 1) % 4)
                pe.wait_ge(o_high, NT + 2 * k + p + 1)
                at_least(pe, r2_made, 2 * k + p)
                three_passes(ps[:, BY, :], o_hi, o_lo, expert_part(w_hi, e), expert_part(w_lo, e),
                             (h1_copied, 2 * k + p + 1)).then_inc(y1_made, 1)
                if left:
                    up(j + 1, *after_it(p, k))

            pe.wait_ge(r1_made, NT)
            pe.wait_ge(o_gated, NT)
            pe.wait_ge(slot_sorted, 1)
            pe.wait_ge(w_split, 4 + E1)
            turn_x(0, 0, 0)
            up(0, 0, 0)
            slot_tiles(pe, b_tile)
            route((SLOT_T - 2) % 2, (SLOT_T - 2) // 2)
            turn_x2((SLOT_T - 1) % 2, (SLOT_T - 1) // 2, (SLOT_T - 1) % 4)
            route((SLOT_T - 1) % 2, (SLOT_T - 1) // 2)

            pe.wait_ge(tab_v, 2)
            pe.wait_ge(c_half, 2)
            for half in range(2):
                js = slice(half * NT // 2, (half + 1) * NT // 2)
                out = ps[:, half, 0:NT // 2 * E2]
                pe.matmul(out, before_b[:, :], sel[:, js, :].rearrange("p j n -> p (j n)"), start=True, stop=False)
                pe.matmul(out, ones_b[:, :], sel_so_far[:, :, js].rearrange("p n j -> p j n"),
                          start=False, stop=True).then_inc(pos_made, 1)

            def table(g):
                pe.wait_ge(hot_made, g + 1)
                at_least(pe, tab_masked, g)
                for j in range(NT):
                    m = pe.matmul(ps[0:GE * NA, 6, 0:GE * NBB], hot_id[:, j].rearrange("p n a -> p (n a)"),
                                  hot_b[:, j].rearrange("p n b -> p (n b)"), start=(j == 0), stop=(j == NT - 1))
                m.then_inc(tab_made, 1)

            def between(g, m):
                if m == 1:
                    table(g + 1)

            table(0)
            pe.wait_ge(tstep, 11)

            CT, CG, CY = 0, 2, 4

            def c_turn(p, k):
                pe.wait_ge(got[p], 32 * (k + 1))
                at_least(pe, c_copied, 2 * (2 * k + p))
                for q in range(KC):
                    for h in range(2):
                        o = (q % 2) * CAP + h * HALF
                        m = pe.transpose(ps[:, CT + q // 2, o:o + HALF], xg[:, p, h, q * P:(q + 1) * P], eye[0:HALF, 0:HALF])
                m.then_inc(c_turned[p], 1)

            def c_up(p, k):
                pe.wait_ge(gu_in[p], 16 * (k + 1))
                pe.wait_ge(c_copied, 2 * (2 * k + p + 1))
                at_least(pe, h_made, 2 * (2 * k + p))
                for part in range(3):
                    out = ps[:, CG, part * CAP:(part + 1) * CAP] if part < 2 else ps[:, CG + 1, 0:CAP]
                    for q in range(KC):
                        m = pe.matmul(out, wgu[p][:, q, part * P:(part + 1) * P], xgT[:, p, q, :], start=(q == 0), stop=(q == KC - 1))
                m.then_inc(gu_made[p], 1)

            def c_down(p, k):
                pe.wait_ge(dn_split[p], k + 1)
                pe.wait_ge(h_split, 2 * k + p + 1)
                at_least(pe, y_scaled[1 - p], 2 * (k + p))
                for h in range(2):
                    cols = slice(h * HALF, (h + 1) * HALF)
                    parts = [(ha_hi[:, p, cols], wdn_hi[p][:, 0, :]), (ha_hi[:, p, cols], wdn_lo[p][:, 0, :]),
                             (ha_lo[:, p, cols], wdn_hi[p][:, 0, :]), (hc[:, p, cols], wdn_hi[p][:, 1, :]),
                             (hc[0:P // 2, p, cols], wdn_lo[p][0:P // 2, 1, :])]
                    for i, (lhs, rhs) in enumerate(parts):
                        m = pe.matmul(ps[0:HALF, CY + h, :], lhs, rhs, start=(i == 0), stop=(i == len(parts) - 1))
                m.then_inc(dn_made[p], 1)

            def c_expert(n, p, k, left):
                first, last = is_first(n), left == 0
                c_up(p, k)
                if not last:
                    c_turn(1 - p, k + p)
                if not first:
                    c_down(1 - p, k - (1 - p))

            c_turn(0, 0)
            experts(pe, c_expert, between)
            c_down(1, E2 // 2 - 1)

        @block.scalar
        def _(act):
            def copy_v(b, c):
                t = 4 * b + c
                act.wait_ge(v_made, t + 1)
                if not (isinstance(t, int) and t < 2):
                    act.wait_ge(o_made, t - 1)
                act.activation(v[:, c % 2, :], ps[:, PV, :], ACT.Copy).then_inc(v_copied, 1)

            def sigmoids(b, c, which):
                t = 4 * b + c
                bank, buf, made, done, free = ((PQ, q_act, q_made, q_sig, q_rotated), (PK, k_act, k_made, k_sig, k_rotated))[which]
                act.wait_ge(made, t + 1)
                at_least(act, free, t)
                act.activation(buf[:, :], ps[:, bank, :], ACT.Sigmoid).then_inc(done, 1)

            def a_tile(b, c, first, last):
                t = 4 * b + c
                bn, cn = next_of(b, c)
                act.wait_ge(q_turned, t + 1)
                for j in range(HG):
                    rows = slice(j * HD, (j + 1) * HD)
                    m = act.activation(q_blocks[rows, :, j, :], ps[rows, PT, :].rearrange("p (g t) -> p g t", g=G), ACT.Copy)
                m.then_inc(qT_copied, 1)
                if not last:
                    copy_v(bn, cn)
                act.wait_ge(g1_made, t + 1)
                act.activation(g1T[:, :], ps[0:RANK, PM, 0:P], ACT.Copy).then_inc(g1_copied, 1)
                act.wait_ge(k_turned, t + 1)
                act.activation(whole(kT), ps[:, PT, :].rearrange("p (g t) -> p g t", g=G), ACT.Copy).then_inc(kT_copied, 1)
                act.wait_ge(gate_made, t + 1)
                at_least(act, o_gated, t)
                act.activation(sig_gate[:, :], ps[:, PM, :], ACT.Sigmoid).then_inc(gate_sig, 1)
                if not last:
                    sigmoids(bn, cn, 0)
                if not first:
                    act.wait_ge(o_turned, t)
                    at_least(act, wo_made, t - 1)
                    act.activation(whole(o_hi), ps[:, PT, :].rearrange("p (k t) -> p k t", k=KC), ACT.Copy).then_inc(o_high, 1)
                if not last:
                    sigmoids(bn, cn, 1)
                if split_ahead(b, c):
                    high_x(*next_of(bn, cn))
                if last:
                    act.wait_ge(ctx_in, 16)
                    act.wait_ge(k_made, NT)
                    for e in range(E1 - 1):
                        high_ctx(e)
                act.wait_ge(o_gated, t + 1)
                act.activation(squares[:, :], gated[:, :], ACT.Square).then_inc(squared, 1)

            def high_x(b, c):
                t = 4 * b + c
                act.wait_ge(xT_in[c % 2], 16 * (2 * b + c // 2 + 1))
                at_least(act, k_made, t)
                act.activation(whole(x_hi), xT[:, c % 2], ACT.Copy).then_inc(x_high, 1)

            def high_w(n):
                act.activation(w_hi[:, n], raw[:, n], ACT.Copy).then_inc(w_high, 1)

            def high_ctx(e):
                act.activation(w_hi[:, e], raw[:, e], ACT.Copy).then_inc(w_high, 1)

            act.wait_ge(setup, 2)
            act.activation(warm[:, :], minus_half[:, :], ACT.Sigmoid)
            high_x(0, 0)
            act.wait_ge(wv_in, 16)
            high_w(2)
            act.wait_ge(wqk_in, 32)
            high_w(0)
            high_w(1)
            copy_v(0, 0)
            sigmoids(0, 0, 0)
            sigmoids(0, 0, 1)
            high_x(0, 1)
            act.wait_ge(wo_scaled, 1)
            high_w(3)
            act.wait_ge(zeroed, 2)
            tiles_of_a(act, a_tile)
            act.wait_ge(o_turned, NT)
            act.wait_ge(wo_made, NT - 1)
            act.activation(whole(o_hi), ps[:, PT, :].rearrange("p (k t) -> p k t", k=KC), ACT.Copy).then_inc(o_high, 1)
            act.wait_ge(wo_made, NT)
            high_ctx(E1 - 1)

            BT, BS, BH, BX = 0, 1, 3, 6

            def high_x1(p, k):
                act.wait_ge(xg1_turned, 2 * k + p + 1)
                at_least(act, s_made, 2 * (2 * k + p))
                act.activation(whole(x_hi).rearrange("p k t -> p (k t)"), ps[:, BT, :], ACT.Copy).then_inc(x_high, 1)

            def front(p, k):
                at_least(act, s_silu, 2 * (2 * k + p))
                for half in range(2):
                    cols = slice(half * HALF_D, (half + 1) * HALF_D)
                    act.wait_ge(s_made, 2 * (2 * k + p) + half + 1)
                    act.activation(sig_s[:, cols], ps[:, BS + half, 0:HALF_D], ACT.Sigmoid).then_inc(s_sig, 1)

            def copy_x2(p, k):
                act.wait_ge(x2_turned, 2 * k + p + 1)
                act.activation(whole(x2T).rearrange("p k t -> p (k t)"), ps[:, BX, :], ACT.Copy).then_inc(x2T_copied, 1)

            def exps(p, k):
                act.wait_ge(router_v, 4 * (2 * k + p) + 4)
                act.activation(es[:, :], logits[:, :], ACT.Sigmoid, bias=neg_max[:, 0:1]).then_inc(es_made, 1)

            def b_tile(j, p, k, left, place):
                act.wait_ge(h1_turned, 2 * k + p + 1)
                at_least(act, y1_made, 2 * k + p)
                act.activation(whole(o_hi).rearrange("p k t -> p (k t)"), ps[:, BH, :], ACT.Copy).then_inc(o_high, 1)
                if left:
                    high_x1(*after_it(p, k))
                if is_later(j):
                    exps(p, k - 1)
                if not is_first(j):
                    copy_x2(*before_it(p, k))
                if left:
                    front(*after_it(p, k))

            high_x1(0, 0)
            front(0, 0)
            slot_tiles(act, b_tile)
            exps((SLOT_T - 2) % 2, (SLOT_T - 2) // 2)
            copy_x2((SLOT_T - 1) % 2, (SLOT_T - 1) // 2)
            exps((SLOT_T - 1) % 2, (SLOT_T - 1) // 2)

            CT, CG, CY = 0, 2, 4

            def copy_x(p, k):
                act.wait_ge(c_turned[p], k + 1)
                act.activation(xgT[:, p, 0:2, :], ps[:, CT, 0:2 * CAP].rearrange("p (q s) -> p q s", q=2), ACT.Copy)\
                   .then_inc(c_copied, 1)

            def scale_y(p, k):
                act.wait_ge(dn_made[p], k + 1)
                act.wait_ge(w_copied[p], k + 1)
                at_least(act, y_added[p], 32 * k)
                act.activation(ye[:, p, 0, :], ps[0:HALF, CY, :], ACT.Copy, scale=w_col[:, p, 0:1]).then_inc(y_scaled[p], 1)

            def c_expert(n, p, k, left):
                first, last = is_first(n), left == 0
                act.wait_ge(gu_made[p], k + 1)
                at_least(act, h_made, 2 * (2 * k + p))
                act.activation(sig_a[:, :], ps[:, CG, 0:CAP], ACT.Sigmoid)
                act.activation(sig_c[0:P // 2, :], ps[0:P // 2, CG + 1, 0:CAP], ACT.Sigmoid).then_inc(c_sig, 1)
                if not last:
                    copy_x(1 - p, k + p)
                if not first:
                    scale_y(1 - p, k - (1 - p))
                act.wait_ge(dn_in[p], 32 * (k + 1))
                at_least(act, dn_made[p], k)
                act.activation(wdn_hi[p][:, 0, :], wdn[p][:, 0, :], ACT.Copy)
                act.activation(wdn_hi[p][0:P // 2, 1, :], wdn[p][P // 2:P, 1, :], ACT.Copy)
                act.activation(wdn_hi[p][P // 2:P, 1, :], wdn[p][P // 2:P, 1, :], ACT.Copy).then_inc(dn_high, 1)
                act.wait_ge(h_made, 2 * (2 * k + p + 1))
                act.activation(ha_hi[:, p, :], h_a[:, p, :], ACT.Copy)
                act.activation(hc[0:P // 2, p, :], h_c[P // 2:P, p, :], ACT.Copy)
                act.activation(hc_hi[P // 2:P, p, :], h_c[P // 2:P, p, :], ACT.Copy).then_inc(h_high, 1)

            copy_x(0, 0)
            experts(act, c_expert)
            scale_y(1, E2 // 2 - 1)

            for q in range(4):
                act.wait_ge(shift_made, 2 * q + 2)
                for j in range(4 * q, 4 * q + 4):
                    m = act.activation(y_all[:, j, :], y_all[:, j, :], ACT.Identity, bias=shift3[:, j:j + 1], scale=rstd3[:, j:j + 1])
                    if j % 2:
                        m.then_inc(out_made, 1)
                        act.wait_ge(out_made, (j + 1) // 2)
                        act.dma_start(d["out"][(j - 1) * P:(j + 1) * P, :].rearrange("(j p) n -> p j n", p=P), y_all[:, j - 1:j + 1, :])\
                           .then_inc(out_kept, 16)
            act.wait_ge(out_kept, 16 * NT // 2)

        @block.vector
        def _(dve):
            dve.memset(ones[:, :], 1.0).then_inc(setup, 1)
            dve.memset(zero[:, :], 0.0).then_inc(zeroed, 1)
            dve.wait_ge(sort_in, 32)
            dve.tensor_copy(tok_f[:, :], tok_i[:, :]).then_inc(sort_v, 1)
            dve.wait_ge(sort_v, 1)
            for e in range(E1 - 1):
                m = dve.tensor_scalar(ge[:, e, :], tok_f[:, :], float(PER * (e + 1)), None, ALU.is_ge)
            m.then_inc(sort_v, 1)
            dve.wait_ge(sort_v, 2)
            dve.tensor_scalar(onehot[:, 0, :], ge[:, 0, :], -1.0, 1.0, ALU.mult, ALU.add)
            dve.tensor_tensor(onehot[:, 1:E1 - 1, :], ge[:, 0:E1 - 2, :], ge[:, 1:E1 - 1, :], ALU.subtract)
            dve.tensor_copy(onehot[:, E1 - 1, :], ge[:, E1 - 2, :]).then_inc(sort_v, 1)
            dve.wait_ge(sort_p, 1)
            dve.tensor_copy(whole(total).rearrange("p e j -> p (e j)"), ps[:, PO, 64:64 + E1 * NT]).then_inc(sort_v, 1)
            dve.tensor_copy(whole(rank).rearrange("p e j -> p (e j)"), ps[:, PO, 0:E1 * NT]).then_inc(sort_v, 1)
            dve.wait_ge(sort_v, 5)
            for e in range(E1):
                m = dve.tensor_tensor_scan(cum[:, e, :], ones[:, 0:NT], total[:, e, :], 0.0, ALU.mult, ALU.add)
            m.then_inc(sort_v, 1)
            dve.wait_ge(sort_v, 6)
            for e in range(E1):
                m = dve.tensor_scalar(lot[:, e, :], tile_no[:, 0:NT], float(P), cum[:, e, NT - 1:NT], ALU.mult, ALU.is_lt)
            m.then_inc(sort_v, 1)
            dve.tensor_tensor(whole(rank), whole(rank), whole(cum), ALU.add).then_inc(sort_v, 1)
            dve.wait_ge(sort_v, 8)
            dve.tensor_reduce(tiles[:, :], whole(lot), AX.X, ALU.add).then_inc(sort_v, 1)
            dve.tensor_tensor(whole(rank), whole(rank), whole(total), ALU.subtract).then_inc(sort_v, 1)
            dve.wait_ge(sort_v, 10)
            dve.tensor_tensor_scan(tiles_cum[:, :], ones[:, 0:E1], tiles[:, :], 0.0, ALU.mult, ALU.add).then_inc(sort_v, 1)
            dve.wait_ge(sort_v, 11)
            dve.tensor_tensor(start[:, :], tiles_cum[:, :], tiles[:, :], ALU.subtract).then_inc(sort_v, 1)
            dve.tensor_scalar(eid_f[:, :], tile_no[:, :], tiles_cum[:, 0:1], None, ALU.is_ge).then_inc(sort_v, 1)
            dve.wait_ge(sort_v, 13)
            dve.tensor_scalar(start[:, :], start[:, :], float(P), None, ALU.mult).then_inc(sort_v, 1)
            for e in range(1, E1 - 1):
                dve.wait_ge(sort_v, 13 + (e > 1))
                dve.scalar_tensor_tensor(eid_f[:, :], tile_no[:, :], tiles_cum[:, e:e + 1], eid_f[:, :], ALU.is_ge, ALU.add)\
                   .then_inc(sort_v, 1)
                dve.wait_ge(sort_v, 14 + e)
            dve.tensor_copy(eid_i[:, :], eid_f[:, :]).then_inc(slot_sorted, 1)
            for e in range(E1):
                m = dve.scalar_tensor_tensor(rank[:, e, :], rank[:, e, :], start[:, e:e + 1], onehot[:, e, :], ALU.add, ALU.mult)
            m.then_inc(sort_v, 1)
            dve.wait_ge(sort_v, 17)
            dve.tensor_reduce(dest[:, :], whole(rank).rearrange("p e j -> p j e"), AX.X, ALU.add).then_inc(sort_v, 1)
            dve.wait_ge(sort_v, 18)
            dve.tensor_copy(slot_i[:, :], dest[:, :]).then_inc(sort_v, 1)
            dve.wait_ge(sort_v, 19)
            dve.tensor_single_scalar(row_i[:, :], slot_i[:, :], P - 1, ALU.bitwise_and)
            dve.tensor_single_scalar(slot_i[:, :], slot_i[:, :], 7, ALU.arith_shift_right).then_inc(sort_v, 1)
            dve.wait_ge(sort_v, 20)
            dve.scalar_tensor_tensor(dest_i[:, :], row_i[:, :], float(SLOT_T), slot_i[:, :], ALU.mult, ALU.add).then_inc(sort_v, 1)
            dve.tensor_copy(ids_i[:, :], ids[:, :]).then_inc(sort_v, 1)

            def pick_rows():
                dve.wait_ge(gate_in, 32)
                dve.tensor_copy(o2n_f[:, :], o2n_i[:, :]).then_inc(pick_v, 1)
                dve.wait_ge(pick_v, 1)
                dve.tensor_scalar(pick[:, :], n_iota[:, :], o2n_f[:, 0:1], None, ALU.is_equal).then_inc(pick_v, 1)

            def keep_router():
                dve.wait_ge(sort_p, 2)
                dve.tensor_copy(whole(router).rearrange("p k n -> p (k n)"), ps[:, PS0, 0:KC * E2]).then_inc(pick_v, 1)
                dve.tensor_scalar(kept_bias[:, :], ps[:, PS0, KC * E2:(KC + 1) * E2], -1.0, -NEG, ALU.add, ALU.mult).then_inc(pick_v, 1)

            def silu(b, c, which):
                t = 4 * b + c
                bank, x, r2_, sig, done, second, rotated = (
                    (PQ, q_act, rot2_q, q_sig, q_silu, q_r2, q_rotated),
                    (PK, k_act, rot2_k, k_sig, k_silu, k_r2, k_rotated))[which]
                dve.wait_ge(sig, t + 1)
                at_least(dve, rotated, t)
                dve.tensor_tensor(x[:, :], ps[:, bank, :], x[:, :], ALU.mult).then_inc(done, 1)
                dve.wait_ge(done, t + 1)
                xv = x[:, :].rearrange("p (h a i) -> p h a i", a=2, i=HD // 2)
                rv = r2_[:, :].rearrange("p (h a i) -> p h a i", a=2, i=HD // 2)
                for a in range(2):
                    s = sin[:, c, a * HD // 2:(a + 1) * HD // 2].unsqueeze(1).to_broadcast([P, H, HD // 2])
                    m = dve.tensor_tensor(rv[:, :, a, :], xv[:, :, 1 - a, :], s, ALU.mult)
                m.then_inc(second, 1)

            def rotated_sum(b, c, which):
                t = 4 * b + c
                r1_, r2_, out, one, two, done, turned = (
                    (rot1_q, rot2_q, q_rot, q_r1, q_r2, q_rotated, q_turned),
                    (rot1_k, rot2_k, k_rot, k_r1, k_r2, k_rotated, k_turned))[which]
                dve.wait_ge(one, t + 1)
                dve.wait_ge(two, t + 1)
                at_least(dve, turned, t)
                if which:
                    at_least(dve, k_decayed, 3 * b + c)
                dve.tensor_tensor(out[:, :], r1_[:, :], r2_[:, :], ALU.add).then_inc(done, 1)

            def norm_o(b, c):
                t = 4 * b + c
                dve.wait_ge(rms_made, t + 1)
                at_least(dve, o_turned, t)
                dve.tensor_tensor(normed[:, :].rearrange("p (h i) -> p h i", h=H), gated[:, :].rearrange("p (h i) -> p h i", h=H),
                                  rms_inv[:, :].unsqueeze(2).to_broadcast([P, H, HD]), ALU.mult).then_inc(o_normed, 1)

            def copy_o(b, c):
                t = 4 * b + c
                dve.wait_ge(o_high, t + 1)
                dve.tensor_tensor(whole(o_lo), ps[:, PT, :].rearrange("p (k t) -> p k t", k=KC), whole(o_hi).bitcast(F32),
                                  ALU.subtract).then_inc(oT_copied, 1)

            def layer_norm1(b, c):
                t = 4 * b + c
                dve.wait_ge(wo_made, t + 1)
                dve.wait_ge(x_in[c % 2], 16 * (2 * b + c // 2 + 1))
                at_least(dve, x1_made, t)
                dve.tensor_tensor(r1[:, :], ps[:, PM, :], x_res[:, c % 2, :], ALU.add).then_inc(r1_made, 1)
                dve.wait_ge(r1_made, t + 1)
                dve.bn_stats(stat1[:, :], r1[:, :]).then_inc(stat_made, 1)
                dve.wait_ge(stat_made, t + 1)
                at_least(dve, rstd_made, t)
                settle(dve)
                dve.bn_aggr(mv1[:, :], stat1[:, :]).then_inc(mv_made, 1)

            def finish_x1(b, c):
                t = 4 * b + c
                dve.wait_ge(rstd_made, t + 1)
                dve.wait_ge(x1_kept[c % 2], 16 * (2 * b + c // 2 + 1))
                dve.tensor_scalar(x1o[:, c % 2, :], r1[:, :], mv1[:, 0:1], rstd1[:, 0:1], ALU.subtract, ALU.mult).then_inc(x1_made, 1)

            def a_tile(b, c, first, last):
                t = 4 * b + c
                bn, cn = next_of(b, c)
                dve.wait_ge(qT_copied, t + 1)
                dve.tensor_tensor(whole(q_decT), ps[:, PT, :].rearrange("p (g t) -> p g t", g=G), dq, ALU.mult)\
                   .then_inc(qT_decayed, 1)
                if not (isinstance(t, int) and t < 2):
                    finish_x1(*last_of(*last_of(b, c)))
                if not first:
                    norm_o(*last_of(b, c))
                for g in range(G):
                    dve.wait_ge(scored, 4 * t + g + 1)
                    dve.tensor_tensor(weighted[:, g * HG:(g + 1) * HG, :], ps[:, PS0 + g % 2, :].rearrange("p (h t) -> p h t", h=HG),
                                      decay[:, g * HG:(g + 1) * HG, :], ALU.mult).then_inc(masked, 1)
                if not first:
                    copy_o(*last_of(b, c))
                if c < CH - 1:
                    n = 3 * b + c
                    dve.wait_ge(add_made, n + 1)
                    at_least(dve, st_new, n)
                    dve.tensor_tensor(whole(state_add), ps[:, PM, :].rearrange("p (g t) -> p g t", g=G),
                                      block_diag[:, :].unsqueeze(1).to_broadcast([P, G, P]), ALU.mult).then_inc(add_cut, 1)
                    dve.wait_ge(add_cut, n + 1)
                    at_least(dve, o_made, t)
                    if c:
                        dve.wait_ge(st_decayed, 2 * b + c)
                        dve.tensor_tensor(state[:, c % 2], whole(state_add), whole(state_dec), ALU.add).then_inc(st_new, 1)
                    else:
                        dve.tensor_copy(state[:, c % 2], whole(state_add)).then_inc(st_new, 1)
                if not last:
                    silu(bn, cn, 0)
                if first:
                    dve.wait_ge(w_high, 4)
                    low_part(3).then_inc(w_split, 1)
                if not last:
                    rotated_sum(bn, cn, 0)
                if not last:
                    silu(bn, cn, 1)
                    rotated_sum(bn, cn, 1)
                if split_ahead(b, c):
                    low_x(*next_of(bn, cn))
                if last:
                    for e in range(E1 - 1):
                        low_ctx(e)
                dve.wait_ge(o_made, t + 1)
                dve.wait_ge(gate_sig, t + 1)
                at_least(dve, o_normed, t)
                dve.tensor_tensor(gated[:, :], ps[:, PO, :], sig_gate[:, :], ALU.mult).then_inc(o_gated, 1)
                if not first:
                    layer_norm1(*last_of(b, c))
                dve.wait_ge(squared, t + 1)
                at_least(dve, rms_made, t)
                dve.tensor_reduce(ms[:, :], squares[:, :].rearrange("p (h i) -> p h i", h=H), AX.X, ALU.add).then_inc(ms_made, 1)

            def low_x(b, c):
                t = 4 * b + c
                dve.wait_ge(x_high, t + 1)
                dve.tensor_tensor(whole(x_lo), xT[:, c % 2], whole(x_hi).bitcast(F32), ALU.subtract).then_inc(x_split, 1)

            def low_part(n):
                return dve.tensor_tensor(w_lo[:, n], raw[:, n], w_hi[:, n].bitcast(F32), ALU.subtract)

            def low_ctx(e):
                dve.wait_ge(w_high, 4 + e + 1)
                low_part(e).then_inc(w_split, 1)

            low_x(0, 0)
            for i, n in enumerate((2, 0, 1)):
                dve.wait_ge(w_high, i + 1)
                low_part(n).then_inc(w_split, 1)
            pick_rows()
            dve.wait_ge(attn_in, 16)
            silu(0, 0, 0)
            rotated_sum(0, 0, 0)
            silu(0, 0, 1)
            rotated_sum(0, 0, 1)
            keep_router()
            low_x(0, 1)
            dve.wait_ge(late_in, 48)
            tiles_of_a(dve, a_tile)
            norm_o(NB - 1, CH - 1)
            copy_o(NB - 1, CH - 1)
            finish_x1(NB - 1, CH - 2)
            layer_norm1(NB - 1, CH - 1)
            finish_x1(NB - 1, CH - 1)
            low_ctx(E1 - 1)

            BT, BS, BH, BY, BL = 0, 1, 3, 4, 7

            def hidden(p, k, half):
                n = 2 * (2 * k + p) + half
                cols = slice(half * HALF_D, (half + 1) * HALF_D)
                dve.wait_ge(s_sig, n + 1)
                dve.tensor_tensor(s_act[:, cols], ps[:, BS + half, 0:HALF_D], sig_s[:, cols], ALU.mult).then_inc(s_silu, 1)
                dve.wait_ge(s_silu, n + 1)
                at_least(dve, h1_turned, 2 * k + p)
                dve.tensor_tensor(h1[:, cols], ps[:, BS + half, 0:HALF_D], s_act[:, cols], ALU.mult).then_inc(h1_made, 1)

            def route(p, k):
                j = 2 * k + p
                v0 = 4 * j
                dve.wait_ge(lg_made, 2 * k + p + 1)
                dve.tensor_tensor(logits[:, :], ps[:, BL, 0:E2], kept_bias[:, :], ALU.add).then_inc(router_v, 1)
                dve.wait_ge(router_v, v0 + 1)
                settle(dve)
                dve.max(top8[:, :], logits[:, :]).then_inc(router_v, 1)
                dve.wait_ge(router_v, v0 + 2)
                settle(dve)
                dve.match_replace(marked[:, :], top8[:, :], logits[:, :], TAKEN).then_inc(router_v, 1)
                dve.tensor_scalar(neg_max[:, :], top8[:, 0:1], -1.0, None, ALU.mult).then_inc(router_v, 1)

            def low_h(p, k):
                dve.wait_ge(o_high, NT + 2 * k + p + 1)
                dve.tensor_tensor(whole(o_lo).rearrange("p k t -> p (k t)"), ps[:, BH, :],
                                  whole(o_hi).bitcast(F32).rearrange("p k t -> p (k t)"), ALU.subtract).then_inc(h1_copied, 1)

            def low_x1(p, k):
                dve.wait_ge(x_high, NT + 2 * k + p + 1)
                dve.tensor_tensor(whole(x_lo).rearrange("p k t -> p (k t)"), ps[:, BT, :],
                                  whole(x_hi).bitcast(F32).rearrange("p k t -> p (k t)"), ALU.subtract).then_inc(xg1_copied, 1)

            def route_weights(p, k, place):
                j = 2 * k + p
                v0 = 4 * j
                dve.wait_ge(router_v, v0 + 4)
                dve.tensor_scalar(not_chosen[:, :], marked[:, :], TAKEN / 2, -1.0, ALU.is_le, ALU.add).then_inc(rstep, 1)
                dve.wait_ge(es_made, 2 * k + p + 1)
                r0 = 5 * j
                dve.tensor_scalar(es1[:, :], es[:, :], -1.0, 1.0, ALU.mult, ALU.add).then_inc(rstep, 1)
                dve.wait_ge(rstep, r0 + 2)
                dve.reciprocal(es_inv[:, :], es1[:, :]).then_inc(rstep, 1)
                dve.wait_ge(rstep, r0 + 3)
                dve.tensor_tensor(expo[:, :], es[:, :], es_inv[:, :], ALU.mult).then_inc(rstep, 1)
                dve.wait_ge(rstep, r0 + 4)
                dve.scalar_tensor_tensor(chosen[:, :], marked[:, :], TAKEN / 2, expo[:, :], ALU.is_le, ALU.mult,
                                         accum_out=w_sum[:, :]).then_inc(rstep, 1)
                dve.wait_ge(rstep, r0 + 5)
                dve.reciprocal(w_inv[:, :], w_sum[:, :]).then_inc(w_inverted, 1)
                dve.wait_ge(w_inverted, j + 1)
                dve.scalar_tensor_tensor(x2o[:, place, D:ROW], chosen[:, :], w_inv[:, 0:1], not_chosen[:, :], ALU.mult, ALU.add)\
                   .then_inc(routed, 1)

            def b_tile(j, p, k, left, place):
                if is_later(j):
                    route(p, k - 1)
                low_h(p, k)
                if left:
                    low_x1(*after_it(p, k))
                if is_later(j):
                    route_weights(p, k - 1, (place - 2) % 4)
                dve.wait_ge(y1_made, 2 * k + p + 1)
                at_least(dve, x2_made, 2 * k + p)
                dve.tensor_tensor(r2[:, :], ps[:, BY, :], x1g[:, place, :], ALU.add).then_inc(r2_made, 1)
                dve.wait_ge(r2_made, 2 * k + p + 1)
                dve.bn_stats(stat2[:, :], r2[:, :]).then_inc(stat_made, 1)
                dve.wait_ge(stat_made, NT + 2 * k + p + 1)
                settle(dve)
                dve.bn_aggr(mv2[:, :], stat2[:, :]).then_inc(mv_made, 1)
                if left:
                    hidden(*after_it(p, k), 0)
                    hidden(*after_it(p, k), 1)
                dve.wait_ge(rstd_made, NT + 2 * k + p + 1)
                at_least(dve, x2_kept[p], 16 * (k - 1))
                dve.tensor_scalar(x2o[:, place, 0:D], r2[:, :], mv2[:, 0:1], rstd2[:, 0:1], ALU.subtract, ALU.mult).then_inc(x2_made, 1)

            low_x1(0, 0)
            hidden(0, 0, 0)
            hidden(0, 0, 1)
            slot_tiles(dve, b_tile)
            for j in (SLOT_T - 2, SLOT_T - 1):
                route(j % 2, j // 2)
                route_weights(j % 2, j // 2, j % 4)

            def cut_table(g):
                dve.wait_ge(tab_made, g + 1)
                at_least(dve, tab_step, 2 * g)
                dve.tensor_tensor(whole(tab), ps[0:GE * NA, 6, 0:GE * NBB].rearrange("r (n b) -> r n b", n=GE),
                                  diag8[:, :].unsqueeze(2).to_broadcast([GE * NA, GE, NBB]), ALU.mult).then_inc(tab_masked, 1)
                dve.wait_ge(tab_masked, g + 1)
                at_least(dve, tab_cut, g)
                dve.tensor_reduce(tab_r[:, :], whole(tab).rearrange("r n b -> r b n"), AX.X, ALU.add).then_inc(tab_step, 1)
                dve.wait_ge(tab_step, 2 * g + 1)
                dve.scalar_tensor_tensor(tab_spare[:, :], tab_r[:, :], 0.0, place_no[:, :], ALU.is_equal, ALU.mult).then_inc(tab_step, 1)
                dve.wait_ge(tab_step, 2 * g + 2)
                at_least(dve, places_kept, 16 * g)
                dve.scalar_tensor_tensor(tab_i[:, :], tab_r[:, :], float(TOK), tab_spare[:, :], ALU.add, ALU.add).then_inc(tab_cut, 1)

            dve.memset(before_b[:, :], 0.0).then_inc(c_half, 1)
            dve.wait_ge(c_half, 1)
            dve.tensor_scalar(before_b[:, :], before[:, :], -1.0, None, ALU.add)
            dve.memset(same_expert[:, :, 1:NT], 1.0)
            dve.memset(same_expert[:, :, 0:1], 0.0)
            dve.tensor_copy(ab_h[:, :], ab_iota[:, :])
            dve.tensor_scalar(ids_h[:, :], ids[:, :], -float(TOK), None, ALU.add)
            dve.tensor_copy(ones_b[:, :], ones[:, :]).then_inc(c_half, 1)
            dve.wait_ge(wnat_in, 16)
            dve.tensor_scalar(whole(sel), whole(wnat), 0.0, None, ALU.is_ge)
            dve.tensor_scalar(sel_t[:, :, :], whole(wnat).rearrange("p j n -> p n j"), 0.0, None, ALU.is_ge).then_inc(tab_v, 1)
            dve.wait_ge(tab_v, 1)
            dve.tensor_tensor_scan(sel_so_far[:, :, :].rearrange("p n j -> p (n j)"), same_expert[:, :, :].rearrange("p n j -> p (n j)"),
                                   sel_t[:, :, :].rearrange("p n j -> p (n j)"), 0.0, ALU.mult, ALU.add).then_inc(tab_v, 1)

            def places(ns, done):
                for half in range(2):
                    js = slice(half * NT // 2, (half + 1) * NT // 2)
                    out = ps[:, half, 0:NT // 2 * E2].rearrange("p (j n) -> p j n", n=E2)[:, :, ns]
                    dve.wait_ge(pos_made, half + 1)
                    dve.scalar_tensor_tensor(ok[:, js, ns], out, float(CAP), sel[:, js, ns], ALU.is_lt, ALU.mult).then_inc(tstep, 1)
                    dve.wait_ge(tstep, done + 2 * half + 1)
                    dve.scalar_tensor_tensor(place[:, js, ns], out, 1.0, ok[:, js, ns], ALU.add, ALU.mult).then_inc(tstep, 1)
                dve.wait_ge(tstep, done + 4)
                dve.tensor_scalar(place_i[:, :, ns], place[:, :, ns], -1.0, None, ALU.add).then_inc(tstep, 1)
                dve.wait_ge(tstep, done + 5)
                dve.tensor_single_scalar(a_i[:, :, ns], place_i[:, :, ns], 4, ALU.arith_shift_right)
                dve.tensor_single_scalar(b_i[:, :, ns], place_i[:, :, ns], NBB - 1, ALU.bitwise_and).then_inc(tstep, 1)
                dve.wait_ge(tstep, done + 6)
                dve.tensor_copy(a_h[:, :, ns], a_i[:, :, ns])
                dve.tensor_copy(b_h[:, :, ns], b_i[:, :, ns]).then_inc(tstep, 1)
                dve.wait_ge(tstep, done + 7)

            dve.memset(a_h[:, :, E2:], 0.0)
            dve.memset(b_h[:, :, E2:], 0.0)
            places(slice(0, GE), 0)
            dve.wait_ge(c_half, 2)

            def one_hots_b(g, halves=(0, 1)):
                at_least(dve, tab_made, g)
                for half in halves:
                    js = slice(half * NT // 2, (half + 1) * NT // 2)
                    shape = [P, NT // 2, GE, NBB]
                    dve.tensor_tensor(hot_b[:, js], b_h[:, js, bass.ds(g * GE, GE)].unsqueeze(3).to_broadcast(shape),
                                      ab_h[:, NA:NA + NBB].unsqueeze(1).unsqueeze(1).to_broadcast(shape), ALU.is_equal)

            def one_hots_a(g):
                shape = [P, NT, GE, NA]
                dve.tensor_tensor(whole(hot_a), a_h[:, :, bass.ds(g * GE, GE)].unsqueeze(3).to_broadcast(shape),
                                  ab_h[:, 0:NA].unsqueeze(1).unsqueeze(1).to_broadcast(shape), ALU.is_equal).then_inc(hot_parts, 1)

            def hot_ids(g):
                dve.wait_ge(hot_parts, g + 1)
                dve.tensor_tensor(whole(hot_id).rearrange("p j n a -> p j (n a)"), whole(hot_a).rearrange("p j n a -> p j (n a)"),
                                  ids_h[:, :].unsqueeze(2).to_broadcast([P, NT, GE * NA]), ALU.mult).then_inc(hot_made, 1)

            def between(g, m):
                if m == 0:
                    hot_ids(g + 1)
                if m == 1:
                    cut_table(g + 1)
                if m == 5:
                    one_hots_b(g + 2, (0,))
                if m == 6:
                    one_hots_b(g + 2, (1,))
                if m == 7:
                    one_hots_a(g + 2)

            one_hots_b(0)
            one_hots_a(0)
            hot_ids(0)
            cut_table(0)
            places(slice(GE, E2), 7)
            one_hots_b(1)
            one_hots_a(1)

            CT, CG, CY = 0, 2, 4
            LO, HI = slice(0, P // 2), slice(P // 2, P)

            def copy_x(p, k):
                dve.wait_ge(c_turned[p], k + 1)
                dve.tensor_copy(xgT[:, p, 2:4, :], ps[:, CT + 1, 0:2 * CAP].rearrange("p (q s) -> p q s", q=2))\
                   .then_inc(c_copied, 1)

            def keep_w(n, p, k):
                dve.wait_ge(c_turned[p], k + 1)
                at_least(dve, y_scaled[p], 2 * k)
                dve.tensor_copy(w_col[:, p, :], xg[:, p, :, bass.ds(n + D, 1)].rearrange("p h a -> p (h a)")).then_inc(w_copied[p], 1)

            def scale_y(p, k):
                dve.wait_ge(dn_made[p], k + 1)
                dve.wait_ge(w_copied[p], k + 1)
                at_least(dve, y_added[p], 32 * k)
                dve.tensor_scalar(ye[:, p, 1, :], ps[0:HALF, CY + 1, :], w_col[:, p, 1:2], None, ALU.mult).then_inc(y_scaled[p], 1)

            def c_expert(n, p, k, left):
                first, last = is_first(n), left == 0
                dve.wait_ge(c_sig, 2 * k + p + 1)
                at_least(dve, h_made, 2 * (2 * k + p))
                dve.tensor_tensor(g_a[:, :], ps[:, CG, 0:CAP], sig_a[:, :], ALU.mult).then_inc(g_made, 1)
                dve.tensor_tensor(g_c[HI, :], ps[LO, CG + 1, 0:CAP], sig_c[LO, :], ALU.mult).then_inc(g_made, 1)
                dve.wait_ge(g_made, 2 * (2 * k + p) + 1)
                at_least(dve, dn_made[p], k)
                dve.tensor_tensor(h_a[:, p, :], ps[:, CG, CAP:2 * CAP], g_a[:, :], ALU.mult).then_inc(h_made, 1)
                dve.wait_ge(g_made, 2 * (2 * k + p) + 2)
                dve.tensor_tensor(h_c[HI, p, :], ps[HI, CG + 1, 0:CAP], g_c[HI, :], ALU.mult).then_inc(h_made, 1)
                if not last:
                    copy_x(1 - p, k + p)
                if not first:
                    scale_y(1 - p, k - (1 - p))
                if not last:
                    keep_w(n + 1, 1 - p, k + p)
                dve.wait_ge(dn_high, 2 * k + p + 1)
                dve.tensor_tensor(wdn_lo[p][:, 0, :], wdn[p][:, 0, :], wdn_hi[p][:, 0, :].bitcast(F32), ALU.subtract)
                dve.tensor_tensor(wdn_lo[p][LO, 1, :], wdn[p][HI, 1, :], wdn_hi[p][HI, 1, :].bitcast(F32), ALU.subtract)\
                   .then_inc(dn_split[p], 1)
                dve.wait_ge(h_high, 2 * k + p + 1)
                dve.tensor_tensor(ha_lo[:, p, :], h_a[:, p, :], ha_hi[:, p, :].bitcast(F32), ALU.subtract)
                dve.tensor_tensor(hc[HI, p, :], h_c[HI, p, :], hc_hi[HI, p, :].bitcast(F32), ALU.subtract).then_inc(h_split, 1)

            copy_x(0, 0)
            keep_w(0, 0, 0)
            experts(dve, c_expert, between)
            scale_y(1, E2 // 2 - 1)

            dve.wait_ge(x2_in, 16 * NG)
            for q in range(4):
                js = slice(4 * q, 4 * q + 4)
                dve.wait_ge(y_in[q % 2], 16 * (q // 2 + 1))
                dve.tensor_tensor(y_all[:, 4 * q:4 * q + 3, :], y_all[:, 4 * q:4 * q + 3, :], x2_all[:, 4 * q:4 * q + 3, :], ALU.add).then_inc(r3_made, 1)
                dve.wait_ge(r3_made, q + 1)
                dve.wait_ge(r3_too, q + 1)
                for j in range(4 * q, 4 * q + 4):
                    m = dve.bn_stats(stat3[:, j, :], y_all[:, j, :])
                m.then_inc(stat_made, 1)
                dve.wait_ge(stat_made, NT + SLOT_T + q + 1)
                for j in range(4 * q, 4 * q + 4):
                    m = dve.bn_aggr(mv3[:, j, :], stat3[:, j, :])
                m.then_inc(mv_made, 1)

        @block.gpsimd
        def _(pool):
            pool.memset(minus_half[:, :], -0.5).then_inc(setup, 1)
            pool.memset(whole(q_blocks), 0.0).then_inc(zeroed, 1)

            def cosines(b, c, which):
                t = 4 * b + c
                x, r1_, silu_, one = ((q_act, rot1_q, q_silu, q_r1), (k_act, rot1_k, k_silu, k_r1))[which]
                pool.wait_ge(silu_, t + 1)
                pool.tensor_tensor(r1_[:, :].rearrange("p (h i) -> p h i", h=H), x[:, :].rearrange("p (h i) -> p h i", h=H),
                                   cos[:, c, :].unsqueeze(1).to_broadcast([P, H, HD]), ALU.mult).then_inc(one, 1)

            def decay_k(b, c):
                pool.wait_ge(k_rotated, 4 * b + c + 1)
                at_least(pool, add_made, 3 * b + max(c - 1, 0))
                pool.tensor_tensor(k_dec[:, c % 2, :].rearrange("p (h i) -> p h i", h=H), k_rot[:, :].rearrange("p (h i) -> p h i", h=H),
                                   dk[:, :].unsqueeze(2).to_broadcast([P, H, HD]), ALU.mult).then_inc(k_decayed, 1)

            def rstd1_of(b, c):
                t = 4 * b + c
                pool.wait_ge(mv_made, t + 1)
                settle(pool)
                pool.tensor_scalar(ve1[:, :], mv1[:, 1:2], 1.0, LN_EPS, ALU.mult, ALU.add).then_inc(ve_made, 1)
                pool.wait_ge(ve_made, t + 1)
                at_least(pool, x1_made, t)
                pool.tensor_tensor(rstd1[:, :], ve1[:, :], minus_half[:, 0:1], ALU.pow).then_inc(rstd_made, 1)

            def name_slots(t):
                at_least(pool, slots_named, 16 * t)
                settle(pool)
                pool.tensor_copy(name_to[:, :], dest_i[:, bass.ds(t, 1)])
                pool.tensor_copy(name_of[:, :], ids_i[:, bass.ds(t, 1)]).then_inc(name_set, 1)
                pool.wait_ge(name_set, t + 1)
                settle(pool)
                pool.indirect_dma_start(out=token_of_slot_d, out_offset=bass.IndirectOffsetOnAxis(ap=name_to[:, :], axis=0),
                                        in_=name_of[:, :], in_offset=None).then_inc(slots_named, 16)

            def a_tile(b, c, first, last):
                t = 4 * b + c
                bn, cn = next_of(b, c)
                if 0 < c < CH - 1:
                    pool.wait_ge(st_new, 3 * b + c)
                    pool.tensor_tensor(whole(state_dec), state[:, (c - 1) % 2], lam[:, :].unsqueeze(2).to_broadcast([P, G, P]),
                                       ALU.mult).then_inc(st_decayed, 1)
                if not last:
                    cosines(bn, cn, 0)
                if not last:
                    name_slots(t + 1)
                if not last:
                    cosines(bn, cn, 1)
                    if cn < CH - 1:
                        decay_k(bn, cn)
                if not first:
                    rstd1_of(*last_of(b, c))
                pool.wait_ge(ms_made, t + 1)
                settle(pool)
                pool.tensor_scalar(ms_eps[:, :], ms[:, :], 1.0 / HD, RMS_EPS, ALU.mult, ALU.add).then_inc(ms_plus, 1)
                pool.wait_ge(ms_plus, t + 1)
                at_least(pool, o_normed, t)
                pool.tensor_tensor(rms_inv[:, :], ms_eps[:, :], minus_half[:, :], ALU.pow).then_inc(rms_made, 1)

            pool.wait_ge(attn_in, 16)
            pool.wait_ge(wo_in, 16)
            pool.tensor_tensor(raw[:, 3], raw[:, 3], nw.unsqueeze(2).to_broadcast([P, KC, D]), ALU.mult).then_inc(wo_scaled, 1)
            cosines(0, 0, 0)
            cosines(0, 0, 1)
            decay_k(0, 0)
            pool.wait_ge(sort_v, 22)
            pool.wait_ge(slots_cleared, 16)
            name_slots(0)
            tiles_of_a(pool, a_tile)
            rstd1_of(NB - 1, CH - 1)

            def gather(j, p, k, place):
                at_least(pool, r2_made, 2 * k + p - 3)
                at_least(pool, x1_got[p], 16 * k)
                settle(pool)
                pool.tensor_copy(idx_g[:, p:p + 1], slot_token[:, bass.ds(j, 1)]).then_inc(idx_g_set, 1)
                pool.wait_ge(idx_g_set, 2 * k + p + 1)
                settle(pool)
                pool.indirect_dma_start(out=x1g[:, place, :], out_offset=None, in_=x1_d,
                                        in_offset=bass.IndirectOffsetOnAxis(ap=idx_g[:, p:p + 1].bitcast(U32), axis=0)).then_inc(x1_got[p], 16)

            def scatter(j, p, k, place):
                at_least(pool, x2_kept[p], 16 * k)
                settle(pool)
                pool.tensor_copy(idx_s[:, p:p + 1], slot_token[:, bass.ds(j, 1)]).then_inc(idx_s_set, 1)
                pool.wait_ge(idx_s_set, 2 * k + p + 1)
                pool.wait_ge(routed, 2 * k + p + 1)
                settle(pool)
                pool.indirect_dma_start(out=x2_d, out_offset=bass.IndirectOffsetOnAxis(ap=idx_s[:, p:p + 1].bitcast(U32), axis=0),
                                        in_=x2o[:, place, :], in_offset=None).then_inc(x2_kept[p], 16)

            def b_tile(j, p, k, left, place):
                if left == 2:
                    gather(j + 2, p, k + 1, (place + 2) % 4)
                if is_later(j):
                    scatter(j - 2, p, k - 1, (place - 2) % 4)
                pool.wait_ge(mv_made, NT + 2 * k + p + 1)
                settle(pool)
                pool.tensor_scalar(ve2[:, :], mv2[:, 1:2], 1.0, LN_EPS, ALU.mult, ALU.add).then_inc(ve_made, 1)
                pool.wait_ge(ve_made, NT + 2 * k + p + 1)
                pool.tensor_tensor(rstd2[:, :], ve2[:, :], minus_half[:, 0:1], ALU.pow).then_inc(rstd_made, 1)

            pool.wait_ge(slot_token_in, 16)
            pool.wait_ge(rows_cleared, 3 * 16 * SPARE // P)
            pool.wait_ge(x1_kept[0], 16 * (NT // 2 + 1))
            pool.wait_ge(x1_kept[1], 16 * (NT // 2 + 1))
            gather(0, 0, 0, 0)
            gather(1, 1, 0, 1)
            slot_tiles(pool, b_tile)
            for j in (SLOT_T - 2, SLOT_T - 1):
                scatter(j, j % 2, j // 2, j % 4)

            def c_gather(n, p, k):
                at_least(pool, w_copied[p], k)
                at_least(pool, c_turned[p], k)
                at_least(pool, got[p], 32 * k)
                settle(pool)
                pool.tensor_copy(cidx_g[:, p, :], place_token[:, bass.ds(n, 1), :].rearrange("p a h -> p (a h)")).then_inc(cg_set, 1)
                pool.wait_ge(cg_set, 2 * k + p + 1)
                settle(pool)
                for h in range(2):
                    pool.indirect_dma_start(out=xg[:, p, h, :], out_offset=None, in_=x2_d,
                                            in_offset=bass.IndirectOffsetOnAxis(ap=cidx_g[:, p, h:h + 1].bitcast(U32), axis=0))\
                        .then_inc(got[p], 16)

            def c_scatter(n, p, k):
                at_least(pool, y_added[p], 32 * k)
                settle(pool)
                pool.tensor_copy(cidx_s[:, p, :], place_token[:, bass.ds(n, 1), :].rearrange("p a h -> p (a h)")).then_inc(cs_set, 1)
                pool.wait_ge(cs_set, 2 * k + p + 1)
                pool.wait_ge(y_scaled[p], 2 * (k + 1))
                at_least(pool, y_added[1 - p], 32 * (k + p))
                settle(pool)
                for h in range(2):
                    pool.indirect_dma_start(out=y_d, out_offset=bass.IndirectOffsetOnAxis(ap=cidx_s[:, p, h:h + 1].bitcast(U32), axis=0),
                                            in_=ye[:, p, h, :], in_offset=None, compute_op=ALU.add).then_inc(y_added[p], 16)

            def c_expert(n, p, k, left):
                if left == 2:
                    c_gather(n + 2, p, k + 1)
                if not is_first(n):
                    c_scatter(n - 1, *before_it(p, k))

            def between(g, m):
                if m == 3:
                    pool.wait_ge(place_token_in, 16 * (g + 2))

            pool.wait_ge(place_token_in, 16)
            pool.wait_ge(y_cleared, 16 * NT)
            c_gather(0, 0, 0)
            c_gather(1, 1, 0)
            experts(pool, c_expert, between)
            c_scatter(E2 - 1, 1, E2 // 2 - 1)

            def last_sum(q):
                pool.wait_ge(y_in[q % 2], 16 * (q // 2 + 1))
                pool.tensor_tensor(y_all[:, 4 * q + 3, :], y_all[:, 4 * q + 3, :], x2_all[:, 4 * q + 3, :], ALU.add).then_inc(r3_too, 1)

            pool.wait_ge(x2_in, 16 * NG)
            last_sum(0)
            for q in range(4):
                js = slice(4 * q, 4 * q + 4)
                if q < 3:
                    last_sum(q + 1)
                pool.wait_ge(mv_made, NT + SLOT_T + q + 1)
                pool.tensor_scalar(ve3[:, js], mv3[:, js, 1], 1.0, LN_EPS, ALU.mult, ALU.add).then_inc(ve_made, 1)
                pool.wait_ge(ve_made, NT + SLOT_T + q + 1)
                pool.tensor_tensor(rstd3[:, js], ve3[:, js], minus_half[:, 0:4], ALU.pow).then_inc(rstd_made, 1)
                pool.wait_ge(rstd_made, NT + SLOT_T + q + 1)
                pool.tensor_tensor(shift3[:, js], mv3[:, js, 0], rstd3[:, js], ALU.mult).then_inc(shift_made, 1)
                pool.wait_ge(shift_made, 2 * q + 1)
                pool.tensor_scalar(shift3[:, js], shift3[:, js], -1.0, None, ALU.mult).then_inc(shift_made, 1)


def kernel(**inputs):
    import concourse.bacc as bacc
    from concourse.bass_utils import run_bass_kernel_spmd as run

    a = {k: np.asarray(v) for k, v in inputs.items()}
    x = a["x"].reshape(TOK, D)

    def rows(w):
        return w.reshape(KC, P, -1).transpose(1, 0, 2)

    gu = a["L0_ffn_gate_up_proj"]
    gu = np.concatenate([gu[:, 0:P], gu[:, FI:FI + P], gu[:, P:FI], gu[:, FI + P:]], 1)
    arrays = {
        "x": x,
        "xT": x.reshape(NT, P, KC, P).transpose(0, 3, 2, 1),
        "wqkv": np.stack([rows(a["L0_attn_W" + n]) for n in "qkv"], 1),
        "wo": rows(a["L0_attn_Wo"]),
        "wg1": rows(a["L0_attn_Wg1"]),
        "wg2": a["L0_attn_Wg2"],
        "nw": a["L0_attn_norm_weight"].reshape(KC, P).T,
        "ctxw": a["ctx_2048"].reshape(E1, D, KC, P).transpose(3, 0, 2, 1),
        "tok": a["itok_BxS_13_99985"].reshape(NT, P).T,
        "gate_weight": a["L0_ffn_gate_weight"],
        "o2n": a["L0_ffn_old_to_new"].reshape(OLD, 1),
        "gu": gu.reshape(E2, 2 * FI, KC, P).transpose(0, 3, 2, 1),
        "dn": a["L0_ffn_down_proj"].transpose(0, 2, 1),
        **shape_constants(),
    }
    arrays["attn_pack"] = pack_rows(arrays, ATTN_PACK)
    arrays["sort_pack"] = pack_rows(arrays, SORT_PACK)
    arrays = {"in_" + k: np.ascontiguousarray(v) for k, v in arrays.items()}
    nc = bacc.Bacc("TRN2", target_bir_lowering=False, num_devices=1)
    d = {k[3:]: nc.dram_tensor(k, v.shape, mybir.dt.from_np(v.dtype), kind="ExternalInput").ap() for k, v in arrays.items()}
    d["out"] = nc.dram_tensor("out", (TOK, D), F32, kind="ExternalOutput").ap()
    build(nc, d)
    r = run(nc, [arrays], core_ids=[0])
    return np.asarray(r.results[0]["out"]).reshape(a["x"].shape)
```
